# Optimizing a Trainium2 kernel written in Bass

```python
import numpy as np
import jax
import jax.numpy as jnp

def _softmax(x, axis=-1):
    return jax.nn.softmax(x, axis=axis)

def _gelu(x):
    return jax.nn.gelu(x, approximate=True)

def _silu(x):
    return jax.nn.silu(x)

def _sigmoid(x):
    return jax.nn.sigmoid(x)

def _layernorm(x, axis=-1, eps=1e-05):
    m = jnp.mean(x, axis=axis, keepdims=True)
    v = jnp.var(x, axis=axis, keepdims=True)
    return (x - m) / jnp.sqrt(v + eps)

def _scatter_add(tgt, idx, src, axis=0):
    return tgt.at[idx].add(src)

def _segment_sum(src, seg, n):
    return jax.ops.segment_sum(src, seg, n)
kernel_name = 'mk_gnn_resnorm_d4_gnn_r64_07108a'

def setup_inputs(seed: int=0):
    np.random.seed(seed)
    _w = jnp.asarray

    def _rec_inputs():
        import jax
        import jax.numpy as jnp
        _gk = jax.random.key(seed)
        x = -0.0003713 + 1 * jax.random.normal(jax.random.fold_in(_gk, 1), (100000, 128), jnp.float32)
        src = jax.random.randint(jax.random.fold_in(_gk, 2), (25000,), 0, 100000, jnp.int32)
        dst = jnp.minimum((100000 * jax.random.uniform(jax.random.fold_in(_gk, 3), (25000,)) ** 2.0).astype(jnp.int32), 99999)
        _o = jnp.argsort(dst, stable=True)
        src = src[_o]
        dst = dst[_o]
        edge_type_4 = jax.random.randint(jax.random.fold_in(_gk, 13), (25000,), 0, 4, jnp.int32)
        edge_weight = jax.random.uniform(jax.random.fold_in(_gk, 14), (25000,), jnp.float32, 0.0, 1)
        node_type_3 = jax.random.randint(jax.random.fold_in(_gk, 15), (100000,), 0, 3, jnp.int32)
        return (x, src, dst, edge_type_4, edge_weight, node_type_3)
    x, src, dst, edge_type_4, edge_weight, node_type_3 = _rec_inputs()

    def _L0_gnn_setup():
        import jax, jax.numpy as jnp
        import numpy as np
        N_NODES = 100000
        HOP = 3

        def _spmm(edge_row, edge_col, edge_vals, emb):
            msgs = edge_vals[:, None] * emb[edge_col]
            return jax.ops.segment_sum(msgs, edge_row, num_segments=N_NODES)
        key = jax.random.key(seed)
        k1, k2, k3, k4 = jax.random.split(key, 4)
        n_edges = 50000
        users_emb = jax.random.normal(k1, (N_NODES, 128), dtype=jnp.float32)
        edge_row = jax.random.randint(k2, (n_edges,), 0, N_NODES, dtype=jnp.int64)
        edge_col = jax.random.randint(k3, (n_edges,), 0, N_NODES, dtype=jnp.int64)
        edge_vals = jax.random.uniform(k4, (n_edges,), dtype=jnp.float32)
        return {'users_emb': users_emb, 'edge_row': edge_row, 'edge_col': edge_col, 'edge_vals': edge_vals}
    _L0_gnn_all = _L0_gnn_setup()
    _L0_gnn_in = {k: v for k, v in _L0_gnn_all.items() if k in ()}
    del _L0_gnn_all

    def _L1_gnn_setup():
        import jax, jax.numpy as jnp
        import numpy as np
        N, E = (100000, 500000)
        IN, H, D = (128, 4, 32)
        NT, ET = (3, 4)

        def typed_linear(x, types, W):
            out = jnp.zeros((x.shape[0], W.shape[2]), x.dtype)
            for t in range(W.shape[0]):
                out = jnp.where((types == t)[:, None], x @ W[t], out)
            return out

        def edge_typed(xe, etype, W):
            out = jnp.zeros_like(xe)
            for t in range(W.shape[1]):
                yt = jnp.einsum('ehd,hdf->ehf', xe, W[:, t])
                out = jnp.where((etype == t)[:, None, None], yt, out)
            return out
        key = jax.random.key(seed)
        ks = jax.random.split(key, 9)
        x = jax.random.normal(ks[0], (N, IN), jnp.float32)
        ntype = jax.random.randint(ks[1], (N,), 0, NT)
        etype = jax.random.randint(ks[2], (E,), 0, ET)
        src = jax.random.randint(ks[3], (E,), 0, N)
        dst = jax.random.randint(ks[4], (E,), 0, N)
        W_kqv = jax.random.normal(ks[5], (NT, IN, H * D), jnp.float32) * (1.0 / np.sqrt(IN))
        W_a = jax.random.normal(ks[6], (NT, H * D, H * D), jnp.float32) * (1.0 / np.sqrt(H * D))
        rel_pri = jnp.ones((H, ET), jnp.float32)
        rel_att = jax.random.normal(ks[7], (H, ET, D, D), jnp.float32) * (1.0 / np.sqrt(D))
        return {'x': x, 'ntype': ntype, 'etype': etype, 'src': src, 'dst': dst, 'W_kqv': W_kqv, 'W_a': W_a, 'rel_pri': rel_pri, 'rel_att': rel_att}
    _L1_gnn_all = _L1_gnn_setup()
    _L1_gnn_in = {k: v for k, v in _L1_gnn_all.items() if k in ('W_kqv', 'W_a', 'rel_pri', 'rel_att')}
    del _L1_gnn_all

    def _L2_gnn_setup():
        import jax, jax.numpy as jnp
        import numpy as np
        ALPHA = 0.5
        N_NODES = 100000
        N_EDGES = 25000
        D = 128
        key = jax.random.key(seed)
        k1, k2, k3 = jax.random.split(key, 3)
        edge_feats = jax.random.normal(k1, (N_NODES, D), dtype=jnp.float32)
        src = jax.random.randint(k2, (N_EDGES,), 0, N_NODES, dtype=jnp.int32)
        dst = jax.random.randint(k3, (N_EDGES,), 0, N_NODES, dtype=jnp.int32)
        return {'edge_feats': edge_feats, 'src': src, 'dst': dst}
    _L2_gnn_all = _L2_gnn_setup()
    _L2_gnn_in = {k: v for k, v in _L2_gnn_all.items() if k in ()}
    del _L2_gnn_all

    def _L3_gnn_setup():
        import jax, jax.numpy as jnp
        import numpy as np
        N_NODES = 50000

        def gcn_conv(x, W, b, src, dst, n_nodes):
            loop = jnp.arange(n_nodes, dtype=src.dtype)
            s = jnp.concatenate([src, loop])
            d = jnp.concatenate([dst, loop])
            deg = jax.ops.segment_sum(jnp.ones(d.shape[0], x.dtype), d, num_segments=n_nodes)
            dinv = jnp.where(deg > 0, jax.lax.rsqrt(deg), 0.0)
            h = x @ W
            norm = (dinv[s] * dinv[d])[:, None]
            msg = h[s] * norm
            out = jax.ops.segment_sum(msg, d, num_segments=n_nodes)
            return out + b
        key = jax.random.key(seed)
        k1, k2, k3, k4 = jax.random.split(key, 4)
        N, E, din, dh, dout = (N_NODES, 12500, 128, 256, 128)
        x = jax.random.normal(k1, (N, din), jnp.float32)
        edge_index = jax.random.randint(k2, (2, E), 0, N, jnp.int64)
        W1 = jax.random.normal(k3, (din, dh), jnp.float32) / np.sqrt(din)
        b1 = jnp.zeros((dh,), jnp.float32)
        W2 = jax.random.normal(k4, (dh, dout), jnp.float32) / np.sqrt(dh)
        b2 = jnp.zeros((dout,), jnp.float32)
        return {'x': x, 'edge_index': edge_index, 'W1': W1, 'b1': b1, 'W2': W2, 'b2': b2}
    _L3_gnn_all = _L3_gnn_setup()
    _L3_gnn_in = {k: v for k, v in _L3_gnn_all.items() if k in ('W1', 'b1', 'W2', 'b2')}
    del _L3_gnn_all
    return {'x': x, 'src': src, 'dst': dst, 'edge_type_4': edge_type_4, 'edge_weight': edge_weight, 'node_type_3': node_type_3, 'L1_gnn_W_kqv': _L1_gnn_in['W_kqv'], 'L1_gnn_W_a': _L1_gnn_in['W_a'], 'L1_gnn_rel_pri': _L1_gnn_in['rel_pri'], 'L1_gnn_rel_att': _L1_gnn_in['rel_att'], 'L3_gnn_W1': _L3_gnn_in['W1'], 'L3_gnn_b1': _L3_gnn_in['b1'], 'L3_gnn_W2': _L3_gnn_in['W2'], 'L3_gnn_b2': _L3_gnn_in['b2']}

def reference(x, src, dst, edge_type_4, edge_weight, node_type_3, L1_gnn_W_kqv, L1_gnn_W_a, L1_gnn_rel_pri, L1_gnn_rel_att, L3_gnn_W1, L3_gnn_b1, L3_gnn_W2, L3_gnn_b2):
    import jax
    import jax.numpy as jnp

    def _L0_gnn_ref(users_emb, edge_row, edge_col, edge_vals):
        import jax, jax.numpy as jnp
        import numpy as np
        N_NODES = 100000
        HOP = 3

        def _spmm(edge_row, edge_col, edge_vals, emb):
            msgs = edge_vals[:, None] * emb[edge_col]
            return jax.ops.segment_sum(msgs, edge_row, num_segments=N_NODES)
        acc = users_emb
        emb = users_emb
        for _ in range(HOP):
            emb = _spmm(edge_row, edge_col, edge_vals, emb)
            acc = acc + emb
        return acc / jnp.asarray(HOP + 1, dtype=users_emb.dtype)

    def _L1_gnn_ref(x, ntype, etype, src, dst, W_kqv, W_a, rel_pri, rel_att):
        import jax, jax.numpy as jnp
        import numpy as np
        N, E = (100000, 500000)
        IN, H, D = (128, 4, 32)
        NT, ET = (3, 4)

        def typed_linear(x, types, W):
            out = jnp.zeros((x.shape[0], W.shape[2]), x.dtype)
            for t in range(W.shape[0]):
                out = jnp.where((types == t)[:, None], x @ W[t], out)
            return out

        def edge_typed(xe, etype, W):
            out = jnp.zeros_like(xe)
            for t in range(W.shape[1]):
                yt = jnp.einsum('ehd,hdf->ehf', xe, W[:, t])
                out = jnp.where((etype == t)[:, None, None], yt, out)
            return out
        n = x.shape[0]
        kqv = typed_linear(x, ntype, W_kqv).reshape(n, H, D)
        k_e = kqv[src]
        q_e = kqv[dst]
        v_e = kqv[src]
        kw = edge_typed(k_e, etype, rel_att)
        a = (kw * q_e).sum(-1) * rel_pri.T[etype] / jnp.sqrt(jnp.float32(D))
        m = edge_typed(v_e, etype, rel_att)
        amax = jax.ops.segment_max(a, dst, num_segments=n)
        ex = jnp.exp(a - amax[dst])
        esum = jax.ops.segment_sum(ex, dst, num_segments=n)
        attn = ex / esum[dst]
        h = jax.ops.segment_sum(m * attn[..., None], dst, num_segments=n)
        h = h.reshape(n, H * D)
        h = typed_linear(h, ntype, W_a)
        h = jax.nn.relu(h)
        return h

    def _L2_gnn_ref(edge_feats, src, dst):
        import jax, jax.numpy as jnp
        import numpy as np
        ALPHA = 0.5
        N_NODES = 100000
        N_EDGES = 25000
        D = 128
        msg = edge_feats[src]
        n = edge_feats.shape[0]
        s = jax.ops.segment_sum(msg, dst, num_segments=n)
        cnt = jax.ops.segment_sum(jnp.ones((src.shape[0],), edge_feats.dtype), dst, num_segments=n)
        h_new = s / jnp.maximum(cnt, 1.0)[:, None]
        return ALPHA * edge_feats + (1.0 - ALPHA) * h_new

    def _L3_gnn_ref(x, edge_index, W1, b1, W2, b2):
        import jax, jax.numpy as jnp
        import numpy as np
        N_NODES = 50000

        def gcn_conv(x, W, b, src, dst, n_nodes):
            loop = jnp.arange(n_nodes, dtype=src.dtype)
            s = jnp.concatenate([src, loop])
            d = jnp.concatenate([dst, loop])
            deg = jax.ops.segment_sum(jnp.ones(d.shape[0], x.dtype), d, num_segments=n_nodes)
            dinv = jnp.where(deg > 0, jax.lax.rsqrt(deg), 0.0)
            h = x @ W
            norm = (dinv[s] * dinv[d])[:, None]
            msg = h[s] * norm
            out = jax.ops.segment_sum(msg, d, num_segments=n_nodes)
            return out + b
        src, dst = (edge_index[0], edge_index[1])
        n = x.shape[0]
        h = jax.nn.relu(gcn_conv(x, W1, b1, src, dst, n))
        return gcn_conv(h, W2, b2, src, dst, n)
    edge_index = jnp.stack([src, dst])
    x = _layernorm(x + _L0_gnn_ref(x, src, dst, edge_weight), axis=-1)
    x = _layernorm(x + _L1_gnn_ref(x, node_type_3, edge_type_4, src, dst, L1_gnn_W_kqv, L1_gnn_W_a, L1_gnn_rel_pri, L1_gnn_rel_att), axis=-1)
    x = _layernorm(x + _L2_gnn_ref(x, src, dst), axis=-1)
    x = _layernorm(x + _L3_gnn_ref(x, edge_index, L3_gnn_W1, L3_gnn_b1, L3_gnn_W2, L3_gnn_b2), axis=-1)
    return x

_drawn_inputs = setup_inputs


def setup_inputs(seed=0):
    import zlib

    import numpy as np

    out = dict(_drawn_inputs(seed))
    spreads = {'L1_gnn_rel_pri': (1.0, 0.2), 'L3_gnn_b1': (0.0, 0.1), 'L3_gnn_b2': (0.0, 0.1)}
    factors = {}
    for name, (base, spread) in spreads.items():
        noise = np.random.default_rng([zlib.crc32(name.encode()), seed]).standard_normal(out[name].shape)
        drawn = base * np.exp(spread * noise) if base else spread * noise
        out[name] = jnp.asarray(drawn.astype(out[name].dtype))
    for name, factor in factors.items():
        out[name] = (out[name] * factor).astype(out[name].dtype)
    return out
```

```python
import concourse.bass as bass
from concourse import mybir
from contextlib import ExitStack

ALU = mybir.AluOpType
ACT = mybir.ActivationFunctionType
F32 = mybir.dt.float32
BF16 = mybir.dt.bfloat16
I32 = mybir.dt.int32

P = 128
D = 128
TG = 4
GE = TG * P
BODY = 2 * GE
HEADS, HD = 4, 32
EPS = 1e-5
BIG = 1e30
FAR = 1 << 20


class Phase(ExitStack):

    def __init__(self, nc):
        super().__init__()
        self.nc, self.sems = nc, []

    def __exit__(self, *problem):
        if self.sems and problem[0] is None:
            self.nc.clear_and_free_semaphores(self.sems)
            self.nc.all_engine_barrier()
        return super().__exit__(*problem)


class Chain:

    def __init__(self, eng, sem):
        self.eng, self.sem, self.n = eng, sem, 0

    def link(self, ins):
        self.n += 1
        ins.then_inc(self.sem, 1)
        self.eng.wait_ge(self.sem, self.n)

    def close(self):
        if self.n:
            self.eng.sem_inc(self.sem, -self.n)
        self.n = 0


def take(eng, sem, n=1):
    eng.wait_ge(sem, n)
    eng.sem_inc(sem, -n)


def gnn_kernel(nc, x, src, dst, etype, weight, ntype, w_kqv, w_a, rel_pri, rel_att, w1, b1, w2, b2, out):
    N = x.shape[0]
    E = src.shape[0]
    NTYPES, ETYPES = w_kqv.shape[0], rel_att.shape[1]
    BODIES = -(-E // BODY)
    EP = BODIES * BODY
    NT = EP // P
    HALF = NT // 2
    NONE = EP
    assert D == P and NT % 2 == 0 and HALF <= P and NTYPES == 3 and ETYPES == 4
    NGROUPS = -(-N // GE)
    NODE_P = 125
    assert N % NODE_P == 0

    main = ExitStack()
    with main:
        def sb(stack, name, shape, dt=F32):
            return stack.enter_context(nc.sbuf_tensor(name, shape, dt))

        def pb(stack, name, shape=(P, GE), dt=F32):
            return stack.enter_context(nc.psum_tensor(name, list(shape), dt))

        def sem(stack, name):
            handle = nc.alloc_semaphore(name=name)
            if stack is not main:
                stack.sems.append(handle)
            return handle

        def two(make, stack, name, *a):
            return [make(stack, f"{name}{s}", *a) for s in range(2)]

        def dram(name, shape, dt=F32):
            return nc.dram_tensor(name, shape, dt, kind="Internal").ap()

        node_table = dram("node_table", (N, 4), I32)
        rec_low = dram("rec_low", (EP, 4), I32)
        rec_src = dram("rec_src", (EP + 2, 4), I32)
        keep_src = dram("keep_src", (1, EP), BF16)
        edge_dst = dram("edge_dst", (EP + 2,), I32)
        seq_rows = dram("seq_rows", (7, EP), BF16)
        onehot_rows = dram("onehot_rows", (ETYPES, EP))
        dinv_row = dram("dinv_row", (1, EP))
        src_x1 = dram("src_x1", (EP, D))
        x1_nodes = dram("x1_nodes", (EP, D))
        e1_rows = dram("e1_rows", (EP + 1, D))
        e2_rows = dram("e2_rows", (EP + 1, D))
        x1_rows = dram("x1_rows", (EP, D))
        x2_rows = dram("x2_rows", (EP, D))
        x3s_rows = dram("x3s_rows", (EP, D))
        lrm = dram("lrm", (EP // GE, P, 3, GE))
        h2_src = dram("h2_src", (EP, D))
        h2s_rows = dram("h2s_rows", (EP, D))
        z_rows = dram("z_rows", (EP, D))
        KEEP, NFIRST, NOTLAST, NLAST, ET, NTS, NTD = range(7)

        def rows_of(table, i, s):
            v = table[0:EP, :].rearrange("(b s j p) f -> b s p j f", s=2, j=TG, p=P)
            return v[bass.ds(i, 1), s].rearrange("o p j f -> (o p) j f")

        def seq_of(table, i, s, a, b):
            return table[a:b, bass.ds(i * BODY + s * GE, GE)].partition_broadcast(P)

        def lrm_of(i, s, a, b):
            v = lrm.rearrange("(b s) p k e -> b s p k e", s=2)
            return v[bass.ds(i, 1), s, :, a:b].rearrange("o p k e -> (o p) k e")

        ident = sb(main, "ident", [P, P])
        head_ones = sb(main, "head_ones", [P, P])
        wk = sb(main, "wk", [P, NTYPES, D])
        wa = sb(main, "wa", [P, NTYPES, D])
        ra = sb(main, "ra", [P, ETYPES, D])
        pri = sb(main, "pri", [ETYPES, D])
        w1s = sb(main, "w1s", [P, 2 * D])
        w2s = sb(main, "w2s", [P, 2, D])
        b1s = sb(main, "b1s", [P, 2])
        b2_all = sb(main, "b2_all", [P, D])
        b2_parts = sb(main, "b2_parts", [3, GE], BF16)
        ones3 = sb(main, "ones3", [3, P], BF16)
        eps_col = sb(main, "eps_col", [P, 7])
        EPS1, EPS16, EPS_SQ, EPS_CB, EPS_1, EPS_M, ONE = range(7)
        i_src = sb(main, "i_src", [P, NT + 2 * TG], I32)
        i_dst = sb(main, "i_dst", [P, NT + 2 * TG], I32)
        i_out = sb(main, "i_out", [P, NT + 2 * TG], I32)
        i_pick = sb(main, "i_pick", [P, NT + 2 * TG], I32)
        i_node1 = sb(main, "i_node1", [P, NT + 2 * TG], I32)
        i_dst1 = sb(main, "i_dst1", [P, NT + 2 * TG], I32)
        i_srcout = sb(main, "i_srcout", [P, NT + 2 * TG], I32)
        entry_dst = sb(main, "entry_dst", [P, NT + 2 * TG, 1], I32)
        k_src = sb(main, "k_src", [P, NT + 2 * TG], I32)
        k_out = sb(main, "k_out", [P, NT + 2 * TG], I32)
        k_dst = sb(main, "k_dst", [P, NT + 2 * TG], I32)
        k_pick = sb(main, "k_pick", [P, NT + 2 * TG], I32)
        k_w = sb(main, "k_w", [P, NT])
        entry_src = sb(main, "entry_src", [P, NT + 2 * TG, 2], I32)
        c_last = sb(main, "c_last", [P, NT])
        c_third = sb(main, "c_third", [P, NT])
        c_dinv = sb(main, "c_dinv", [P, NT])
        c_root = sb(main, "c_root", [P, NT])
        c_nts = sb(main, "c_nts", [P, NT])
        c_ntd = sb(main, "c_ntd", [P, NT])
        src_stats = sb(main, "src_stats", [P, NT, 6])
        local = [sb(main, f"local{n}", [P, NT, 2]) for n in range(2)]

        dx = two(sb, main, "dx", [P, TG, D])
        dn = two(sb, main, "dn", [P, TG, D])
        dxT = two(sb, main, "dxT", [P, GE])
        dh = two(sb, main, "dh", [P, 2, GE])
        dy = two(sb, main, "dy", [P, TG, D])
        dst1 = two(sb, main, "dst1", [P, TG, 6])
        dst2 = two(sb, main, "dst2", [P, TG, 6])
        dmv1 = two(sb, main, "dmv1", [P, TG, 2])
        dmv2 = two(sb, main, "dmv2", [P, TG, 2])
        dsd1 = two(sb, main, "dsd1", [P, TG])
        dsd2 = two(sb, main, "dsd2", [P, TG])
        dr1 = two(sb, main, "dr1", [P, TG])
        dr2 = two(sb, main, "dr2", [P, TG])
        db1 = two(sb, main, "db1", [P, TG])
        db2 = two(sb, main, "db2", [P, TG])
        d_loaded = two(sem, main, "d_loaded")
        d_stored = two(sem, main, "d_stored")
        (d_var1, d_std1, d_affine1, d_normed, d_free, d_turned, d_copied, d_hidden, d_relu, d_summed, d_taken,
         d_var2, d_std2, d_out) = [sem(main, f"d_{n}") for n in (
            "var1", "std1", "affine1", "normed", "free", "turned", "copied", "hidden", "relu", "summed",
            "taken", "var2", "std2", "out")]
        dve_done = sem(main, "dve_done")
        act_done = sem(main, "act_done")

        def node_rows(table, k):
            start = min(k * GE, N - GE) if isinstance(k, int) else k * GE
            v = table[bass.ds(start, GE), :] if not isinstance(start, int) else table[start:start + GE, :]
            return v.rearrange("(p j) f -> p j f", j=TG)

        def d_load(sp, k, s):
            take(sp, d_free)
            sp.dma_start(dx[s][:], node_rows(x, k)).then_inc(d_loaded[s], 16)

        def d_store(sp, k, s):
            take(sp, d_out)
            sp.dma_start(node_rows(out, k), dy[s][:]).then_inc(d_stored[s], 16)

        def d_stats1(dve, ch, s, n):
            dve.wait_ge(d_loaded[s], 16 * n + 16)
            for j in range(TG):
                last = nc.vector.bn_stats(dst1[s][:, j, :], dx[s][:, j, :])
            ch.link(last)
            for j in range(TG):
                last = nc.vector.bn_aggr(dmv1[s][:, j, :], dst1[s][:, j, :])
            last.then_inc(d_var1, 1)

        def d_affine(dve, ch, s, std, mv, r, b, sd, done):
            take(dve, std)
            ch.link(nc.vector.reciprocal(r[s][:], sd[s][:]))
            ins = nc.vector.scalar_tensor_tensor(out=b[s][:], in0=mv[s][:, :, 0], scalar=-1.0, in1=r[s][:],
                                                 op0=ALU.mult, op1=ALU.mult)
            if done is None:
                ch.link(ins)
            else:
                ins.then_inc(done, 1)

        def d_residual(dve, ch, s, n):
            take(dve, d_summed)
            dve.wait_ge(d_stored[s], 16 * n + 16)
            ch.link(nc.vector.tensor_tensor(dy[s][:], ps_do[:].rearrange("p (j f) -> p j f", j=TG), dn[s][:],
                                            ALU.add))
            nc.vector.nop().then_inc(d_taken, 1)
            for j in range(TG):
                last = nc.vector.bn_stats(dst2[s][:, j, :], dy[s][:, j, :])
            ch.link(last)
            for j in range(TG):
                last = nc.vector.bn_aggr(dmv2[s][:, j, :], dst2[s][:, j, :])
            last.then_inc(d_var2, 1)

        def d_final(dve, ch, s):
            d_affine(dve, ch, s, d_std2, dmv2, dr2, db2, dsd2, None)
            for j in range(TG):
                last = nc.vector.tensor_scalar(dy[s][:, j, :], dy[s][:, j, :], dr2[s][:, j:j + 1],
                                               db2[s][:, j:j + 1], ALU.mult, ALU.add)
            last.then_inc(d_out, 1)

        def d_root1(act, s):
            take(act, d_var1)
            nc.scalar.activation(dsd1[s][:], dmv1[s][:, :, 1], ACT.Sqrt, bias=eps_col[:, EPS_CB:EPS_CB + 1],
                                 scale=C3).then_inc(d_std1, 1)

        def d_root2(act, s):
            take(act, d_var2)
            nc.scalar.activation(dsd2[s][:], dmv2[s][:, :, 1], ACT.Sqrt, bias=eps_col[:, EPS1:EPS1 + 1])\
                .then_inc(d_std2, 1)

        def d_norm1(act, s):
            take(act, d_affine1)
            for j in range(TG):
                last = nc.scalar.activation(dn[s][:, j, :], dx[s][:, j, :], ACT.Identity, bias=db1[s][:, j:j + 1],
                                            scale=dr1[s][:, j:j + 1])
            last.then_inc(d_normed, 1)

        def d_copy(act, s):
            take(act, d_turned)
            nc.scalar.activation(dxT[s][:], ps_dt[:], ACT.Copy).then_inc(d_copied, 1)

        def d_hid(act, s):
            for c in range(2):
                take(act, d_hidden)
                nc.scalar.activation(dh[s][:, c, :], ps_dh[c][:], ACT.Relu, bias=b1s[:, c:c + 1])\
                    .then_inc(d_relu, 1)

        def d_turn(pe, s):
            take(pe, d_normed)
            nc.tensor.nop().then_inc(d_free, 1)
            for j in range(TG):
                last = nc.tensor.transpose(ps_dt[:, j * P:(j + 1) * P], dn[s][:, j, :], ident[:])
            last.then_inc(d_turned, 1)

        def d_first(pe, s):
            take(pe, d_copied)
            for c in range(2):
                nc.tensor.matmul(ps_dh[c][:], w1s[:, c * D:(c + 1) * D], dxT[s][:], start=True, stop=True)\
                    .then_inc(d_hidden, 1)

        def d_second(pe, s):
            take(pe, d_relu, 2)
            take(pe, d_taken)
            nc.tensor.matmul(ps_do[:], ones3[:], b2_parts[:], start=True, stop=False, skip_group_check=True)
            for j in range(TG):
                for c in range(2):
                    last = nc.tensor.matmul(ps_do[:, j * P:(j + 1) * P], dh[s][:, c, j * P:(j + 1) * P],
                                            w2s[:, c, :], start=False, stop=(j == TG - 1 and c == 1),
                                            skip_group_check=True)
            last.then_inc(d_summed, 1)

        E1 = EPS / 1.5625
        CS = 1 + EPS / 2.25
        ES = EPS * EPS / 2.25
        C3 = (2.25 * 1.5625 + EPS * 1.5625 * (1 + EPS)) / (2.25 * 1.5625)
        E3 = EPS ** 3 / (2.25 * 1.5625)

        with Phase(nc) as st:
            raw = sb(st, "raw_edges", [HALF, 4, 2, P], I32)
            raw_et = sb(st, "raw_et", [HALF, 2, P], I32)
            pads = sb(st, "pads", [1, EP + 2 - E], I32)
            tab = sb(st, "tab", [NODE_P, N // NODE_P, 4], I32)
            tab_nt = sb(st, "tab_nt", [NODE_P, N // NODE_P], I32)
            fA = sb(st, "fA", [HALF, 4, 2, P])
            etA = sb(st, "etA", [HALF, 2, P])
            pos_i = sb(st, "pos_i", [HALF, 2, P], I32)
            pos = sb(st, "pos", [HALF, 2, P])
            first = sb(st, "first", [HALF, 2, P])
            last_ = sb(st, "last_", [HALF, 2, P])
            t1 = sb(st, "t1", [HALF, 2, P])
            t2 = sb(st, "t2", [HALF, 2, P])
            t3 = sb(st, "t3", [HALF, 2, P])
            cnt = sb(st, "cnt", [HALF, 2, P])
            rootA = sb(st, "rootA", [HALF, 2, P])
            dinvA = sb(st, "dinvA", [HALF, 2, P])
            thirdA = sb(st, "thirdA", [HALF, 2, P])
            dclA = sb(st, "dclA", [HALF, 2, P])
            outA = sb(st, "outA", [HALF, 2, P])
            starts = sb(st, "starts", [HALF, 2, P])
            bfA = sb(st, "bfA", [HALF, 5, 2, P], BF16)
            ohA = sb(st, "ohA", [HALF, ETYPES, 2, P])
            zero_keep = sb(st, "zero_keep", [P, NT])
            run_rows = sb(st, "run_rows", [1, NT + 1])
            carry = sb(st, "carry", [HALF, 2])
            one = sb(st, "one", [1, 1])
            b2r = sb(st, "b2r", [1, 3, D])
            pri_h = sb(st, "pri_h", [HEADS, ETYPES])
            spread = sb(st, "spread", [HEADS, D])
            b1r = sb(st, "b1r", [2, P])
            b2h = sb(st, "b2h", [1, 3, D], BF16)
            zrow = sb(st, "zrow", [1, D])
            ps = [pb(st, f"pp{n}") for n in range(8)]
            p_pad, p_dst, p_w, p_ld, p_tab, p_b2, p_z, p_st, p_b2c = [sem(st, f"p_{n}") for n in (
                "pad", "dst", "w", "ld", "tab", "b2", "z", "st", "b2c")]
            p_mem, p_own, p_ident, p_tot, p_scan, p_carry, p_root, p_rooted, p_field, p_turn, p_seq, p_bseq, p_tabd, p_raw, p_pri = [
                sem(st, f"p_{n}") for n in ("mem", "own", "ident", "tot", "scan", "carry", "root", "rooted",
                                            "field", "turn", "seq", "bseq", "tabd", "raw", "pri")]
            FULL = E // P - HALF
            REST = E - (HALF + FULL) * P

            def halves(view_out, flat, n):
                whole = n // P - HALF
                rest = n - (HALF + whole) * P
                got = [(view_out[:, 0, :], flat[0:HALF * P].rearrange("(t c) -> t c", c=P)),
                       (view_out[0:whole, 1, :], flat[HALF * P:(HALF + whole) * P].rearrange("(t c) -> t c", c=P))]
                if rest:
                    got.append((view_out[whole:whole + 1, 1, 0:rest],
                                flat[(HALF + whole) * P:n].rearrange("(a c) -> a c", a=1)))
                return got

            with nc.Block() as block:
                @block.sync
                def _(sp):
                    take(sp, p_pad)
                    sp.dma_start(edge_dst[1:E + 1], dst).then_inc(p_dst, 16)
                    sp.dma_start(edge_dst[E + 1:EP + 2].rearrange("(a c) -> a c", a=1), pads[0:1, 1:]).then_inc(p_dst, 16)
                    sp.dma_start(edge_dst[0:1].rearrange("(a c) -> a c", a=1), pads[0:1, 0:1]).then_inc(p_dst, 16)
                    take(sp, p_raw)
                    for t in range(NTYPES):
                        sp.dma_start(wk[:, t, :], w_kqv[t]).then_inc(p_w, 16)
                        sp.dma_start(wa[:, t, :], w_a[t]).then_inc(p_w, 16)
                    for h in range(HEADS):
                        sp.dma_start(ra[h * HD:(h + 1) * HD, :, h * HD:(h + 1) * HD],
                                     rel_att[h].rearrange("t d f -> d t f")).then_inc(p_w, 16)
                    sp.dma_start(pri_h[:], rel_pri).then_inc(p_w, 16)
                    sp.dma_start(w1s[:], w1).then_inc(p_w, 16)
                    sp.dma_start(w2s[:], w2.rearrange("(c p) f -> p c f", p=P)).then_inc(p_w, 16)
                    sp.dma_start(b1r[:], b1.rearrange("(c p) -> c p", p=P)).then_inc(p_w, 16)
                    sp.dma_start(b2_all[:], b2.rearrange("(a f) -> a f", a=1).to_broadcast([P, D])).then_inc(p_w, 16)
                    sp.dma_start(b2r[:, 0, :], b2.rearrange("(a f) -> a f", a=1)).then_inc(p_b2, 16)
                    sp.dma_start(tab_nt[:], ntype.rearrange("(p c) -> p c", p=NODE_P)).then_inc(p_tab, 16)
                    for o, f in halves(raw[:, 0], src, E) + halves(raw_et[:], etype, E):
                        sp.dma_start(o, f).then_inc(p_ld, 16)
                    sp.wait_ge(p_dst, 48)
                    for k, off in ((1, 1), (2, 2), (3, 0)):
                        for h in range(2):
                            sp.dma_start(raw[:, k, h, :], edge_dst[off + h * HALF * P:off + (h + 1) * HALF * P]
                                         .rearrange("(t c) -> t c", c=P)).then_inc(p_ld, 16)
                    sp.dma_start(e1_rows[EP:EP + 1, :], zrow[:]).then_inc(p_z, 16)
                    sp.dma_start(e2_rows[EP:EP + 1, :], zrow[:]).then_inc(p_z, 16)
                    take(sp, p_tabd)
                    sp.dma_start(node_table.rearrange("(p c) k -> p c k", p=NODE_P), tab[:]).then_inc(p_st, 16)
                    take(sp, p_b2c)
                    for k in range(3):
                        for j in range(TG):
                            sp.dma_start(b2_parts[k:k + 1, j * D:(j + 1) * D], b2h[0:1, k, :]).then_inc(p_st, 16)
                    take(sp, p_seq)
                    for k in range(5):
                        sp.dma_start(seq_rows[k].rearrange("(h t c) -> t h c", h=2, c=P), bfA[:, k]).then_inc(p_st, 16)
                    for k in range(ETYPES):
                        sp.dma_start(onehot_rows[k].rearrange("(h t c) -> t h c", h=2, c=P), ohA[:, k])\
                            .then_inc(p_st, 16)
                    sp.dma_start(dinv_row[0].rearrange("(h t c) -> t h c", h=2, c=P), dinvA[:]).then_inc(p_st, 16)
                    sp.wait_ge(p_z, 32)
                    sp.wait_ge(p_st, 16 * (1 + 3 * TG + 5 + ETYPES + 1))

                @block.gpsimd
                def _(gp):
                    nc.gpsimd.memset(pads[:], 2 * FAR)
                    nc.gpsimd.memset(zrow[:], 0.0)
                    nc.gpsimd.memset(ident[:], 0.0).then_inc(p_own, 1)
                    gp.wait_ge(p_own, 1)
                    nc.gpsimd.memset(pads[0:1, 0:1], -1).then_inc(p_pad, 1)
                    nc.gpsimd.memset(raw_et[:], 0)
                    nc.gpsimd.memset(raw[:, 0], 0)
                    nc.gpsimd.memset(ra[:], 0.0).then_inc(p_raw, 1)
                    nc.gpsimd.affine_select(out=ident[:], in_=ident[:], compare_op=ALU.not_equal, fill=1.0,
                                            base=0, pattern=[[-1, P]], channel_multiplier=1).then_inc(p_ident, 1)
                    nc.gpsimd.memset(tab[:], 0)
                    nc.gpsimd.iota(pos_i[:], pattern=[[HALF * P, 2], [1, P]], base=1, channel_multiplier=P)
                    nc.gpsimd.memset(entry_dst[:], 0)
                    nc.gpsimd.memset(entry_src[:], 0)
                    nc.gpsimd.memset(head_ones[:], 0.0).then_inc(p_mem, 1)
                    gp.wait_ge(p_mem, 1)
                    nc.gpsimd.iota(entry_dst[:, 0:NT, 0], pattern=[[P, NT]], base=1, channel_multiplier=1)
                    for t in (i_src, i_dst, i_out, i_pick, i_node1, i_dst1, i_srcout, k_src, k_out, k_dst, k_pick):
                        nc.gpsimd.memset(t[:, NT:NT + 2 * TG], 0)
                    nc.gpsimd.memset(one[:], 1.0)
                    nc.gpsimd.memset(run_rows[:], 0.0)
                    nc.gpsimd.memset(zero_keep[:], 0.0)
                    nc.gpsimd.memset(ones3[:], 1.0)
                    for k, v in ((EPS1, EPS), (EPS16, 16 * EPS), (EPS_SQ, ES), (EPS_CB, E3), (EPS_1, E1), (EPS_M, EPS / 2.25),
                                 (ONE, 1.0)):
                        last = nc.gpsimd.memset(eps_col[:, k:k + 1], v)
                    last.then_inc(p_mem, 1)
                    for h in range(HEADS):
                        gp.wait_ge(p_mem, 2 + h)
                        nc.gpsimd.memset(head_ones[h * HD:(h + 1) * HD, h * HD:(h + 1) * HD], 1.0).then_inc(p_mem, 1)
                    gp.wait_ge(p_mem, 2 + HEADS)
                    nc.gpsimd.memset(spread[:], 1.0).then_inc(p_mem, 1)
                    gp.wait_ge(p_mem, 3 + HEADS)
                    nc.gpsimd.affine_select(out=spread[:], in_=spread[:], compare_op=ALU.is_ge, fill=0.0,
                                            base=0, pattern=[[1, D]], channel_multiplier=-HD).then_inc(p_mem, 1)
                    gp.wait_ge(p_mem, 4 + HEADS)
                    nc.gpsimd.affine_select(out=spread[:], in_=spread[:], compare_op=ALU.is_ge, fill=0.0,
                                            base=HD - 1, pattern=[[-1, D]], channel_multiplier=HD).then_inc(p_mem, 1)

                @block.vector
                def _(dve):
                    ch = Chain(dve, dve_done)
                    V = nc.vector
                    dve.wait_ge(p_w, 16 * (2 * NTYPES + HEADS + 5))
                    for t in range(1, NTYPES):
                        V.tensor_tensor(wk[:, t, :], wk[:, t, :], wk[:, 0, :], ALU.subtract)
                        V.tensor_tensor(wa[:, t, :], wa[:, t, :], wa[:, 0, :], ALU.subtract)
                    for t in range(1, ETYPES):
                        V.tensor_tensor(ra[:, t, :], ra[:, t, :], ra[:, 0, :], ALU.subtract)
                    dve.wait_ge(p_b2, 16)
                    for k in range(3):
                        ch.link(V.tensor_copy(b2h[:, k, :], b2r[:, k, :]))
                        if k < 2:
                            ch.link(V.tensor_tensor(b2r[:, k + 1, :], b2r[:, k, :], b2h[:, k, :], ALU.subtract))
                    V.nop().then_inc(p_b2c, 1)
                    dve.wait_ge(p_mem, 2 + HEADS)
                    dve.wait_ge(p_tab, 16)
                    V.tensor_copy(tab[:, :, 1], tab_nt[:]).then_inc(p_tabd, 1)
                    dve.wait_ge(p_ld, 16 * 12)
                    V.tensor_copy(fA[:], raw[:])
                    V.tensor_copy(pos[:], pos_i[:])
                    ch.link(V.tensor_copy(etA[:], raw_et[:]))
                    SRC, DST, NEXT, PREV = range(4)
                    V.tensor_tensor(first[:], fA[:, DST], fA[:, PREV], ALU.not_equal)
                    V.tensor_tensor(t1[:], fA[:, DST], fA[:, NEXT], ALU.not_equal)
                    V.tensor_scalar(t2[:], fA[:, DST], float(N), None, ALU.is_lt)
                    V.tensor_scalar(dclA[:], fA[:, DST], float(N - 1), None, ALU.min)
                    ch.link(V.tensor_scalar(outA[:], fA[:, DST], float(FAR), None, ALU.add))
                    ch.link(V.tensor_tensor(last_[:], t1[:], t2[:], ALU.mult))
                    V.scalar_tensor_tensor(out=t3[:], in0=last_[:], scalar=-float(FAR), in1=outA[:], op0=ALU.mult,
                                           op1=ALU.add)
                    ch.link(V.tensor_tensor(t1[:], pos[:], first[:], ALU.mult))
                    for h in range(2):
                        last = V.tensor_tensor_scan(starts[:, h, :], zero_keep[0:HALF, 0:P], t1[:, h, :], 0.0,
                                                    ALU.add, ALU.max)
                    last.then_inc(p_tot, 1)
                    take(dve, p_scan)
                    V.tensor_tensor_scan(run_rows[:, 1:NT + 1], zero_keep[0:1, :], ps[0][0:1, 0:NT], 0.0,
                                         ALU.add, ALU.max).then_inc(p_carry, 1)
                    take(dve, p_scan)
                    ch.link(V.tensor_copy(carry[:], ps[1][0:HALF, 0:2]))
                    for h in range(2):
                        last = V.tensor_scalar(starts[:, h, :], starts[:, h, :], carry[:, h:h + 1], None, ALU.max)
                    ch.link(last)
                    ch.link(V.tensor_tensor(t2[:], pos[:], starts[:], ALU.subtract))
                    V.tensor_scalar(t1[:], t2[:], 3.0, 3.0, ALU.mult, ALU.add)
                    ch.link(V.tensor_scalar(cnt[:], t2[:], 1.0, None, ALU.add))
                    V.nop().then_inc(p_root, 1)
                    V.reciprocal(thirdA[:], t1[:])
                    V.tensor_scalar(bfA[:, KEEP], first[:], -1.0, 1.0, ALU.mult, ALU.add)
                    V.tensor_scalar(bfA[:, NFIRST], first[:], -BIG, None, ALU.mult)
                    V.tensor_scalar(bfA[:, NOTLAST], last_[:], -1.0, 1.0, ALU.mult, ALU.add)
                    V.tensor_scalar(bfA[:, NLAST], last_[:], -BIG, None, ALU.mult)
                    V.tensor_copy(bfA[:, ET], etA[:])
                    for t in range(ETYPES):
                        V.tensor_scalar(ohA[:, t], etA[:], float(t), None, ALU.is_equal)
                    take(dve, p_rooted)
                    ch.link(V.reciprocal(dinvA[:], rootA[:]))
                    V.nop().then_inc(p_seq, 1)
                    V.nop().then_inc(p_field, 1)
                    outs = (i_src, i_dst, i_out, c_last, c_third, c_dinv, c_root)
                    take(dve, p_turn)
                    for n, o in enumerate(outs):
                        V.tensor_copy(o[:, 0:NT], ps[n][:, 0:NT])
                    V.tensor_scalar(pri[:], ps[7][0:ETYPES, 0:D], HD ** -0.5, None, ALU.mult)
                    V.tensor_copy(b1s[:], ps[7][:, D:D + 2])
                    ch.close()

                @block.scalar
                def _(act):
                    nc.scalar.preload_act_table(ACT.Sqrt)
                    take(act, p_root)
                    nc.scalar.activation(rootA[:], cnt[:], ACT.Sqrt, bias=eps_col[0:HALF, ONE:ONE + 1])\
                        .then_inc(p_rooted, 1)

                @block.tensor
                def _(pe):
                    pe.wait_ge(p_ident, 1)
                    take(pe, p_tot)
                    for h in range(2):
                        last = nc.tensor.matmul(ps[0][0:1, h * HALF:(h + 1) * HALF], starts[:, h, P - 1:P],
                                                ident[0:HALF, 0:HALF], start=True, stop=True)
                    last.then_inc(p_scan, 1)
                    take(pe, p_carry)
                    for h in range(2):
                        last = nc.tensor.matmul(ps[1][0:HALF, h:h + 1], run_rows[0:1, h * HALF:(h + 1) * HALF],
                                                one[:], start=True, stop=True)
                    last.then_inc(p_scan, 1)
                    take(pe, p_field)
                    for n, f in enumerate((fA[:, 0], dclA, t3, last_, thirdA, dinvA, rootA)):
                        for h in range(2):
                            last = nc.tensor.transpose(ps[n][:, h * HALF:(h + 1) * HALF], f[:, h, :],
                                                       ident[0:HALF, 0:HALF])
                    pe.wait_ge(p_w, 16 * (2 * NTYPES + HEADS + 5))
                    pe.wait_ge(p_mem, 5 + HEADS)
                    nc.tensor.matmul(ps[7][0:ETYPES, 0:D], pri_h[:], spread[:], start=True, stop=True)
                    last = nc.tensor.transpose(ps[7][:, D:D + 2], b1r[:], ident[0:2, 0:2])
                    last.then_inc(p_turn, 1)

        dense_psum = ExitStack()
        main.push(dense_psum)
        ps_dt = pb(dense_psum, "ps_dt")
        ps_dh = two(pb, dense_psum, "ps_dh")
        ps_do = pb(dense_psum, "ps_do")

        def table_phase(tag, k0, jobs):
            dense = k0 is not None
            with Phase(nc) as st:
                stage = [two(sb, st, f"{tag}_stage{n}", [P, TG], I32) for n in range(len(jobs))]
                moved = [two(sb, st, f"{tag}_moved{n}", [P, TG, job[3]], I32) for n, job in enumerate(jobs)]
                staged = sem(st, f"{tag}_staged")
                done = two(sem, st, f"{tag}_done")
                per = 64 * len(jobs)
                with nc.Block() as block:
                    @block.gpsimd
                    def _(gp):
                        bound = gp.to_reg(N - 1)
                        with gp.Fori(0, BODIES) as i:
                            for s in range(2):
                                take(gp, staged)
                                for n, (table, col, _, width, rows, _) in enumerate(jobs):
                                    for j in range(TG):
                                        at = bass.IndirectOffsetOnAxis(ap=stage[n][s][:, j:j + 1], axis=0)
                                        if rows is None:
                                            gp.indirect_dma_start(moved[n][s][:, j, :], None, table, at,
                                                                  bounds_check=bound, oob_is_err=False)\
                                                .then_inc(done[s], 16)
                                        else:
                                            gp.indirect_dma_start(table, at, moved[n][s][:, j, :], None,
                                                                  element_offset=col, bounds_check=bound,
                                                                  oob_is_err=False).then_inc(done[s], 16)

                    @block.vector
                    def _(dve):
                        ch = Chain(dve, dve_done)
                        V = nc.vector

                        def put(s, tile):
                            reg = not isinstance(tile, int)
                            for n, (_, _, index, _, rows, _) in enumerate(jobs):
                                if rows is not None:
                                    V.tensor_copy(moved[n][s][:], sl(rows, tile, reg))
                                last = V.tensor_copy(stage[n][s][:], sl(index, tile, reg))
                            last.then_inc(staged, 1)

                        def used(s, tile, reg):
                            last = None
                            for n, job in enumerate(jobs):
                                if job[5] is not None:
                                    last = job[5](V, moved[n][s], tile, reg)
                            if last is not None:
                                ch.link(last)

                        put(0, 0)
                        put(1, TG)
                        n0 = k0 // 2 if dense else 0
                        with dve.Fori(0, BODIES - 1) as i:
                            for s in range(2):
                                if dense:
                                    d_stats1(dve, ch, 1 - s, i + (n0 + s))
                                dve.wait_ge(done[s], per * i + per)
                                used(s, i * (2 * TG) + s * TG, True)
                                put(s, i * (2 * TG) + (2 + s) * TG)
                                if dense:
                                    d_affine(dve, ch, 1 - s, d_std1, dmv1, dr1, db1, dsd1, d_affine1)
                                    d_residual(dve, ch, s, i + n0)
                                    d_final(dve, ch, s)
                            ch.close()
                        b = BODIES - 1
                        for s in range(2):
                            if dense:
                                d_stats1(dve, ch, 1 - s, b + n0 + s)
                            dve.wait_ge(done[s], per * b + per)
                            used(s, b * 2 * TG + s * TG, False)
                            if dense:
                                d_affine(dve, ch, 1 - s, d_std1, dmv1, dr1, db1, dsd1, d_affine1)
                                d_residual(dve, ch, s, b + n0)
                                d_final(dve, ch, s)
                        ch.close()

                    if dense:
                        dense_beside(block, k0)

        def dense_beside(block, k0):
            @block.sync
            def _(sp):
                if k0 == 0:
                    sp.dma_start(dx[0][:], node_rows(x, 0)).then_inc(d_loaded[0], 16)
                    sp.dma_start(dx[1][:], node_rows(x, 1)).then_inc(d_loaded[1], 16)
                    for s in range(2):
                        sp.nop().then_inc(d_stored[s], 16)
                with sp.Fori(0, BODIES) as i:
                    for s in range(2):
                        d_load(sp, i * 2 + (k0 + 2 + s), s)
                        d_store(sp, i * 2 + (k0 + s), s)

            @block.scalar
            def _(act):
                nc.scalar.preload_act_table(ACT.Sqrt)
                if k0 == 0:
                    d_root1(act, 0)
                    d_norm1(act, 0)
                    d_copy(act, 0)
                    d_hid(act, 0)
                with act.Fori(0, BODIES) as i:
                    for s in range(2):
                        dense_act(act, s)

            @block.tensor
            def _(pe):
                if k0 == 0:
                    d_turn(pe, 0)
                    d_first(pe, 0)
                with pe.Fori(0, BODIES) as i:
                    for s in range(2):
                        dense_pe(pe, s)

        def dense_act(act, s):
            d_root1(act, 1 - s)
            d_norm1(act, 1 - s)
            d_copy(act, 1 - s)
            d_root2(act, s)
            d_hid(act, 1 - s)

        def dense_pe(pe, s):
            d_turn(pe, 1 - s)
            d_second(pe, s)
            d_first(pe, 1 - s)

        def sl(t, tile, reg, k=TG):
            return t[:, bass.ds(tile, k)] if reg else t[:, tile:tile + k]

        LOW_BITS = 9
        BINS = 1 << LOW_BITS
        HIGH_BINS = (N >> LOW_BITS) + 1
        PAD_EDGES = EP - E

        def radix_phase(tag, k0, first_pass, bins, load, target, target_row):
            with Phase(nc) as st:
                rec = sb(st, f"{tag}_rec", [P, NT + 2 * TG, 4], I32)
                raw = sb(st, f"{tag}_raw", [P, 3, NT], I32)
                digit_i = sb(st, f"{tag}_digit_i", [P, NT + 2 * TG], I32)
                digit = sb(st, f"{tag}_digit", [P, NT + 2 * TG])
                number_i = sb(st, f"{tag}_number_i", [P, bins], I32)
                number = sb(st, f"{tag}_number", [P, bins])
                count = sb(st, f"{tag}_count", [P, bins])
                before = sb(st, f"{tag}_before", [P, bins])
                total = sb(st, f"{tag}_total", [P, bins])
                hit = sb(st, f"{tag}_hit", [P, bins])
                zeros = sb(st, f"{tag}_zeros", [P, bins])
                lower = sb(st, f"{tag}_lower", [P, P])
                ones = sb(st, f"{tag}_ones", [P, P])
                place = two(sb, st, f"{tag}_place", [P, TG])
                stage = two(sb, st, f"{tag}_stage", [P, TG], I32)
                moved = two(sb, st, f"{tag}_moved", [P, TG, 4], I32)
                ps_lower, ps_total = pb(st, f"{tag}_pslower"), pb(st, f"{tag}_pstotal")
                loaded, ready, cleared, triangle, counted, summed, staged = [sem(st, f"{tag}_{n}") for n in (
                    "loaded", "ready", "cleared", "triangle", "counted", "summed", "staged")]
                sent = two(sem, st, f"{tag}_sent")
                with nc.Block() as block:
                    @block.gpsimd
                    def _(gp):
                        nc.gpsimd.memset(rec[:], 0)
                        nc.gpsimd.memset(raw[:], 0).then_inc(ready, 1)
                        gp.wait_ge(ready, 1)
                        nc.gpsimd.memset(raw[96:P, 0, :], N).then_inc(ready, 1)
                        gp.wait_ge(ready, 2)
                        nc.gpsimd.iota(number_i[:], pattern=[[1, bins]], base=0, channel_multiplier=0)
                        nc.gpsimd.memset(zeros[:], 0.0)
                        nc.gpsimd.memset(count[:], 0.0)
                        nc.gpsimd.memset(ones[:], 1.0)
                        nc.gpsimd.memset(lower[:], 1.0).then_inc(cleared, 1)
                        gp.wait_ge(cleared, 1)
                        nc.gpsimd.affine_select(out=lower[:], in_=lower[:], compare_op=ALU.is_gt, fill=0.0,
                                                base=0, pattern=[[1, P]], channel_multiplier=-1).then_inc(triangle, 1)
                        if first_pass:
                            nc.gpsimd.iota(rec[:, 0:NT, 3], pattern=[[1, NT]], base=0, channel_multiplier=NT)\
                                .then_inc(triangle, 1)

                    @block.sync
                    def _(sp):
                        sp.wait_ge(ready, 2)
                        if first_pass:
                            for n, a in enumerate((src, dst, weight.bitcast(I32))):
                                sp.dma_start(raw[0:E // NT, n, :], a.rearrange("(p t) -> p t", t=NT))\
                                    .then_inc(loaded, 16)
                        else:
                            sp.dma_start(rec[:, 0:NT, :], load.rearrange("(p t) k -> p t k", p=P)).then_inc(loaded, 16)

                    @block.vector
                    def _(dve):
                        ch = Chain(dve, dve_done)
                        V = nc.vector
                        dve.wait_ge(loaded, 48 if first_pass else 16)
                        if first_pass:
                            dve.wait_ge(triangle, 2)
                            for n in range(3):
                                last = V.tensor_copy(rec[:, 0:NT, n], raw[:, n, :])
                            ch.link(last)
                        else:
                            dve.wait_ge(triangle, 1)
                        if first_pass:
                            ch.link(V.tensor_scalar(digit_i[:], rec[:, :, 0], bins - 1, None, ALU.bitwise_and))
                        else:
                            ch.link(V.tensor_scalar(digit_i[:], rec[:, :, 0], LOW_BITS, None, ALU.logical_shift_right))
                        V.tensor_copy(digit[:], digit_i[:])
                        ch.link(V.tensor_copy(number[:], number_i[:]))
                        ch.close()
                        with dve.Fori(0, BODIES) as i:
                            for j in range(2 * TG):
                                t = i * (2 * TG) + j
                                ch.link(V.scalar_tensor_tensor(out=count[:], in0=number[:], scalar=digit[:, bass.ds(t, 1)],
                                                               in1=count[:], op0=ALU.is_equal, op1=ALU.add))
                            ch.close()
                        V.nop().then_inc(counted, 1)
                        take(dve, summed)
                        ch.link(V.tensor_copy(total[:], ps_total[:, 0:bins]))
                        ch.link(V.tensor_tensor_scan(before[:], zeros[:], total[:], 0.0, ALU.add, ALU.add))
                        ch.link(V.tensor_tensor(before[:], before[:], total[:], ALU.subtract))
                        ch.link(V.tensor_tensor(before[:], ps_lower[:, 0:bins], before[:], ALU.add))
                        ch.close()

                    @block.tensor
                    def _(pe):
                        pe.wait_ge(triangle, 1)
                        take(pe, counted)
                        nc.tensor.matmul(ps_lower[:, 0:bins], lower[:], count[:], start=True, stop=True)
                        nc.tensor.matmul(ps_total[:, 0:bins], ones[:], count[:], start=True, stop=True).then_inc(summed, 1)

                with nc.Block() as block:
                    @block.gpsimd
                    def _(gp):
                        bound = gp.to_reg(EP - 1 + target_row)
                        with gp.Fori(0, BODIES) as i:
                            for s in range(2):
                                take(gp, staged)
                                for j in range(TG):
                                    gp.indirect_dma_start(
                                        target, bass.IndirectOffsetOnAxis(ap=stage[s][:, j:j + 1], axis=0),
                                        moved[s][:, j, :], None, bounds_check=bound, oob_is_err=False)\
                                        .then_inc(sent[s], 16)

                    @block.vector
                    def _(dve):
                        ch = Chain(dve, dve_done)
                        V = nc.vector

                        def put(s, tile):
                            for j in range(TG):
                                d = digit[:, bass.ds(tile + j, 1)]
                                V.scalar_tensor_tensor(out=hit[:], in0=number[:], scalar=d, in1=before[:],
                                                       op0=ALU.is_equal, op1=ALU.mult, accum_out=place[s][:, j:j + 1])\
                                    .then_inc(dve_done, 1)
                                ch.n += 1
                                dve.wait_ge(dve_done, ch.n)
                                ch.link(V.scalar_tensor_tensor(out=before[:], in0=number[:], scalar=d, in1=before[:],
                                                               op0=ALU.is_equal, op1=ALU.add))
                            V.tensor_copy(moved[s][:], rec[:, bass.ds(tile, TG), :])
                            V.tensor_scalar(stage[s][:], place[s][:], float(target_row), None, ALU.add)\
                                .then_inc(staged, 1)

                        put(0, 0)
                        put(1, TG)
                        ch.close()
                        n0 = k0 // 2
                        if k0 == 0:
                            V.nop().then_inc(d_taken, 1)
                            d_stats1(dve, ch, 0, 0)
                            d_affine(dve, ch, 0, d_std1, dmv1, dr1, db1, dsd1, d_affine1)
                            ch.close()

                        def step(i, s, more):
                            d_stats1(dve, ch, 1 - s, i + (n0 + s))
                            dve.wait_ge(sent[s], 64 * i + 64)
                            if more:
                                put(s, i * (2 * TG) + (2 + s) * TG)
                            d_affine(dve, ch, 1 - s, d_std1, dmv1, dr1, db1, dsd1, d_affine1)
                            d_residual(dve, ch, s, i + n0)
                            d_final(dve, ch, s)

                        with dve.Fori(0, BODIES - 1) as i:
                            for s in range(2):
                                step(i, s, True)
                            ch.close()
                        for s in range(2):
                            step(BODIES - 1, s, False)
                        ch.close()

                    dense_beside(block, k0)

        assert E % NT == 0 and E // NT >= 96
        radix_phase("ra", 0, True, BINS, None, rec_low, 0)
        radix_phase("rb", 2 * BODIES, False, HIGH_BINS, rec_low, rec_src, 1)

        with Phase(nc) as st:
            recA = [sb(st, f"g_rec{n}", [HALF, 2, P, 4], I32) for n in range(3)]
            kA = [sb(st, f"g_key{n}", [HALF, 2, P]) for n in range(3)]
            first, last_, t1, outA, srcA, dstA, numA, wA = [sb(st, f"g_{n}", [HALF, 2, P]) for n in (
                "first", "last", "t1", "out", "src", "dst", "num", "w")]
            keepA = sb(st, "g_keep", [HALF, 2, P], BF16)
            edge_pads = sb(st, "g_pads", [1, 4], I32)
            g_pad, g_padded, g_ld, g_own, g_field, g_turn, g_keep_ok, g_st = [sem(st, f"g_{n}") for n in (
                "pad", "padded", "ld", "own", "field", "turn", "keep_ok", "stored")]
            psg = [pb(st, f"g_ps{n}") for n in range(3)]
            with nc.Block() as block:
                @block.gpsimd
                def _(gp):
                    nc.gpsimd.memset(edge_pads[:], -1).then_inc(g_pad, 1)
                    nc.gpsimd.iota(entry_src[:, 0:NT, 0], pattern=[[P, NT]], base=1, channel_multiplier=1)

                @block.sync
                def _(sp):
                    take(sp, g_pad)
                    for r in (0, EP + 1):
                        sp.dma_start(rec_src[r:r + 1, :], edge_pads[:]).then_inc(g_padded, 16)
                    sp.wait_ge(g_padded, 32)
                    for n in range(3):
                        for h in range(2):
                            sp.dma_start(recA[n][:, h], rec_src[n + h * HALF * P:n + (h + 1) * HALF * P, :]
                                         .rearrange("(t c) k -> t c k", c=P)).then_inc(g_ld, 16)
                    take(sp, g_keep_ok)
                    sp.dma_start(keep_src[0].rearrange("(h t c) -> t h c", h=2, c=P), keepA[:]).then_inc(g_st, 16)
                    sp.wait_ge(g_st, 16)

                @block.vector
                def _(dve):
                    ch = Chain(dve, dve_done)
                    V = nc.vector
                    dve.wait_ge(g_ld, 16 * 6)
                    for n in range(3):
                        V.tensor_copy(kA[n][:], recA[n][:, :, :, 0])
                    V.tensor_copy(t1[:], recA[1][:, :, :, 1])
                    V.tensor_copy(wA[:].bitcast(I32), recA[1][:, :, :, 2])
                    ch.link(V.tensor_copy(numA[:], recA[1][:, :, :, 3]))
                    V.tensor_scalar(dstA[:], t1[:], float(N - 1), None, ALU.min)
                    V.tensor_scalar(srcA[:], kA[1][:], float(N - 1), None, ALU.min)
                    V.tensor_tensor(first[:], kA[1][:], kA[0][:], ALU.not_equal)
                    V.tensor_tensor(last_[:], kA[1][:], kA[2][:], ALU.not_equal)
                    ch.link(V.tensor_scalar(outA[:], kA[1][:], float(FAR), None, ALU.add))
                    V.tensor_scalar(keepA[:], first[:], -1.0, 1.0, ALU.mult, ALU.add).then_inc(g_keep_ok, 1)
                    V.scalar_tensor_tensor(out=outA[:], in0=last_[:], scalar=-float(FAR), in1=outA[:], op0=ALU.mult,
                                           op1=ALU.add).then_inc(g_field, 1)
                    take(dve, g_turn)
                    V.tensor_copy(k_src[:, 0:NT], psg[0][:, 0:NT])
                    V.tensor_copy(k_dst[:, 0:NT], psg[0][:, NT:2 * NT])
                    V.tensor_copy(k_out[:, 0:NT], psg[1][:, 0:NT])
                    V.tensor_copy(k_w[:], psg[1][:, NT:2 * NT])
                    V.tensor_scalar(entry_src[:, 0:NT, 1], psg[2][:, 0:NT], 1.0, None, ALU.add)
                    ch.close()

                @block.tensor
                def _(pe):
                    take(pe, g_field)
                    for n, f in enumerate((srcA, dstA, outA, wA, numA)):
                        for h in range(2):
                            c = (n % 2) * NT + h * HALF
                            last = nc.tensor.transpose(psg[n // 2][:, c:c + HALF], f[:, h, :], ident[0:HALF, 0:HALF])
                    last.then_inc(g_turn, 1)

        c_got = [sb(main, f"c_got{n}", [P, NT]) for n in range(2)]
        c_got_dst = sb(main, "c_got_dst", [P, NT])
        c_num = sb(main, "c_num", [P, NT])

        def of_edge_src(V, moved, tile, reg):
            return V.tensor_copy(sl(k_pick, tile, reg), moved[:, :, 2])

        def of_src(V, moved, tile, reg):
            V.tensor_copy(sl(c_got[0], tile, reg), moved[:, :, 0])
            V.tensor_copy(sl(c_nts, tile, reg), moved[:, :, 1])
            V.tensor_copy(sl(c_got[1], tile, reg), moved[:, :, 2])
            return V.tensor_copy(sl(c_num, tile, reg), moved[:, :, 3])

        def of_dst(V, moved, tile, reg):
            V.tensor_copy(sl(c_ntd, tile, reg), moved[:, :, 1])
            return V.tensor_copy(sl(c_got_dst, tile, reg), moved[:, :, 2])

        table_phase("tp", 4 * BODIES, [(node_table, 0, i_out, 1, entry_dst, None),
                                       (node_table, 2, k_out, 2, entry_src, None)])
        table_phase("tg", None, [(node_table, 0, k_dst, 4, None, of_edge_src),
                                 (node_table, 0, i_src, 4, None, of_src),
                                 (node_table, 0, i_dst, 4, None, of_dst)])
        K_P1 = 6 * BODIES

        with Phase(nc) as st:
            pf = sb(st, "pf", [P, NT])
            t1, t2, t3 = [sb(st, f"q_t{n}", [P, NT]) for n in range(3)]
            codes = sb(st, "codes", [HALF, 2, 2, P], BF16)
            q_turn, q_code, q_st = [sem(st, f"q_{n}") for n in ("turn", "code", "st")]
            psq = two(pb, st, "psq", (P, GE))
            with nc.Block() as block:
                @block.vector
                def _(dve):
                    ch = Chain(dve, dve_done)
                    V = nc.vector
                    ch.link(V.tensor_copy(pf[:], k_pick[:, 0:NT]))
                    for got, to in ((pf, k_pick), (c_got[0], i_pick)):
                        ch.link(V.tensor_scalar(t1[:], got[:], 0.0, float(NONE + 1), ALU.is_equal, ALU.mult))
                        ch.link(V.scalar_tensor_tensor(out=to[:, 0:NT], in0=got[:], scalar=-1.0, in1=t1[:],
                                                       op0=ALU.add, op1=ALU.add))
                    V.tensor_scalar(t1[:], c_got_dst[:], 0.0, None, ALU.is_equal)
                    ch.link(V.tensor_scalar(t2[:], c_last[:], -1.0, 1.0, ALU.mult, ALU.add))
                    ch.link(V.tensor_tensor(t1[:], t1[:], t2[:], ALU.max))
                    ch.link(V.tensor_scalar(t1[:], t1[:], float(NONE + 1), None, ALU.mult))
                    ch.link(V.scalar_tensor_tensor(out=i_dst1[:, 0:NT], in0=c_got_dst[:], scalar=-1.0, in1=t1[:],
                                                   op0=ALU.add, op1=ALU.add))
                    V.tensor_scalar(i_node1[:, 0:NT], c_got[1][:], -1.0, 0.0, ALU.add, ALU.max)
                    V.tensor_copy(t1[:], entry_dst[:, 0:NT, 0])
                    V.tensor_scalar(t2[:], c_got[0][:], 0.0, None, ALU.is_equal)
                    ch.link(V.tensor_copy(t3[:], i_src[:, 0:NT]))
                    ch.link(V.tensor_tensor(t1[:], t1[:], c_num[:], ALU.is_equal))
                    ch.link(V.tensor_tensor(t1[:], t1[:], t2[:], ALU.mult))
                    ch.link(V.tensor_scalar(t1[:], t1[:], -float(FAR), float(FAR), ALU.mult, ALU.add))
                    ch.link(V.tensor_tensor(i_srcout[:, 0:NT], t1[:], t3[:], ALU.add))
                    take(dve, q_turn)
                    for n in range(2):
                        last = V.tensor_copy(codes[:, n], psq[n][0:HALF, 0:2 * P].rearrange("t (h c) -> t h c", h=2))
                    last.then_inc(q_code, 1)
                    ch.close()

                @block.tensor
                def _(pe):
                    for n, c in enumerate((c_nts, c_ntd)):
                        for h in range(2):
                            last = nc.tensor.transpose(psq[n][0:HALF, h * P:(h + 1) * P],
                                                       c[:, h * HALF:(h + 1) * HALF], ident[:])
                    last.then_inc(q_turn, 1)

                @block.sync
                def _(sp):
                    take(sp, q_code)
                    for n, k in enumerate((NTS, NTD)):
                        sp.dma_start(seq_rows[k].rearrange("(h t c) -> t h c", h=2, c=P), codes[:, n]).then_inc(q_st, 16)
                    sp.wait_ge(q_st, 32)

        PEN = 4

        def hop_phase(tag, table, index, first_hop, last_hop):
            with Phase(nc) as st:
                stage = two(sb, st, f"{tag}_stage", [P, TG], I32)
                rows = two(sb, st, f"{tag}_rows", [P, TG, D])
                scaled = two(sb, st, f"{tag}_scaled", [P, TG, D])
                keep = two(sb, st, f"{tag}_keep", [P, 1, GE], BF16)
                sums = two(sb, st, f"{tag}_sums", [P, GE])
                outr = two(sb, st, f"{tag}_outr", [P, TG, D])
                ps_m = two(pb, st, f"{tag}_psm")
                ps_r = two(pb, st, f"{tag}_psr")
                gathered = two(sem, st, f"{tag}_gathered")
                kept = two(sem, st, f"{tag}_kept")
                stored = two(sem, st, f"{tag}_stored")
                staged, freed, rdy, turned, scanned, scan_sp, back, copied = [sem(st, f"{tag}_{n}") for n in (
                    "staged", "freed", "rdy", "turned", "scanned", "scan_sp", "back", "copied")]
                if last_hop:
                    stage2 = two(sb, st, f"{tag}_stage2", [P, TG], I32)
                    brow = two(sb, st, f"{tag}_brow", [P, TG, D])
                    e1r = two(sb, st, f"{tag}_e1r", [P, TG, D])
                    e2r = two(sb, st, f"{tag}_e2r", [P, TG, D])
                    acc = two(sb, st, f"{tag}_acc", [P, TG, D])
                    stt = two(sb, st, f"{tag}_stt", [P, TG, 6])
                    mv = two(sb, st, f"{tag}_mv", [P, TG, 2])
                    sd = two(sb, st, f"{tag}_sd", [P, TG])
                    rr = two(sb, st, f"{tag}_rr", [P, TG])
                    bb = two(sb, st, f"{tag}_bb", [P, TG])
                    hops_in = two(sem, st, f"{tag}_hops_in")
                    var, std, affine, loads_free = [sem(st, f"{tag}_{n}") for n in ("var", "std", "affine", "loads_free")]
                per = 128 if last_hop else 64
                dense_bodies = BODIES - PEN if first_hop else 0

                with nc.Block() as block:
                    @block.gpsimd
                    def _(gp):
                        bound = gp.to_reg(N - 1 if first_hop else NONE)
                        bound2 = gp.to_reg(N - 1)
                        with gp.Fori(0, BODIES) as i:
                            for s in range(2):
                                take(gp, staged)
                                for j in range(TG):
                                    gp.indirect_dma_start(
                                        rows[s][:, j, :], None, table,
                                        bass.IndirectOffsetOnAxis(ap=stage[s][:, j:j + 1], axis=0),
                                        bounds_check=bound, oob_is_err=False).then_inc(gathered[s], 16)
                                if last_hop:
                                    for j in range(TG):
                                        gp.indirect_dma_start(
                                            brow[s][:, j, :], None, x,
                                            bass.IndirectOffsetOnAxis(ap=stage2[s][:, j:j + 1], axis=0),
                                            bounds_check=bound2, oob_is_err=False).then_inc(gathered[s], 16)

                    @block.sync
                    def _(sp):
                        for s in range(2):
                            sp.nop().then_inc(stored[s], 16)

                        def step(i, s, dense):
                            take(sp, scan_sp)
                            sp.dma_start(keep[s][:], seq_of(keep_src, i, s, 0, 1)).then_inc(kept[s], 16)
                            if last_hop:
                                take(sp, loads_free)
                                sp.dma_start(e1r[s][:], rows_of(e1_rows, i, s)).then_inc(hops_in[s], 16)
                                sp.dma_start(e2r[s][:], rows_of(e2_rows, i, s)).then_inc(hops_in[s], 16)
                            if dense:
                                d_load(sp, i * 2 + (K_P1 + 2 + s), s)
                                d_store(sp, i * 2 + (K_P1 + s), s)
                            sp.wait_ge(copied, 2 * i + (3 + s))
                            sp.dma_start(rows_of(x1_nodes if last_hop else e1_rows if first_hop else e2_rows, i, s),
                                         outr[s][:]).then_inc(stored[s], 16)

                        if dense_bodies:
                            with sp.Fori(0, dense_bodies) as i:
                                for s in range(2):
                                    step(i, s, True)
                            k = K_P1 + 2 * dense_bodies
                            while k < NGROUPS:
                                if k + 2 < NGROUPS:
                                    d_load(sp, k + 2, k % 2)
                                if k == NGROUPS - 1:
                                    sp.wait_ge(d_stored[1 - k % 2], 16 * (1 + (k + 1) // 2))
                                d_store(sp, k, k % 2)
                                k += 1
                        with sp.Fori(dense_bodies, BODIES) as i:
                            for s in range(2):
                                step(i, s, False)
                        for s in range(2):
                            sp.wait_ge(stored[s], 16 * (BODIES + 1))
                            if first_hop:
                                sp.wait_ge(d_stored[s], 16 * (1 + NGROUPS // 2))

                    @block.vector
                    def _(dve):
                        ch = Chain(dve, dve_done)
                        V = nc.vector

                        def put(s, tile):
                            reg = not isinstance(tile, int)
                            if last_hop:
                                V.tensor_copy(stage2[s][:], sl(k_src, tile, reg))
                            V.tensor_copy(stage[s][:], sl(index, tile, reg)).then_inc(staged, 1)

                        ch.link(V.memset(sums[1][:], 0.0))
                        ch.close()
                        V.nop().then_inc(scan_sp, 2)
                        if last_hop:
                            V.nop().then_inc(loads_free, 2)
                        put(0, 0)
                        put(1, TG)
                        n0 = K_P1 // 2

                        def step(i, s, dense):
                            tile = i * (2 * TG) + s * TG
                            if dense:
                                d_stats1(dve, ch, 1 - s, i + (n0 + s))
                            dve.wait_ge(gathered[s], per * i + per)
                            V.tensor_tensor(scaled[s][:], rows[s][:],
                                            k_w[:, bass.ds(tile, TG)].unsqueeze(2).to_broadcast([P, TG, D]),
                                            ALU.mult).then_inc(rdy, 1)
                            if last_hop:
                                dve.wait_ge(hops_in[s], 32 * i + 32)
                                ch.link(V.tensor_tensor(acc[s][:], e1r[s][:], e2r[s][:], ALU.add))
                                V.nop().then_inc(loads_free, 1)
                                ch.link(V.scalar_tensor_tensor(out=acc[s][:], in0=brow[s][:], scalar=5.0,
                                                               in1=acc[s][:], op0=ALU.mult, op1=ALU.add))
                            dve.wait_ge(kept[s], 16 * i + 16)
                            take(dve, turned)
                            put(s, i * (2 * TG) + (2 + s) * TG)
                            ch.link(V.tensor_tensor_scan(sums[s][:], keep[s][:, 0, :], ps_m[s][:],
                                                         sums[1 - s][:, GE - 1:GE], ALU.mult, ALU.add))
                            V.nop().then_inc(scanned, 1)
                            V.nop().then_inc(scan_sp, 1)
                            if last_hop:
                                take(dve, back)
                                ch.link(V.tensor_tensor(acc[s][:], ps_r[s][:].rearrange("p (j f) -> p j f", j=TG),
                                                        acc[s][:], ALU.add))
                                for j in range(TG):
                                    last = V.bn_stats(stt[s][:, j, :], acc[s][:, j, :])
                                ch.link(last)
                                for j in range(TG):
                                    last = V.bn_aggr(mv[s][:, j, :], stt[s][:, j, :])
                                last.then_inc(var, 1)
                                take(dve, std)
                                ch.link(V.reciprocal(rr[s][:], sd[s][:]))
                                V.scalar_tensor_tensor(out=bb[s][:], in0=mv[s][:, :, 0], scalar=-1.0, in1=rr[s][:],
                                                       op0=ALU.mult, op1=ALU.mult).then_inc(affine, 1)
                            if dense:
                                d_affine(dve, ch, 1 - s, d_std1, dmv1, dr1, db1, dsd1, d_affine1)
                                d_residual(dve, ch, s, i + n0)
                                d_final(dve, ch, s)

                        if dense_bodies:
                            with dve.Fori(0, dense_bodies) as i:
                                for s in range(2):
                                    step(i, s, True)
                                ch.close()
                            k = K_P1 + 2 * dense_bodies
                            while k < NGROUPS:
                                s = k % 2
                                if k + 1 < NGROUPS:
                                    d_stats1(dve, ch, 1 - s, (k + 1) // 2)
                                if k + 1 < NGROUPS:
                                    d_affine(dve, ch, 1 - s, d_std1, dmv1, dr1, db1, dsd1, d_affine1)
                                d_residual(dve, ch, s, k // 2)
                                d_final(dve, ch, s)
                                k += 1
                            ch.close()
                        with dve.Fori(dense_bodies, BODIES) as i:
                            for s in range(2):
                                step(i, s, False)
                            ch.close()

                    @block.scalar
                    def _(act):
                        nc.scalar.preload_act_table(ACT.Sqrt)
                        nc.scalar.nop().then_inc(copied, 2)

                        def step(i, s, dense):
                            if dense:
                                d_root1(act, 1 - s)
                                d_norm1(act, 1 - s)
                            if last_hop:
                                act.wait_ge(stored[s], 16 * i + 16)
                                take(act, var)
                                nc.scalar.activation(sd[s][:], mv[s][:, :, 1], ACT.Sqrt,
                                                     bias=eps_col[:, EPS16:EPS16 + 1]).then_inc(std, 1)
                                take(act, affine)
                                for j in range(TG):
                                    last = nc.scalar.activation(outr[s][:, j, :], acc[s][:, j, :], ACT.Identity,
                                                                bias=bb[s][:, j:j + 1], scale=rr[s][:, j:j + 1])
                                last.then_inc(copied, 1)
                            else:
                                act.wait_ge(stored[s], 16 * i + 16)
                                take(act, back)
                                nc.scalar.activation(outr[s][:].rearrange("p j f -> p (j f)"), ps_r[s][:],
                                                     ACT.Copy).then_inc(copied, 1)
                            if dense:
                                d_copy(act, 1 - s)
                                d_root2(act, s)
                                d_hid(act, 1 - s)

                        if dense_bodies:
                            with act.Fori(0, dense_bodies) as i:
                                for s in range(2):
                                    step(i, s, True)
                            k = K_P1 + 2 * dense_bodies
                            while k < NGROUPS:
                                s = k % 2
                                if k + 1 < NGROUPS:
                                    d_root1(act, 1 - s)
                                    d_norm1(act, 1 - s)
                                if k + 1 < NGROUPS:
                                    d_copy(act, 1 - s)
                                d_root2(act, s)
                                if k + 1 < NGROUPS:
                                    d_hid(act, 1 - s)
                                k += 1
                        with act.Fori(dense_bodies, BODIES) as i:
                            for s in range(2):
                                step(i, s, False)

                    @block.tensor
                    def _(pe):
                        def step(i, s, dense):
                            take(pe, rdy)
                            for j in range(TG):
                                last = nc.tensor.transpose(ps_m[s][:, j * P:(j + 1) * P], scaled[s][:, j, :], ident[:])
                            last.then_inc(turned, 1)
                            if dense:
                                d_turn(pe, 1 - s)
                            pe.wait_ge(copied, 2 * i + (1 + s))
                            take(pe, scanned)
                            for j in range(TG):
                                last = nc.tensor.transpose(ps_r[s][:, j * P:(j + 1) * P],
                                                           sums[s][:, j * P:(j + 1) * P], ident[:])
                            last.then_inc(back, 1)
                            if dense:
                                d_second(pe, s)
                                d_first(pe, 1 - s)

                        if dense_bodies:
                            with pe.Fori(0, dense_bodies) as i:
                                for s in range(2):
                                    step(i, s, True)
                            k = K_P1 + 2 * dense_bodies
                            while k < NGROUPS:
                                s = k % 2
                                if k + 1 < NGROUPS:
                                    d_turn(pe, 1 - s)
                                d_second(pe, s)
                                if k + 1 < NGROUPS:
                                    d_first(pe, 1 - s)
                                k += 1
                        with pe.Fori(dense_bodies, BODIES) as i:
                            for s in range(2):
                                step(i, s, False)

        hop_phase("h1", x, k_dst, True, False)
        dense_psum.close()
        hop_phase("h2", e1_rows, k_pick, False, False)
        hop_phase("h3", e2_rows, k_pick, False, True)

        def norm_stats(V, ch, y, stt, mv, s, var):
            for j in range(TG):
                last = V.bn_stats(stt[s][:, j, :], y[s][:, j, :])
            ch.link(last)
            for j in range(TG):
                last = V.bn_aggr(mv[s][:, j, :], stt[s][:, j, :])
            last.then_inc(var, 1)

        def norm_rows(act, out_rows, y, rr, bb, s):
            for j in range(TG):
                last = nc.scalar.activation(out_rows[s][:, j, :], y[s][:, j, :], ACT.Identity,
                                            bias=bb[s][:, j:j + 1], scale=rr[s][:, j:j + 1])
            return last

        def turn(out_bank, rows3d):
            for j in range(TG):
                last = nc.tensor.transpose(out_bank[:, j * P:(j + 1) * P], rows3d[:, j, :], ident[:])
            return last

        def tiles(t):
            return t.rearrange("p (j f) -> p j f", j=TG)

        def cols(c, i, s):
            return c[:, bass.ds(i * (2 * TG) + s * TG, TG)].unsqueeze(2).to_broadcast([P, TG, D])

        def bodies(eng, order, step, ch=None):
            with eng.Fori(0, BODIES - 1) as i:
                for o, s in enumerate(order):
                    step(i, o, s, True)
                if ch:
                    ch.close()
            for o, s in enumerate(order):
                step(BODIES - 1, o, s, False)
            if ch:
                ch.close()

        def local_put(V, which, aff, stage, b, s, aff_ok, staged):
            t = b * (2 * TG) + s * TG
            if which is not None:
                V.tensor_copy(aff[s][:], local[which][:, bass.ds(t, TG), :]).then_inc(aff_ok, 1)
            V.tensor_copy(stage[s][:], i_pick[:, bass.ds(t, TG)]).then_inc(staged, 1)

        def local_rows(act, i, s, a0_in, aff_ok, x_ok, xs, a0r, aff):
            act.wait_ge(a0_in[s], 16 * i + 16)
            take(act, aff_ok)
            for j in range(TG):
                last = nc.scalar.activation(xs[s][:, j, :], a0r[s][:, j, :], ACT.Identity,
                                            bias=aff[s][:, j, 1:2], scale=aff[s][:, j, 0:1])
            last.then_inc(x_ok, 1)

        def picks(gp, bound, table, xs, stage, picked, s):
            for j in range(TG):
                gp.indirect_dma_start(xs[s][:, j, :], None, table,
                                      bass.IndirectOffsetOnAxis(ap=stage[s][:, j:j + 1], axis=0),
                                      bounds_check=bound, oob_is_err=False).then_inc(picked[s], 16)

        with Phase(nc) as st:
            xr, dr, outd = [two(sb, st, n, [P, TG, D]) for n in ("b_xr", "b_dr", "b_out")]
            stage = two(sb, st, "b_stage", [P, 3, TG], I32)
            stt = two(sb, st, "b_stt", [P, TG, 6])
            mv = two(sb, st, "b_mv", [P, TG, 2])
            sd, rr, bb = [two(sb, st, n, [P, TG]) for n in ("b_sd", "b_rr", "b_bb")]
            got, src_got, picked, src_st, dst_st = [two(sem, st, f"b_{n}") for n in (
                "got", "src_got", "picked", "src_st", "dst_st")]
            staged, stats_ok, std, affine, normed = [sem(st, f"b_{n}") for n in (
                "staged", "stats", "std", "affine", "normed")]
            with nc.Block() as block:
                @block.gpsimd
                def _(gp):
                    bound = gp.to_reg(EP - 1)
                    bound_x = gp.to_reg(N - 1)

                    def load(i, s):
                        if not isinstance(i, int) or i:
                            gp.wait_ge(src_st[s], 16 * i)
                        take(gp, staged)
                        for t, k, table, b, q in ((xr, 0, x1_nodes, bound, src_got), (dr, 1, x, bound_x, got)):
                            for j in range(TG):
                                gp.indirect_dma_start(t[s][:, j, :], None, table,
                                                      bass.IndirectOffsetOnAxis(ap=stage[s][:, k, j:j + 1], axis=0),
                                                      bounds_check=b, oob_is_err=False).then_inc(q[s], 16)

                    load(0, 0)
                    load(0, 1)

                    def step(i, o, s, more):
                        take(gp, normed)
                        for j in range(TG):
                            gp.indirect_dma_start(outd[s][:, j, :], None, x1_nodes,
                                                  bass.IndirectOffsetOnAxis(ap=stage[s][:, 2, j:j + 1], axis=0),
                                                  bounds_check=bound, oob_is_err=False).then_inc(picked[s], 16)
                        if more:
                            load(i + 1, s)

                    bodies(gp, (0, 1), step)

                @block.sync
                def _(sp):
                    for s in range(2):
                        sp.nop().then_inc(dst_st[s], 16)

                    def step(i, o, s, more):
                        sp.wait_ge(src_got[s], 64 * i + 64)
                        sp.dma_start(rows_of(src_x1, i, s), xr[s][:]).then_inc(src_st[s], 16)
                        sp.wait_ge(picked[s], 64 * i + 64)
                        sp.dma_start(rows_of(x1_rows, i, s), outd[s][:]).then_inc(dst_st[s], 16)

                    bodies(sp, (0, 1), step)
                    for s in range(2):
                        sp.wait_ge(src_st[s], 16 * BODIES)
                        sp.wait_ge(dst_st[s], 16 * (BODIES + 1))

                @block.vector
                def _(dve):
                    ch = Chain(dve, dve_done)
                    V = nc.vector

                    def put(b, s):
                        t = b * (2 * TG) + s * TG
                        V.tensor_copy(stage[s][:, 0, :], i_node1[:, bass.ds(t, TG)])
                        V.tensor_copy(stage[s][:, 1, :], i_dst[:, bass.ds(t, TG)])
                        V.tensor_copy(stage[s][:, 2, :], i_dst1[:, bass.ds(t, TG)]).then_inc(staged, 1)

                    put(0, 0)
                    put(0, 1)

                    def step(i, o, s, more):
                        t = i * (2 * TG) + s * TG
                        dve.wait_ge(src_got[s], 64 * i + 64)
                        for j in range(TG):
                            last = V.bn_stats(src_stats[:, bass.ds(t + j, 1), :], xr[s][:, j, :])
                        ch.link(last)
                        dve.wait_ge(got[s], 64 * i + 64)
                        norm_stats(V, ch, dr, stt, mv, s, stats_ok)
                        take(dve, std)
                        ch.link(V.reciprocal(rr[s][:], sd[s][:]))
                        ch.link(V.tensor_tensor(rr[s][:], rr[s][:], c_last[:, bass.ds(t, TG)], ALU.mult))
                        V.scalar_tensor_tensor(out=bb[s][:], in0=mv[s][:, :, 0], scalar=-1.0, in1=rr[s][:],
                                               op0=ALU.mult, op1=ALU.mult).then_inc(affine, 1)
                        if more:
                            dve.wait_ge(picked[s], 64 * i + 64)
                            put(i + 1, s)

                    bodies(dve, (0, 1), step, ch)

                @block.scalar
                def _(act):
                    nc.scalar.preload_act_table(ACT.Sqrt)

                    def step(i, o, s, more):
                        take(act, stats_ok)
                        nc.scalar.activation(sd[s][:], mv[s][:, :, 1], ACT.Sqrt, bias=eps_col[:, EPS_1:EPS_1 + 1])\
                            .then_inc(std, 1)
                        act.wait_ge(dst_st[s], 16 * i + 16)
                        take(act, affine)
                        norm_rows(act, outd, dr, rr, bb, s).then_inc(normed, 1)

                    bodies(act, (0, 1), step)

        with Phase(nc) as st:
            mean = sb(st, "l_mean", [P, NT])
            diff = sb(st, "l_diff", [P, NT])
            vv = sb(st, "l_var", [P, NT])
            root = [sb(st, f"l_root{n}", [P, NT]) for n in range(2)]
            l_var, l_root = [sem(st, f"l_{n}s") for n in ("var", "root")]
            with nc.Block() as block:
                @block.vector
                def _(dve):
                    ch = Chain(dve, dve_done)
                    V = nc.vector
                    S = src_stats
                    V.tensor_tensor(mean[:], S[:, :, 1], S[:, :, 4], ALU.add)
                    V.tensor_tensor(diff[:], S[:, :, 1], S[:, :, 4], ALU.subtract)
                    ch.link(V.tensor_tensor(vv[:], S[:, :, 2], S[:, :, 5], ALU.add))
                    V.tensor_scalar(mean[:], mean[:], 0.5, None, ALU.mult)
                    V.tensor_scalar(vv[:], vv[:], 1.0 / D, None, ALU.mult)
                    ch.link(V.tensor_tensor(diff[:], diff[:], diff[:], ALU.mult))
                    V.scalar_tensor_tensor(out=vv[:], in0=diff[:], scalar=0.25, in1=vv[:], op0=ALU.mult,
                                           op1=ALU.add).then_inc(l_var, 1)
                    take(dve, l_root)
                    for n in range(2):
                        last = V.reciprocal(local[n][:, :, 0], root[n][:])
                    ch.link(last)
                    for n in range(2):
                        V.scalar_tensor_tensor(out=local[n][:, :, 1], in0=mean[:], scalar=-1.0,
                                               in1=local[n][:, :, 0], op0=ALU.mult, op1=ALU.mult)
                    ch.close()

                @block.scalar
                def _(act):
                    nc.scalar.preload_act_table(ACT.Sqrt)
                    take(act, l_var)
                    for n, (c, e) in enumerate(((1.0, EPS1), (CS, EPS_SQ))):
                        last = nc.scalar.activation(root[n][:], vv[:], ACT.Sqrt, bias=eps_col[:, e:e + 1], scale=c)
                    last.then_inc(l_root, 1)

        with Phase(nc) as st:
            xs, x1r = [two(sb, st, n, [P, TG, D]) for n in ("a_xs", "a_x1r")]
            masks = two(sb, st, "a_masks", [P, 5, GE], BF16)
            onehot = two(sb, st, "a_onehot", [ETYPES, GE])
            sT, dT = [[sb(st, f"{n}{t}", [P, GE]) for t in range(NTYPES)] for n in ("a_sT", "a_dT")]
            kT = [sb(st, f"a_kT{t}", [P, GE]) for t in range(ETYPES)]
            prod = sb(st, "a_prod", [P, GE])
            pri_e, q_all, lg, mx, msg = [two(sb, st, n, [P, GE]) for n in ("a_pri", "a_q", "a_lg", "a_mx", "a_msg")]
            b_sT, b_k, b_m, b_dT, b_q, b_l, b_p = [pb(st, f"a_ps{n}") for n in range(7)]
            xs_in, x1_in, masks_in, msg_st, lm_st = [two(sem, st, f"a_{n}") for n in (
                "xs_in", "x1_in", "masks_in", "msg_st", "lm_st")]
            (in_free, xs_free, s_turned, s_copied, s_masked, k_ok, k_copied, k_masked, m_ok,
             m_copied, x1_turned, x1_copied, x1_masked, q_ok, prod_ok, l_ok, pri_ok, pri_copied, lg_ok, mx_ok) = [
                sem(st, f"a_{n}") for n in (
                    "in_free", "xs_free", "s_turned", "s_copied", "s_masked", "k_ok",
                    "k_copied", "k_masked", "m_ok", "m_copied", "x1_turned", "x1_copied", "x1_masked", "q_ok",
                    "prod_ok", "l_ok", "pri_ok", "pri_copied", "lg_ok", "mx_ok")]
            ORDER = (1, 0)

            def body_of(i):
                return (BODIES - 1) - i

            with nc.Block() as block:
                @block.sync
                def _(sp):
                    for s in range(2):
                        sp.nop().then_inc(msg_st[s], 16)
                        sp.nop().then_inc(lm_st[s], 32)

                    def load_xs(b, s):
                        sp.dma_start(xs[s][:], rows_of(src_x1, b, s)).then_inc(xs_in[s], 16)

                    def load_rest(b, s):
                        sp.dma_start(x1r[s][:], rows_of(x1_rows, b, s)).then_inc(x1_in[s], 16)
                        sp.dma_start(masks[s][:], seq_of(seq_rows, b, s, NOTLAST, NTD + 1)).then_inc(masks_in[s], 16)
                        sp.dma_start(onehot[s][:], onehot_rows[:, bass.ds(b * BODY + s * GE, GE)])\
                            .then_inc(masks_in[s], 16)

                    for s in ORDER:
                        load_xs(BODIES - 1, s)
                        load_rest(BODIES - 1, s)

                    def step(i, o, s, more):
                        b = body_of(i)
                        if more:
                            take(sp, xs_free)
                            load_xs(b - 1, s)
                        sp.wait_ge(m_copied, 2 * i + (o + 1))
                        sp.dma_start(lrm_of(b, s, 2, 3), msg[s][:].unsqueeze(1)).then_inc(msg_st[s], 16)
                        take(sp, lg_ok)
                        sp.dma_start(lrm_of(b, s, 0, 1), lg[s][:].unsqueeze(1)).then_inc(lm_st[s], 16)
                        take(sp, mx_ok)
                        sp.dma_start(lrm_of(b, s, 1, 2), mx[s][:].unsqueeze(1)).then_inc(lm_st[s], 16)
                        if more:
                            take(sp, in_free)
                            load_rest(b - 1, s)

                    bodies(sp, ORDER, step)
                    for s in range(2):
                        sp.wait_ge(msg_st[s], 16 * (BODIES + 1))
                        sp.wait_ge(lm_st[s], 32 * (BODIES + 1))

                @block.scalar
                def _(act):
                    def step(i, o, s, more):
                        take(act, x1_turned)
                        nc.scalar.activation(dT[0][:], b_dT[:], ACT.Copy).then_inc(x1_copied, 1)
                        take(act, pri_ok)
                        nc.scalar.activation(pri_e[s][:], b_p[:], ACT.Copy).then_inc(pri_copied, 1)
                        take(act, s_turned)
                        nc.scalar.activation(sT[0][:], b_sT[:], ACT.Copy).then_inc(s_copied, 1)
                        take(act, k_ok)
                        nc.scalar.activation(kT[0][:], b_k[:], ACT.Copy).then_inc(k_copied, 1)
                        act.wait_ge(msg_st[s], 16 * i + 16)
                        take(act, m_ok)
                        nc.scalar.activation(msg[s][:], b_m[:], ACT.Copy).then_inc(m_copied, 1)

                    bodies(act, ORDER, step)

                @block.vector
                def _(dve):
                    ch = Chain(dve, dve_done)
                    V = nc.vector
                    V.memset(q_all[0][:], 0.0)
                    ch.link(V.memset(mx[0][:], 0.0))
                    ch.close()

                    def step(i, o, s, more):
                        dve.wait_ge(masks_in[s], 32 * i + 32)
                        take(dve, x1_copied)
                        for t in range(1, NTYPES):
                            V.scalar_tensor_tensor(out=dT[t][:], in0=masks[s][:, NTD - NOTLAST, :], scalar=float(t),
                                                   in1=b_dT[:], op0=ALU.is_equal, op1=ALU.mult).then_inc(x1_masked, 1)
                        take(dve, q_ok)
                        ch.link(V.tensor_tensor_scan(q_all[s][:, ::-1], masks[s][:, 0, ::-1], b_q[:, ::-1],
                                                     q_all[1 - s][:, 0:1], ALU.mult, ALU.add))
                        take(dve, s_copied)
                        if more:
                            V.nop().then_inc(xs_free, 1)
                        for t in range(1, NTYPES):
                            V.scalar_tensor_tensor(out=sT[t][:], in0=masks[s][:, NTS - NOTLAST, :], scalar=float(t),
                                                   in1=b_sT[:], op0=ALU.is_equal, op1=ALU.mult).then_inc(s_masked, 1)
                        take(dve, k_copied)
                        for t in range(1, ETYPES):
                            V.scalar_tensor_tensor(out=kT[t][:], in0=masks[s][:, ET - NOTLAST, :], scalar=float(t),
                                                   in1=b_k[:], op0=ALU.is_equal, op1=ALU.mult).then_inc(k_masked, 1)
                        dve.wait_ge(m_copied, 2 * i + (o + 1))
                        V.tensor_tensor(prod[:], q_all[s][:], b_m[:], ALU.mult).then_inc(prod_ok, 1)
                        take(dve, l_ok)
                        take(dve, pri_copied)
                        dve.wait_ge(lm_st[s], 32 * i + 32)
                        ch.link(V.tensor_tensor(lg[s][:], pri_e[s][:], b_l[:], ALU.mult))
                        V.nop().then_inc(lg_ok, 1)
                        ch.link(V.tensor_tensor_scan(mx[s][:, ::-1], masks[s][:, 1, ::-1], lg[s][:, ::-1],
                                                     mx[1 - s][:, 0:1], ALU.add, ALU.max))
                        V.nop().then_inc(mx_ok, 1)
                        V.nop().then_inc(in_free, 1)

                    bodies(dve, ORDER, step, ch)

                @block.tensor
                def _(pe):
                    def step(i, o, s, more):
                        pe.wait_ge(x1_in[s], 16 * i + 16)
                        turn(b_dT, x1r[s]).then_inc(x1_turned, 1)
                        pe.wait_ge(masks_in[s], 32 * i + 32)
                        nc.tensor.matmul(b_p[:], pri[:], onehot[s][:], start=True, stop=True).then_inc(pri_ok, 1)
                        pe.wait_ge(xs_in[s], 16 * i + 16)
                        turn(b_sT, xs[s]).then_inc(s_turned, 1)
                        take(pe, x1_masked, 2)
                        for t in range(NTYPES):
                            last = nc.tensor.matmul(b_q[:], wk[:, t, :], dT[t][:], start=(t == 0),
                                                    stop=(t == NTYPES - 1))
                        last.then_inc(q_ok, 1)
                        take(pe, s_masked, 2)
                        for t in range(NTYPES):
                            last = nc.tensor.matmul(b_k[:], wk[:, t, :], sT[t][:], start=(t == 0),
                                                    stop=(t == NTYPES - 1))
                        last.then_inc(k_ok, 1)
                        take(pe, k_masked, 3)
                        for t in range(ETYPES):
                            last = nc.tensor.matmul(b_m[:], ra[:, t, :], kT[t][:], start=(t == 0),
                                                    stop=(t == ETYPES - 1))
                        last.then_inc(m_ok, 1)
                        take(pe, prod_ok)
                        nc.tensor.matmul(b_l[:], head_ones[:], prod[:], start=True, stop=True).then_inc(l_ok, 1)

                    bodies(pe, ORDER, step)

        with Phase(nc) as st:
            lr = two(sb, st, "s_lr", [P, 3, GE])
            masks = two(sb, st, "s_masks", [P, 2, GE], BF16)
            code = two(sb, st, "s_code", [P, 1, GE], BF16)
            x1r, hr, y, outr = [two(sb, st, n, [P, TG, D]) for n in ("s_x1r", "s_hr", "s_y", "s_outr")]
            mb, ex, es, nm = [two(sb, st, n, [P, GE]) for n in ("s_mb", "s_ex", "s_es", "s_nm")]
            hT = [sb(st, f"s_hT{t}", [P, GE]) for t in range(NTYPES)]
            den = two(sb, st, "s_den", [P, TG, HEADS])
            stt = two(sb, st, "s_stt", [P, TG, 6])
            mv = two(sb, st, "s_mv", [P, TG, 2])
            sd, rr, bb = [two(sb, st, n, [P, TG]) for n in ("s_sd", "s_rr", "s_bb")]
            b_es, b_nm = two(pb, st, "s_bes"), two(pb, st, "s_bnm")
            b_h, b_a = pb(st, "s_bh"), pb(st, "s_ba")
            lr_in, masks_in, x1_in, x2_st = [two(sem, st, f"s_{n}") for n in ("lr_in", "masks_in", "x1_in", "x2_st")]
            (in_free, sub_ok, ex_ok, sums_ok, sums_turned, h_ok, h_turned, h_copied, h_masked, a_ok, var, std,
             affine, x2_ok) = [sem(st, f"s_{n}") for n in (
                "in_free", "sub_ok", "ex_ok", "sums_ok", "sums_turned", "h_ok", "h_turned", "h_copied", "h_masked",
                "a_ok", "var", "std", "affine", "x2_ok")]
            with nc.Block() as block:
                @block.sync
                def _(sp):
                    for s in range(2):
                        sp.nop().then_inc(x2_st[s], 16)
                    with sp.Fori(0, BODIES) as i:
                        for s in range(2):
                            take(sp, in_free)
                            sp.dma_start(lr[s][:], lrm_of(i, s, 0, 3)).then_inc(lr_in[s], 16)
                            sp.dma_start(masks[s][:], seq_of(seq_rows, i, s, KEEP, NFIRST + 1)).then_inc(masks_in[s], 16)
                            sp.dma_start(code[s][:], seq_of(seq_rows, i, s, NTD, NTD + 1)).then_inc(masks_in[s], 16)
                            sp.dma_start(x1r[s][:], rows_of(x1_rows, i, s)).then_inc(x1_in[s], 16)
                        for s in range(2):
                            take(sp, x2_ok)
                            sp.dma_start(rows_of(x2_rows, i, s), outr[s][:]).then_inc(x2_st[s], 16)
                    for s in range(2):
                        sp.wait_ge(x2_st[s], 16 * (BODIES + 1))

                @block.scalar
                def _(act):
                    nc.scalar.preload_act_table(ACT.Exp)
                    with act.Fori(0, BODIES) as i:
                        for s in range(2):
                            take(act, sub_ok)
                            nc.scalar.activation(ex[s][:], ex[s][:], ACT.Exp).then_inc(ex_ok, 1)
                        for s in range(2):
                            take(act, h_turned)
                            nc.scalar.activation(hT[0][:], b_h[:], ACT.Copy).then_inc(h_copied, 1)
                            take(act, var)
                            nc.scalar.activation(sd[s][:], mv[s][:, :, 1], ACT.Sqrt, bias=eps_col[:, EPS1:EPS1 + 1])\
                                .then_inc(std, 1)
                            act.wait_ge(x2_st[s], 16 * i + 16)
                            take(act, affine)
                            norm_rows(act, outr, y, rr, bb, s).then_inc(x2_ok, 1)

                @block.vector
                def _(dve):
                    ch = Chain(dve, dve_done)
                    V = nc.vector
                    for t in (mb, es, nm):
                        last = V.memset(t[1][:], 0.0)
                    ch.link(last)
                    V.nop().then_inc(in_free, 2)
                    ch.close()
                    with dve.Fori(0, BODIES) as i:
                        for s in range(2):
                            dve.wait_ge(masks_in[s], 32 * i + 32)
                            dve.wait_ge(lr_in[s], 16 * i + 16)
                            ch.link(V.tensor_tensor_scan(mb[s][:], masks[s][:, 1, :], lr[s][:, 1, :],
                                                         mb[1 - s][:, GE - 1:GE], ALU.add, ALU.max))
                            V.tensor_tensor(ex[s][:], lr[s][:, 0, :], mb[s][:], ALU.subtract).then_inc(sub_ok, 1)
                        for s in range(2):
                            take(dve, ex_ok)
                            V.tensor_tensor_scan(es[s][:], masks[s][:, 0, :], ex[s][:], es[1 - s][:, GE - 1:GE],
                                                 ALU.mult, ALU.add)
                            ch.link(V.tensor_tensor(lr[s][:, 2, :], lr[s][:, 2, :], ex[s][:], ALU.mult))
                            ch.link(V.tensor_tensor_scan(nm[s][:], masks[s][:, 0, :], lr[s][:, 2, :],
                                                         nm[1 - s][:, GE - 1:GE], ALU.mult, ALU.add))
                            V.nop().then_inc(sums_ok, 1)
                        for s in range(2):
                            take(dve, sums_turned)
                            ch.link(V.tensor_scalar(den[s][:], tiles(b_es[s][:])[:, :, ::HD], 1.0, None, ALU.max))
                            ch.link(V.reciprocal(den[s][:], den[s][:]))
                            V.tensor_tensor(hr[s][:].rearrange("p j (h r) -> p (j h) r", r=HD),
                                            b_nm[s][:].rearrange("p (k r) -> p k r", r=HD),
                                            den[s][:].rearrange("p j h -> p (j h)").unsqueeze(2)
                                            .to_broadcast([P, TG * HEADS, HD]), ALU.mult).then_inc(h_ok, 1)
                            take(dve, h_copied)
                            for t in range(1, NTYPES):
                                V.scalar_tensor_tensor(out=hT[t][:], in0=code[s][:, 0, :], scalar=float(t), in1=b_h[:],
                                                       op0=ALU.is_equal, op1=ALU.mult).then_inc(h_masked, 1)
                            dve.wait_ge(x1_in[s], 16 * i + 16)
                            take(dve, a_ok)
                            ch.link(V.scalar_tensor_tensor(out=y[s][:], in0=tiles(b_a[:]), scalar=0.0, in1=x1r[s][:],
                                                           op0=ALU.max, op1=ALU.add))
                            V.nop().then_inc(in_free, 1)
                            norm_stats(V, ch, y, stt, mv, s, var)
                            take(dve, std)
                            ch.link(V.reciprocal(rr[s][:], sd[s][:]))
                            V.scalar_tensor_tensor(out=bb[s][:], in0=mv[s][:, :, 0], scalar=-1.0, in1=rr[s][:],
                                                   op0=ALU.mult, op1=ALU.mult).then_inc(affine, 1)
                        ch.close()

                @block.tensor
                def _(pe):
                    with pe.Fori(0, BODIES) as i:
                        for s in range(2):
                            take(pe, sums_ok)
                            turn(b_es[s], tiles(es[s][:]))
                            turn(b_nm[s], tiles(nm[s][:])).then_inc(sums_turned, 1)
                        for s in range(2):
                            take(pe, h_ok)
                            turn(b_h, hr[s]).then_inc(h_turned, 1)
                            take(pe, h_masked, 2)
                            for j in range(TG):
                                for t in range(NTYPES):
                                    last = nc.tensor.matmul(b_a[:, j * P:(j + 1) * P], hT[t][:, j * P:(j + 1) * P],
                                                            wa[:, t, :], start=(t == 0), stop=(t == NTYPES - 1))
                            last.then_inc(a_ok, 1)

        with Phase(nc) as st:
            a0r, xs, x2r, y, outr = [two(sb, st, n, [P, TG, D]) for n in ("m_a0r", "m_xs", "m_x2r", "m_y", "m_outr")]
            aff = two(sb, st, "m_aff", [P, TG, 2])
            stage = two(sb, st, "m_stage", [P, TG], I32)
            keep = two(sb, st, "m_keep", [P, 1, GE], BF16)
            sums = two(sb, st, "m_sums", [P, GE])
            stt = two(sb, st, "m_stt", [P, TG, 6])
            mv = two(sb, st, "m_mv", [P, TG, 2])
            sd, rr, bb = [two(sb, st, n, [P, TG]) for n in ("m_sd", "m_rr", "m_bb")]
            b_s, b_r = two(pb, st, "m_bs"), two(pb, st, "m_br")
            a0_in, d_in, picked, x3_st = [two(sem, st, f"m_{n}") for n in ("a0_in", "d_in", "picked", "x3_st")]
            (aff_ok, x_ok, staged, a0_free, d_free2, turned, scanned, back, var, std, affine, x3_ok) = [
                sem(st, f"m_{n}") for n in ("aff_ok", "x_ok", "staged", "a0_free", "d_free", "turned", "scanned",
                                            "back", "var", "std", "affine", "x3_ok")]
            with nc.Block() as block:
                @block.sync
                def _(sp):
                    for s in range(2):
                        sp.nop().then_inc(x3_st[s], 16)

                    def load_a0(b, s):
                        sp.dma_start(a0r[s][:], rows_of(src_x1, b, s)).then_inc(a0_in[s], 16)

                    def load_rest(b, s):
                        sp.dma_start(x2r[s][:], rows_of(x2_rows, b, s)).then_inc(d_in[s], 16)
                        sp.dma_start(keep[s][:], seq_of(seq_rows, b, s, KEEP, KEEP + 1)).then_inc(d_in[s], 16)

                    for s in range(2):
                        load_a0(0, s)
                        load_rest(0, s)

                    def step(i, o, s, more):
                        if more:
                            take(sp, a0_free)
                            load_a0(i + 1, s)
                            take(sp, d_free2)
                            load_rest(i + 1, s)
                        take(sp, x3_ok)
                        sp.dma_start(rows_of(x3s_rows, i, s), outr[s][:]).then_inc(x3_st[s], 16)

                    bodies(sp, (0, 1), step)
                    for s in range(2):
                        sp.wait_ge(x3_st[s], 16 * (BODIES + 1))

                @block.gpsimd
                def _(gp):
                    bound = gp.to_reg(EP - 1)
                    with gp.Fori(0, BODIES) as i:
                        for s in range(2):
                            take(gp, staged)
                            take(gp, x_ok)
                            picks(gp, bound, x2_rows, xs, stage, picked, s)

                @block.scalar
                def _(act):
                    nc.scalar.preload_act_table(ACT.Sqrt)
                    for s in range(2):
                        local_rows(act, 0, s, a0_in, aff_ok, x_ok, xs, a0r, aff)

                    def step(i, o, s, more):
                        if more:
                            local_rows(act, i + 1, s, a0_in, aff_ok, x_ok, xs, a0r, aff)
                        take(act, var)
                        nc.scalar.activation(sd[s][:], mv[s][:, :, 1], ACT.Sqrt, bias=eps_col[:, EPS_M:EPS_M + 1])\
                            .then_inc(std, 1)
                        act.wait_ge(x3_st[s], 16 * i + 16)
                        take(act, affine)
                        norm_rows(act, outr, y, rr, bb, s).then_inc(x3_ok, 1)

                    bodies(act, (0, 1), step)

                @block.vector
                def _(dve):
                    ch = Chain(dve, dve_done)
                    V = nc.vector
                    ch.link(V.memset(sums[1][:], 0.0))
                    ch.close()
                    for s in range(2):
                        local_put(V, 0, aff, stage, 0, s, aff_ok, staged)

                    def step(i, o, s, more):
                        dve.wait_ge(d_in[s], 32 * i + 32)
                        take(dve, turned)
                        if more:
                            local_put(V, 0, aff, stage, i + 1, s, aff_ok, staged)
                            V.nop().then_inc(a0_free, 1)
                        ch.link(V.tensor_tensor_scan(sums[s][:], keep[s][:, 0, :], b_s[s][:], sums[1 - s][:, GE - 1:GE],
                                                     ALU.mult, ALU.add))
                        V.nop().then_inc(scanned, 1)
                        take(dve, back)
                        ch.link(V.tensor_tensor(y[s][:], tiles(b_r[s][:]), cols(c_third, i, s), ALU.mult))
                        ch.link(V.tensor_tensor(y[s][:], y[s][:], x2r[s][:], ALU.add))
                        V.nop().then_inc(d_free2, 1)
                        norm_stats(V, ch, y, stt, mv, s, var)
                        take(dve, std)
                        ch.link(V.reciprocal(rr[s][:], sd[s][:]))
                        ch.link(V.tensor_tensor(rr[s][:], rr[s][:],
                                                c_dinv[:, bass.ds(i * (2 * TG) + s * TG, TG)], ALU.mult))
                        V.scalar_tensor_tensor(out=bb[s][:], in0=mv[s][:, :, 0], scalar=-1.0, in1=rr[s][:],
                                               op0=ALU.mult, op1=ALU.mult).then_inc(affine, 1)

                    bodies(dve, (0, 1), step, ch)

                @block.tensor
                def _(pe):
                    def step(i, o, s, more):
                        pe.wait_ge(picked[s], 64 * i + 64)
                        turn(b_s[s], xs[s]).then_inc(turned, 1)
                        take(pe, scanned)
                        turn(b_r[s], tiles(sums[s][:])).then_inc(back, 1)

                    bodies(pe, (0, 1), step)

        with Phase(nc) as st:
            a0r, xs, x3r, h2l, h2s, zr = [two(sb, st, n, [P, TG, D]) for n in (
                "c_a0r", "c_xs", "c_x3r", "c_h2l", "c_h2s", "c_zr")]
            tmp = sb(st, "c_tmp", [P, TG, D])
            y, outr = [two(sb, st, n, [P, TG, D]) for n in ("c_y", "c_outr")]
            stage_out = two(sb, st, "c_stage_out", [P, TG], I32)
            stt = two(sb, st, "c_stt", [P, TG, 6])
            mv = two(sb, st, "c_mv", [P, TG, 2])
            sd, rr, bb = [two(sb, st, n, [P, TG]) for n in ("c_sd", "c_rr", "c_bb")]
            aff = two(sb, st, "c_aff", [P, TG, 2])
            stage = two(sb, st, "c_stage", [P, TG], I32)
            keep = two(sb, st, "c_keep", [P, 1, GE], BF16)
            dinv_b = two(sb, st, "c_dinv_b", [P, 1, GE])
            sums = two(sb, st, "c_sums", [P, GE])
            uT, xsT = two(sb, st, "c_uT", [P, GE]), two(sb, st, "c_xsT", [P, GE])
            hs, hd = two(sb, st, "c_hs", [P, GE]), two(sb, st, "c_hd", [P, GE])
            b_s, b_d = pb(st, "c_bs"), pb(st, "c_bd")
            b_hs, b_hd = two(pb, st, "c_bhs"), two(pb, st, "c_bhd")
            b_os, b_od = pb(st, "c_bos"), pb(st, "c_bod")
            a0_in, d_in, picked, h2l_st, h2s_st, z_st, sent = [two(sem, st, f"c_{n}") for n in (
                "a0_in", "d_in", "picked", "h2l_st", "h2s_st", "z_st", "sent")]
            var, std, affine, out_ok, y_ok = [sem(st, f"c_{n}") for n in ("var", "std", "affine", "out_ok", "y_ok")]
            (aff_ok, x_ok, staged, a0_free, d_free2, s_turned, s_copied, x3_turned, u_ok, hs_ok, hs_relu, hd_ok,
             hd_relu, os_ok, os_copied, od_ok, h2s_ok, z_ok) = [sem(st, f"c_{n}") for n in (
                "aff_ok", "x_ok", "staged", "a0_free", "d_free", "s_turned", "s_copied", "x3_turned", "u_ok", "hs_ok",
                "hs_relu", "hd_ok", "hd_relu", "os_ok", "os_copied", "od_ok", "h2s_ok", "z_ok")]
            with nc.Block() as block:
                @block.sync
                def _(sp):
                    for s in range(2):
                        for q in (h2l_st, h2s_st, z_st):
                            sp.nop().then_inc(q[s], 16)

                    def load_a0(b, s):
                        sp.dma_start(a0r[s][:], rows_of(src_x1, b, s)).then_inc(a0_in[s], 16)

                    def load_rest(b, s):
                        sp.dma_start(x3r[s][:], rows_of(x3s_rows, b, s)).then_inc(d_in[s], 16)
                        sp.dma_start(keep[s][:], seq_of(seq_rows, b, s, KEEP, KEEP + 1)).then_inc(d_in[s], 16)
                        sp.dma_start(dinv_b[s][:], seq_of(dinv_row, b, s, 0, 1)).then_inc(d_in[s], 16)

                    for s in range(2):
                        load_a0(0, s)
                        load_rest(0, s)

                    def step(i, o, s, more):
                        if more:
                            take(sp, a0_free)
                            load_a0(i + 1, s)
                        take(sp, os_copied)
                        sp.dma_start(rows_of(h2_src, i, s), h2l[s][:]).then_inc(h2l_st[s], 16)
                        take(sp, h2s_ok)
                        sp.dma_start(rows_of(h2s_rows, i, s), h2s[s][:]).then_inc(h2s_st[s], 16)
                        take(sp, z_ok)
                        sp.dma_start(rows_of(z_rows, i, s), zr[s][:]).then_inc(z_st[s], 16)
                        if more:
                            take(sp, d_free2)
                            load_rest(i + 1, s)

                    bodies(sp, (0, 1), step)
                    for s in range(2):
                        for q in (h2l_st, h2s_st, z_st):
                            sp.wait_ge(q[s], 16 * (BODIES + 1))

                @block.gpsimd
                def _(gp):
                    bound = gp.to_reg(EP - 1)
                    bound_out = gp.to_reg(N - 1)

                    def pick(s):
                        take(gp, staged)
                        take(gp, x_ok)
                        picks(gp, bound, x3s_rows, xs, stage, picked, s)

                    for s in range(2):
                        pick(s)

                    def step(i, o, s, more):
                        if more:
                            pick(s)
                        take(gp, out_ok)
                        for j in range(TG):
                            gp.indirect_dma_start(out, bass.IndirectOffsetOnAxis(ap=stage_out[s][:, j:j + 1], axis=0),
                                                  outr[s][:, j, :], None, bounds_check=bound_out, oob_is_err=False)\
                                .then_inc(sent[s], 16)

                    bodies(gp, (0, 1), step)
                    for s in range(2):
                        gp.wait_ge(sent[s], 64 * BODIES)

                @block.scalar
                def _(act):
                    nc.scalar.preload_act_table(ACT.Sqrt)
                    for s in range(2):
                        local_rows(act, 0, s, a0_in, aff_ok, x_ok, xs, a0r, aff)

                    def step(i, o, s, more):
                        take(act, s_turned)
                        nc.scalar.activation(xsT[s][:], b_s[:], ACT.Copy).then_inc(s_copied, 1)
                        for c in range(2):
                            take(act, hs_ok)
                            nc.scalar.activation(hs[c][:], b_hs[c][:], ACT.Relu, bias=b1s[:, c:c + 1])\
                                .then_inc(hs_relu, 1)
                        for c in range(2):
                            take(act, hd_ok)
                            nc.scalar.activation(hd[c][:], b_hd[c][:], ACT.Relu, bias=b1s[:, c:c + 1])\
                                .then_inc(hd_relu, 1)
                        act.wait_ge(h2l_st[s], 16 * i + 16)
                        take(act, y_ok)
                        nc.scalar.activation(h2l[s][:], tiles(b_os[:]), ACT.Copy).then_inc(os_copied, 1)
                        take(act, var)
                        nc.scalar.activation(sd[s][:], mv[s][:, :, 1], ACT.Sqrt, bias=eps_col[:, EPS1:EPS1 + 1])\
                            .then_inc(std, 1)
                        take(act, affine)
                        norm_rows(act, outr, y, rr, bb, s).then_inc(out_ok, 1)
                        if more:
                            local_rows(act, i + 1, s, a0_in, aff_ok, x_ok, xs, a0r, aff)

                    bodies(act, (0, 1), step)

                @block.vector
                def _(dve):
                    ch = Chain(dve, dve_done)
                    V = nc.vector
                    ch.link(V.memset(sums[1][:], 0.0))
                    ch.close()
                    for s in range(2):
                        local_put(V, 1, aff, stage, 0, s, aff_ok, staged)

                    def step(i, o, s, more):
                        dve.wait_ge(d_in[s], 48 * i + 48)
                        take(dve, s_copied)
                        ch.link(V.tensor_tensor(y[s][:], xs[s][:], b2_all[:].unsqueeze(1).to_broadcast([P, TG, D]), ALU.add))
                        if more:
                            local_put(V, 1, aff, stage, i + 1, s, aff_ok, staged)
                            V.nop().then_inc(a0_free, 1)
                        ch.link(V.tensor_tensor_scan(sums[s][:], keep[s][:, 0, :], b_s[:], sums[1 - s][:, GE - 1:GE],
                                                     ALU.mult, ALU.add))
                        take(dve, x3_turned)
                        ch.link(V.tensor_tensor(uT[s][:], sums[s][:], b_d[:], ALU.add))
                        V.tensor_tensor(uT[s][:], uT[s][:], dinv_b[s][:, 0, :], ALU.mult).then_inc(u_ok, 1)
                        ch.link(V.tensor_tensor(tmp[:], x3r[s][:], cols(c_root, i, s), ALU.mult))
                        ch.link(V.tensor_tensor(tmp[:], tmp[:], b2_all[:].unsqueeze(1).to_broadcast([P, TG, D]), ALU.add))
                        V.nop().then_inc(d_free2, 1)
                        take(dve, os_ok)
                        ch.link(V.tensor_tensor(y[s][:], tiles(b_os[:]), y[s][:], ALU.add))
                        V.nop().then_inc(y_ok, 1)
                        norm_stats(V, ch, y, stt, mv, s, var)
                        take(dve, std)
                        ch.link(V.reciprocal(rr[s][:], sd[s][:]))
                        if not isinstance(i, int) or i:
                            dve.wait_ge(sent[s], 64 * i)
                        V.tensor_copy(stage_out[s][:], i_srcout[:, bass.ds(i * (2 * TG) + s * TG, TG)])
                        V.scalar_tensor_tensor(out=bb[s][:], in0=mv[s][:, :, 0], scalar=-1.0, in1=rr[s][:],
                                               op0=ALU.mult, op1=ALU.mult).then_inc(affine, 1)
                        dve.wait_ge(h2s_st[s], 16 * i + 16)
                        take(dve, od_ok)
                        ch.link(V.tensor_tensor(h2s[s][:], tiles(b_od[:]), cols(c_dinv, i, s), ALU.mult))
                        V.nop().then_inc(h2s_ok, 1)
                        dve.wait_ge(z_st[s], 16 * i + 16)
                        ch.link(V.tensor_tensor(zr[s][:], h2s[s][:], cols(c_dinv, i, s), ALU.mult))
                        V.tensor_tensor(zr[s][:], zr[s][:], tmp[:], ALU.add).then_inc(z_ok, 1)

                    for s in range(2):
                        step(0, s, s, True)
                    ch.close()
                    with dve.Fori(1, BODIES - 1) as i:
                        for s in range(2):
                            step(i, s, s, True)
                        ch.close()
                    for s in range(2):
                        step(BODIES - 1, s, s, False)
                    ch.close()

                @block.tensor
                def _(pe):
                    def first(banks, t, ok):
                        for c in range(2):
                            nc.tensor.matmul(banks[c][:], w1s[:, c * D:(c + 1) * D], t[:], start=True, stop=True)\
                                .then_inc(ok, 1)

                    def second(bank, h):
                        for j in range(TG):
                            for c in range(2):
                                last = nc.tensor.matmul(bank[:, j * P:(j + 1) * P], h[c][:, j * P:(j + 1) * P],
                                                        w2s[:, c, :], start=(c == 0), stop=(c == 1))
                        return last

                    def step(i, o, s, more):
                        pe.wait_ge(d_in[s], 48 * i + 48)
                        turn(b_d, x3r[s]).then_inc(x3_turned, 1)
                        pe.wait_ge(picked[s], 64 * i + 64)
                        turn(b_s, xs[s]).then_inc(s_turned, 1)
                        take(pe, u_ok)
                        first(b_hs, xsT[s], hs_ok)
                        first(b_hd, uT[s], hd_ok)
                        take(pe, hs_relu, 2)
                        second(b_os, hs).then_inc(os_ok, 1)
                        take(pe, hd_relu, 2)
                        second(b_od, hd).then_inc(od_ok, 1)

                    bodies(pe, (0, 1), step)

        with Phase(nc) as st:
            xs, zr, y, outr = [two(sb, st, n, [P, TG, D]) for n in ("f_xs", "f_zr", "f_y", "f_outr")]
            stage = two(sb, st, "f_stage", [P, TG], I32)
            stage_out = two(sb, st, "f_stage_out", [P, TG], I32)
            keep = two(sb, st, "f_keep", [P, 1, GE], BF16)
            sums = two(sb, st, "f_sums", [P, GE])
            stt = two(sb, st, "f_stt", [P, TG, 6])
            mv = two(sb, st, "f_mv", [P, TG, 2])
            sd, rr, bb = [two(sb, st, n, [P, TG]) for n in ("f_sd", "f_rr", "f_bb")]
            b_s, b_r = two(pb, st, "f_bs"), two(pb, st, "f_br")
            h2_in, d_in, picked, sent = [two(sem, st, f"f_{n}") for n in ("h2_in", "d_in", "picked", "sent")]
            (staged, xs_free, d_free2, turned, scanned, back, var, std, affine, out_ok) = [
                sem(st, f"f_{n}") for n in ("staged", "xs_free", "d_free", "turned", "scanned", "back", "var", "std",
                                            "affine", "out_ok")]
            with nc.Block() as block:
                @block.sync
                def _(sp):
                    def load_h2(b, s):
                        sp.dma_start(xs[s][:], rows_of(h2_src, b, s)).then_inc(h2_in[s], 16)

                    def load_rest(b, s):
                        sp.dma_start(zr[s][:], rows_of(z_rows, b, s)).then_inc(d_in[s], 16)
                        sp.dma_start(keep[s][:], seq_of(seq_rows, b, s, KEEP, KEEP + 1)).then_inc(d_in[s], 16)

                    for s in range(2):
                        load_h2(0, s)
                        load_rest(0, s)
                    with sp.Fori(0, BODIES - 1) as i:
                        for s in range(2):
                            take(sp, xs_free)
                            load_h2(i + 1, s)
                            take(sp, d_free2)
                            load_rest(i + 1, s)

                @block.gpsimd
                def _(gp):
                    bound = gp.to_reg(EP - 1)
                    bound_out = gp.to_reg(N - 1)

                    def pick(i, s):
                        gp.wait_ge(h2_in[s], 16 * i + 16)
                        take(gp, staged)
                        picks(gp, bound, h2s_rows, xs, stage, picked, s)

                    for s in range(2):
                        pick(0, s)

                    def step(i, o, s, more):
                        take(gp, out_ok)
                        for j in range(TG):
                            gp.indirect_dma_start(out, bass.IndirectOffsetOnAxis(ap=stage_out[s][:, j:j + 1], axis=0),
                                                  outr[s][:, j, :], None, bounds_check=bound_out, oob_is_err=False)\
                                .then_inc(sent[s], 16)
                        if more:
                            pick(i + 1, s)

                    bodies(gp, (0, 1), step)
                    for s in range(2):
                        gp.wait_ge(sent[s], 64 * BODIES)

                @block.scalar
                def _(act):
                    nc.scalar.preload_act_table(ACT.Sqrt)
                    with act.Fori(0, BODIES) as i:
                        for s in range(2):
                            take(act, var)
                            nc.scalar.activation(sd[s][:], mv[s][:, :, 1], ACT.Sqrt, bias=eps_col[:, EPS1:EPS1 + 1])\
                                .then_inc(std, 1)
                            take(act, affine)
                            norm_rows(act, outr, y, rr, bb, s).then_inc(out_ok, 1)

                @block.vector
                def _(dve):
                    ch = Chain(dve, dve_done)
                    V = nc.vector
                    ch.link(V.memset(sums[1][:], 0.0))
                    ch.close()
                    for s in range(2):
                        local_put(V, None, None, stage, 0, s, None, staged)

                    def step(i, o, s, more):
                        dve.wait_ge(d_in[s], 32 * i + 32)
                        take(dve, turned)
                        if more:
                            local_put(V, None, None, stage, i + 1, s, None, staged)
                            V.nop().then_inc(xs_free, 1)
                        ch.link(V.tensor_tensor_scan(sums[s][:], keep[s][:, 0, :], b_s[s][:], sums[1 - s][:, GE - 1:GE],
                                                     ALU.mult, ALU.add))
                        V.nop().then_inc(scanned, 1)
                        take(dve, back)
                        ch.link(V.tensor_tensor(y[s][:], tiles(b_r[s][:]), cols(c_dinv, i, s), ALU.mult))
                        ch.link(V.tensor_tensor(y[s][:], y[s][:], zr[s][:], ALU.add))
                        V.nop().then_inc(d_free2, 1)
                        norm_stats(V, ch, y, stt, mv, s, var)
                        take(dve, std)
                        ch.link(V.reciprocal(rr[s][:], sd[s][:]))
                        if not isinstance(i, int) or i:
                            dve.wait_ge(sent[s], 64 * i)
                        V.tensor_copy(stage_out[s][:], i_out[:, bass.ds(i * (2 * TG) + s * TG, TG)])
                        V.scalar_tensor_tensor(out=bb[s][:], in0=mv[s][:, :, 0], scalar=-1.0, in1=rr[s][:],
                                               op0=ALU.mult, op1=ALU.mult).then_inc(affine, 1)

                    for s in range(2):
                        step(0, s, s, True)
                    ch.close()
                    with dve.Fori(1, BODIES - 1) as i:
                        for s in range(2):
                            step(i, s, s, True)
                        ch.close()
                    for s in range(2):
                        step(BODIES - 1, s, s, False)
                    ch.close()

                @block.tensor
                def _(pe):
                    def step(i, o, s, more):
                        pe.wait_ge(picked[s], 64 * i + 64)
                        turn(b_s[s], xs[s]).then_inc(turned, 1)
                        take(pe, scanned)
                        turn(b_r[s], tiles(sums[s][:])).then_inc(back, 1)

                    bodies(pe, (0, 1), step)


_INS = ["x", "src", "dst", "edge_type_4", "edge_weight", "node_type_3", "L1_gnn_W_kqv", "L1_gnn_W_a",
        "L1_gnn_rel_pri", "L1_gnn_rel_att", "L3_gnn_W1", "L3_gnn_b1", "L3_gnn_W2", "L3_gnn_b2"]


def kernel(**inputs):
    import numpy as _np
    import concourse.bacc as _bacc
    from concourse.bass_utils import run_bass_kernel_spmd as _run

    nc = _bacc.Bacc("TRN2", target_bir_lowering=False, num_devices=1)
    arrays, args = {}, []
    for name in _INS:
        a = _np.ascontiguousarray(inputs[name])
        arrays[f"in_{name}"] = a
        args.append(nc.dram_tensor(f"in_{name}", a.shape, mybir.dt.from_np(a.dtype), kind="ExternalInput").ap())
    x = inputs["x"]
    args.append(nc.dram_tensor("out_0", x.shape, F32, kind="ExternalOutput").ap())
    gnn_kernel(nc, *args)
    r = _run(nc, [arrays], core_ids=[0])
    return r.results[0]["out_0"]
```

```python
import concourse.bass as bass
from concourse import mybir
from contextlib import ExitStack

ALU = mybir.AluOpType
ACT = mybir.ActivationFunctionType
F32 = mybir.dt.float32
BF16 = mybir.dt.bfloat16
I32 = mybir.dt.int32

P = 128
D = 128
TG = 4
GE = TG * P
BODY = 2 * GE
HEADS, HD = 4, 32
EPS = 1e-5
BIG = 1e30
FAR = 1 << 20


class Phase(ExitStack):

    def __init__(self, nc):
        super().__init__()
        self.nc, self.sems = nc, []

    def __exit__(self, *problem):
        if self.sems and problem[0] is None:
            self.nc.clear_and_free_semaphores(self.sems)
            self.nc.all_engine_barrier()
        return super().__exit__(*problem)


class Chain:

    def __init__(self, eng, sem):
        self.eng, self.sem, self.n = eng, sem, 0

    def link(self, ins):
        self.n += 1
        ins.then_inc(self.sem, 1)
        self.eng.wait_ge(self.sem, self.n)

    def close(self):
        if self.n:
            self.eng.sem_inc(self.sem, -self.n)
        self.n = 0


def take(eng, sem, n=1):
    eng.wait_ge(sem, n)
    eng.sem_inc(sem, -n)


def gnn_kernel(nc, x, src, dst, etype, weight, ntype, w_kqv, w_a, rel_pri, rel_att, w1, b1, w2, b2, out):
    N = x.shape[0]
    E = src.shape[0]
    NTYPES, ETYPES = w_kqv.shape[0], rel_att.shape[1]
    BODIES = -(-E // BODY)
    EP = BODIES * BODY
    NT = EP // P
    HALF = NT // 2
    NONE = EP
    assert D == P and NT % 2 == 0 and HALF <= P and NTYPES == 3 and ETYPES == 4
    NGROUPS = -(-N // GE)
    NODE_P = 125
    assert N % NODE_P == 0

    main = ExitStack()
    with main:
        def sb(stack, name, shape, dt=F32):
            return stack.enter_context(nc.sbuf_tensor(name, shape, dt))

        def pb(stack, name, shape=(P, GE), dt=F32):
            return stack.enter_context(nc.psum_tensor(name, list(shape), dt))

        def sem(stack, name):
            handle = nc.alloc_semaphore(name=name)
            if stack is not main:
                stack.sems.append(handle)
            return handle

        def two(make, stack, name, *a):
            return [make(stack, f"{name}{s}", *a) for s in range(2)]

        def dram(name, shape, dt=F32):
            return nc.dram_tensor(name, shape, dt, kind="Internal").ap()

        node_table = dram("node_table", (N, 4), I32)
        rec_low = dram("rec_low", (EP, 4), I32)
        rec_src = dram("rec_src", (EP + 2, 4), I32)
        keep_src = dram("keep_src", (1, EP), BF16)
        edge_dst = dram("edge_dst", (EP + 2,), I32)
        seq_rows = dram("seq_rows", (7, EP), BF16)
        onehot_rows = dram("onehot_rows", (ETYPES, EP))
        dinv_row = dram("dinv_row", (1, EP))
        src_x1 = dram("src_x1", (EP, D))
        x1_nodes = dram("x1_nodes", (EP, D))
        e1_rows = dram("e1_rows", (EP + 1, D))
        e2_rows = dram("e2_rows", (EP + 1, D))
        x1_rows = dram("x1_rows", (EP, D))
        x2_rows = dram("x2_rows", (EP, D))
        x3s_rows = dram("x3s_rows", (EP, D))
        lrm = dram("lrm", (EP // GE, P, 3, GE))
        h2_src = dram("h2_src", (EP, D))
        h2s_rows = dram("h2s_rows", (EP, D))
        z_rows = dram("z_rows", (EP, D))
        KEEP, NFIRST, NOTLAST, NLAST, ET, NTS, NTD = range(7)

        def rows_of(table, i, s):
            v = table[0:EP, :].rearrange("(b s j p) f -> b s p j f", s=2, j=TG, p=P)
            return v[bass.ds(i, 1), s].rearrange("o p j f -> (o p) j f")

        def seq_of(table, i, s, a, b):
            return table[a:b, bass.ds(i * BODY + s * GE, GE)].partition_broadcast(P)

        def lrm_of(i, s, a, b):
            v = lrm.rearrange("(b s) p k e -> b s p k e", s=2)
            return v[bass.ds(i, 1), s, :, a:b].rearrange("o p k e -> (o p) k e")

        ident = sb(main, "ident", [P, P])
        head_ones = sb(main, "head_ones", [P, P])
        wk = sb(main, "wk", [P, NTYPES, D])
        wa = sb(main, "wa", [P, NTYPES, D])
        ra = sb(main, "ra", [P, ETYPES, D])
        pri = sb(main, "pri", [ETYPES, D])
        w1s = sb(main, "w1s", [P, 2 * D])
        w2s = sb(main, "w2s", [P, 2, D])
        b1s = sb(main, "b1s", [P, 2])
        b2_all = sb(main, "b2_all", [P, D])
        b2_parts = sb(main, "b2_parts", [3, GE], BF16)
        ones3 = sb(main, "ones3", [3, P], BF16)
        eps_col = sb(main, "eps_col", [P, 7])
        EPS1, EPS16, EPS_SQ, EPS_CB, EPS_1, EPS_M, ONE = range(7)
        i_src = sb(main, "i_src", [P, NT + 2 * TG], I32)
        i_dst = sb(main, "i_dst", [P, NT + 2 * TG], I32)
        i_out = sb(main, "i_out", [P, NT + 2 * TG], I32)
        i_pick = sb(main, "i_pick", [P, NT + 2 * TG], I32)
        i_node1 = sb(main, "i_node1", [P, NT + 2 * TG], I32)
        i_dst1 = sb(main, "i_dst1", [P, NT + 2 * TG], I32)
        i_srcout = sb(main, "i_srcout", [P, NT + 2 * TG], I32)
        entry_dst = sb(main, "entry_dst", [P, NT + 2 * TG, 1], I32)
        k_src = sb(main, "k_src", [P, NT + 2 * TG], I32)
        k_out = sb(main, "k_out", [P, NT + 2 * TG], I32)
        k_dst = sb(main, "k_dst", [P, NT + 2 * TG], I32)
        k_pick = sb(main, "k_pick", [P, NT + 2 * TG], I32)
        k_w = sb(main, "k_w", [P, NT])
        entry_src = sb(main, "entry_src", [P, NT + 2 * TG, 2], I32)
        c_last = sb(main, "c_last", [P, NT])
        c_third = sb(main, "c_third", [P, NT])
        c_dinv = sb(main, "c_dinv", [P, NT])
        c_root = sb(main, "c_root", [P, NT])
        c_nts = sb(main, "c_nts", [P, NT])
        c_ntd = sb(main, "c_ntd", [P, NT])
        src_stats = sb(main, "src_stats", [P, NT, 6])
        local = [sb(main, f"local{n}", [P, NT, 2]) for n in range(2)]

        dx = two(sb, main, "dx", [P, TG, D])
        dn = two(sb, main, "dn", [P, TG, D])
        dxT = two(sb, main, "dxT", [P, GE])
        dh = two(sb, main, "dh", [P, 2, GE])
        dy = two(sb, main, "dy", [P, TG, D])
        dst1 = two(sb, main, "dst1", [P, TG, 6])
        dst2 = two(sb, main, "dst2", [P, TG, 6])
        dmv1 = two(sb, main, "dmv1", [P, TG, 2])
        dmv2 = two(sb, main, "dmv2", [P, TG, 2])
        dsd1 = two(sb, main, "dsd1", [P, TG])
        dsd2 = two(sb, main, "dsd2", [P, TG])
        dr1 = two(sb, main, "dr1", [P, TG])
        dr2 = two(sb, main, "dr2", [P, TG])
        db1 = two(sb, main, "db1", [P, TG])
        db2 = two(sb, main, "db2", [P, TG])
        d_loaded = two(sem, main, "d_loaded")
        d_stored = two(sem, main, "d_stored")
        (d_var1, d_std1, d_affine1, d_normed, d_free, d_turned, d_copied, d_hidden, d_relu, d_summed, d_taken,
         d_var2, d_std2, d_out) = [sem(main, f"d_{n}") for n in (
            "var1", "std1", "affine1", "normed", "free", "turned", "copied", "hidden", "relu", "summed",
            "taken", "var2", "std2", "out")]
        dve_done = sem(main, "dve_done")
        act_done = sem(main, "act_done")

        def node_rows(table, k):
            start = min(k * GE, N - GE) if isinstance(k, int) else k * GE
            v = table[bass.ds(start, GE), :] if not isinstance(start, int) else table[start:start + GE, :]
            return v.rearrange("(p j) f -> p j f", j=TG)

        def d_load(sp, k, s):
            take(sp, d_free)
            sp.dma_start(dx[s][:], node_rows(x, k)).then_inc(d_loaded[s], 16)

        def d_store(sp, k, s):
            take(sp, d_out)
            sp.dma_start(node_rows(out, k), dy[s][:]).then_inc(d_stored[s], 16)

        def d_stats1(dve, ch, s, n):
            dve.wait_ge(d_loaded[s], 16 * n + 16)
            for j in range(TG):
                last = nc.vector.bn_stats(dst1[s][:, j, :], dx[s][:, j, :])
            ch.link(last)
            for j in range(TG):
                last = nc.vector.bn_aggr(dmv1[s][:, j, :], dst1[s][:, j, :])
            last.then_inc(d_var1, 1)

        def d_affine(dve, ch, s, std, mv, r, b, sd, done):
            take(dve, std)
            ch.link(nc.vector.reciprocal(r[s][:], sd[s][:]))
            ins = nc.vector.scalar_tensor_tensor(out=b[s][:], in0=mv[s][:, :, 0], scalar=-1.0, in1=r[s][:],
                                                 op0=ALU.mult, op1=ALU.mult)
            if done is None:
                ch.link(ins)
            else:
                ins.then_inc(done, 1)

        def d_residual(dve, ch, s, n):
            take(dve, d_summed)
            dve.wait_ge(d_stored[s], 16 * n + 16)
            ch.link(nc.vector.tensor_tensor(dy[s][:], ps_do[:].rearrange("p (j f) -> p j f", j=TG), dn[s][:],
                                            ALU.add))
            nc.vector.nop().then_inc(d_taken, 1)
            for j in range(TG):
                last = nc.vector.bn_stats(dst2[s][:, j, :], dy[s][:, j, :])
            ch.link(last)
            for j in range(TG):
                last = nc.vector.bn_aggr(dmv2[s][:, j, :], dst2[s][:, j, :])
            last.then_inc(d_var2, 1)

        def d_affine1_of(dve, ch, s):
            d_affine(dve, ch, s, d_std1, dmv1, dr1, db1, dsd1, d_affine1)

        def dense_dve_a(dve, ch, s, n, more=2):
            if more > 1:
                d_stats1(dve, ch, s, n + 1)
            d_residual(dve, ch, s, n)

        def dense_dve_b(dve, ch, s, more=2):
            if more > 1:
                d_affine1_of(dve, ch, s)
            d_final(dve, ch, s)

        def d_final(dve, ch, s):
            d_affine(dve, ch, s, d_std2, dmv2, dr2, db2, dsd2, None)
            for j in range(TG):
                last = nc.vector.tensor_scalar(dy[s][:, j, :], dy[s][:, j, :], dr2[s][:, j:j + 1],
                                               db2[s][:, j:j + 1], ALU.mult, ALU.add)
            last.then_inc(d_out, 1)

        def d_root1(act, s):
            take(act, d_var1)
            nc.scalar.activation(dsd1[s][:], dmv1[s][:, :, 1], ACT.Sqrt, bias=eps_col[:, EPS_CB:EPS_CB + 1],
                                 scale=C3).then_inc(d_std1, 1)

        def d_root2(act, s):
            take(act, d_var2)
            nc.scalar.activation(dsd2[s][:], dmv2[s][:, :, 1], ACT.Sqrt, bias=eps_col[:, EPS1:EPS1 + 1])\
                .then_inc(d_std2, 1)

        def d_norm1(act, s):
            take(act, d_affine1)
            for j in range(TG):
                last = nc.scalar.activation(dn[s][:, j, :], dx[s][:, j, :], ACT.Identity, bias=db1[s][:, j:j + 1],
                                            scale=dr1[s][:, j:j + 1])
            last.then_inc(d_normed, 1)

        def d_copy(act, s):
            take(act, d_turned)
            nc.scalar.activation(dxT[s][:], ps_dt[:], ACT.Copy).then_inc(d_copied, 1)

        def d_hid(act, s):
            for c in range(2):
                take(act, d_hidden)
                nc.scalar.activation(dh[s][:, c, :], ps_dh[c][:], ACT.Relu, bias=b1s[:, c:c + 1])\
                    .then_inc(d_relu, 1)

        def d_turn(pe, s):
            take(pe, d_normed)
            nc.tensor.nop().then_inc(d_free, 1)
            for j in range(TG):
                last = nc.tensor.transpose(ps_dt[:, j * P:(j + 1) * P], dn[s][:, j, :], ident[:])
            last.then_inc(d_turned, 1)

        def d_first(pe, s):
            take(pe, d_copied)
            for c in range(2):
                nc.tensor.matmul(ps_dh[c][:], w1s[:, c * D:(c + 1) * D], dxT[s][:], start=True, stop=True)\
                    .then_inc(d_hidden, 1)

        def d_second(pe, s):
            take(pe, d_relu, 2)
            take(pe, d_taken)
            nc.tensor.matmul(ps_do[:], ones3[:], b2_parts[:], start=True, stop=False, skip_group_check=True)
            for j in range(TG):
                for c in range(2):
                    last = nc.tensor.matmul(ps_do[:, j * P:(j + 1) * P], dh[s][:, c, j * P:(j + 1) * P],
                                            w2s[:, c, :], start=False, stop=(j == TG - 1 and c == 1),
                                            skip_group_check=True)
            last.then_inc(d_summed, 1)

        E1 = EPS / 1.5625
        CS = 1 + EPS / 2.25
        ES = EPS * EPS / 2.25
        C3 = (2.25 * 1.5625 + EPS * 1.5625 * (1 + EPS)) / (2.25 * 1.5625)
        E3 = EPS ** 3 / (2.25 * 1.5625)

        with Phase(nc) as st:
            raw = sb(st, "raw_edges", [HALF, 4, 2, P], I32)
            raw_et = sb(st, "raw_et", [HALF, 2, P], I32)
            pads = sb(st, "pads", [1, EP + 2 - E], I32)
            tab = sb(st, "tab", [NODE_P, N // NODE_P, 4], I32)
            tab_nt = sb(st, "tab_nt", [NODE_P, N // NODE_P], I32)
            fA = sb(st, "fA", [HALF, 4, 2, P])
            etA = sb(st, "etA", [HALF, 2, P])
            pos_i = sb(st, "pos_i", [HALF, 2, P], I32)
            pos = sb(st, "pos", [HALF, 2, P])
            first = sb(st, "first", [HALF, 2, P])
            last_ = sb(st, "last_", [HALF, 2, P])
            t1 = sb(st, "t1", [HALF, 2, P])
            t2 = sb(st, "t2", [HALF, 2, P])
            t3 = sb(st, "t3", [HALF, 2, P])
            cnt = sb(st, "cnt", [HALF, 2, P])
            rootA = sb(st, "rootA", [HALF, 2, P])
            dinvA = sb(st, "dinvA", [HALF, 2, P])
            thirdA = sb(st, "thirdA", [HALF, 2, P])
            dclA = sb(st, "dclA", [HALF, 2, P])
            outA = sb(st, "outA", [HALF, 2, P])
            starts = sb(st, "starts", [HALF, 2, P])
            bfA = sb(st, "bfA", [HALF, 5, 2, P], BF16)
            ohA = sb(st, "ohA", [HALF, ETYPES, 2, P])
            zero_keep = sb(st, "zero_keep", [P, NT])
            run_rows = sb(st, "run_rows", [1, NT + 1])
            carry = sb(st, "carry", [HALF, 2])
            one = sb(st, "one", [1, 1])
            b2r = sb(st, "b2r", [1, 3, D])
            pri_h = sb(st, "pri_h", [HEADS, ETYPES])
            spread = sb(st, "spread", [HEADS, D])
            b1r = sb(st, "b1r", [2, P])
            b2h = sb(st, "b2h", [1, 3, D], BF16)
            zrow = sb(st, "zrow", [1, D])
            ps = [pb(st, f"pp{n}") for n in range(8)]
            p_pad, p_dst, p_w, p_ld, p_tab, p_b2, p_z, p_st, p_b2c = [sem(st, f"p_{n}") for n in (
                "pad", "dst", "w", "ld", "tab", "b2", "z", "st", "b2c")]
            p_mem, p_own, p_ident, p_tot, p_scan, p_carry, p_root, p_rooted, p_field, p_turn, p_seq, p_bseq, p_tabd, p_raw, p_pri = [
                sem(st, f"p_{n}") for n in ("mem", "own", "ident", "tot", "scan", "carry", "root", "rooted",
                                            "field", "turn", "seq", "bseq", "tabd", "raw", "pri")]
            FULL = E // P - HALF
            REST = E - (HALF + FULL) * P

            def halves(view_out, flat, n):
                whole = n // P - HALF
                rest = n - (HALF + whole) * P
                got = [(view_out[:, 0, :], flat[0:HALF * P].rearrange("(t c) -> t c", c=P)),
                       (view_out[0:whole, 1, :], flat[HALF * P:(HALF + whole) * P].rearrange("(t c) -> t c", c=P))]
                if rest:
                    got.append((view_out[whole:whole + 1, 1, 0:rest],
                                flat[(HALF + whole) * P:n].rearrange("(a c) -> a c", a=1)))
                return got

            with nc.Block() as block:
                @block.sync
                def _(sp):
                    take(sp, p_pad)
                    sp.dma_start(edge_dst[1:E + 1], dst).then_inc(p_dst, 16)
                    sp.dma_start(edge_dst[E + 1:EP + 2].rearrange("(a c) -> a c", a=1), pads[0:1, 1:]).then_inc(p_dst, 16)
                    sp.dma_start(edge_dst[0:1].rearrange("(a c) -> a c", a=1), pads[0:1, 0:1]).then_inc(p_dst, 16)
                    take(sp, p_raw)
                    for t in range(NTYPES):
                        sp.dma_start(wk[:, t, :], w_kqv[t]).then_inc(p_w, 16)
                        sp.dma_start(wa[:, t, :], w_a[t]).then_inc(p_w, 16)
                    for h in range(HEADS):
                        sp.dma_start(ra[h * HD:(h + 1) * HD, :, h * HD:(h + 1) * HD],
                                     rel_att[h].rearrange("t d f -> d t f")).then_inc(p_w, 16)
                    sp.dma_start(pri_h[:], rel_pri).then_inc(p_w, 16)
                    sp.dma_start(w1s[:], w1).then_inc(p_w, 16)
                    sp.dma_start(w2s[:], w2.rearrange("(c p) f -> p c f", p=P)).then_inc(p_w, 16)
                    sp.dma_start(b1r[:], b1.rearrange("(c p) -> c p", p=P)).then_inc(p_w, 16)
                    sp.dma_start(b2_all[:], b2.rearrange("(a f) -> a f", a=1).to_broadcast([P, D])).then_inc(p_w, 16)
                    sp.dma_start(b2r[:, 0, :], b2.rearrange("(a f) -> a f", a=1)).then_inc(p_b2, 16)
                    sp.dma_start(tab_nt[:], ntype.rearrange("(p c) -> p c", p=NODE_P)).then_inc(p_tab, 16)
                    for o, f in halves(raw[:, 0], src, E) + halves(raw_et[:], etype, E):
                        sp.dma_start(o, f).then_inc(p_ld, 16)
                    sp.wait_ge(p_dst, 48)
                    for k, off in ((1, 1), (2, 2), (3, 0)):
                        for h in range(2):
                            sp.dma_start(raw[:, k, h, :], edge_dst[off + h * HALF * P:off + (h + 1) * HALF * P]
                                         .rearrange("(t c) -> t c", c=P)).then_inc(p_ld, 16)
                    sp.dma_start(e1_rows[EP:EP + 1, :], zrow[:]).then_inc(p_z, 16)
                    sp.dma_start(e2_rows[EP:EP + 1, :], zrow[:]).then_inc(p_z, 16)
                    take(sp, p_tabd)
                    sp.dma_start(node_table.rearrange("(p c) k -> p c k", p=NODE_P), tab[:]).then_inc(p_st, 16)
                    take(sp, p_b2c)
                    for k in range(3):
                        for j in range(TG):
                            sp.dma_start(b2_parts[k:k + 1, j * D:(j + 1) * D], b2h[0:1, k, :]).then_inc(p_st, 16)
                    take(sp, p_seq)
                    for k in range(5):
                        sp.dma_start(seq_rows[k].rearrange("(h t c) -> t h c", h=2, c=P), bfA[:, k]).then_inc(p_st, 16)
                    for k in range(ETYPES):
                        sp.dma_start(onehot_rows[k].rearrange("(h t c) -> t h c", h=2, c=P), ohA[:, k])\
                            .then_inc(p_st, 16)
                    sp.dma_start(dinv_row[0].rearrange("(h t c) -> t h c", h=2, c=P), dinvA[:]).then_inc(p_st, 16)
                    sp.wait_ge(p_z, 32)
                    sp.wait_ge(p_st, 16 * (1 + 3 * TG + 5 + ETYPES + 1))

                @block.gpsimd
                def _(gp):
                    nc.gpsimd.memset(pads[:], 2 * FAR)
                    nc.gpsimd.memset(zrow[:], 0.0)
                    nc.gpsimd.memset(ident[:], 0.0).then_inc(p_own, 1)
                    gp.wait_ge(p_own, 1)
                    nc.gpsimd.memset(pads[0:1, 0:1], -1).then_inc(p_pad, 1)
                    nc.gpsimd.memset(raw_et[:], 0)
                    nc.gpsimd.memset(raw[:, 0], 0)
                    nc.gpsimd.memset(ra[:], 0.0).then_inc(p_raw, 1)
                    nc.gpsimd.affine_select(out=ident[:], in_=ident[:], compare_op=ALU.not_equal, fill=1.0,
                                            base=0, pattern=[[-1, P]], channel_multiplier=1).then_inc(p_ident, 1)
                    nc.gpsimd.memset(tab[:], 0)
                    nc.gpsimd.iota(pos_i[:], pattern=[[HALF * P, 2], [1, P]], base=1, channel_multiplier=P)
                    nc.gpsimd.memset(entry_dst[:], 0)
                    nc.gpsimd.memset(entry_src[:], 0)
                    nc.gpsimd.memset(head_ones[:], 0.0).then_inc(p_mem, 1)
                    gp.wait_ge(p_mem, 1)
                    nc.gpsimd.iota(entry_dst[:, 0:NT, 0], pattern=[[P, NT]], base=1, channel_multiplier=1)
                    for t in (i_src, i_dst, i_out, i_pick, i_node1, i_dst1, i_srcout, k_src, k_out, k_dst, k_pick):
                        nc.gpsimd.memset(t[:, NT:NT + 2 * TG], 0)
                    nc.gpsimd.memset(one[:], 1.0)
                    nc.gpsimd.memset(run_rows[:], 0.0)
                    nc.gpsimd.memset(zero_keep[:], 0.0)
                    nc.gpsimd.memset(ones3[:], 1.0)
                    for k, v in ((EPS1, EPS), (EPS16, 16 * EPS), (EPS_SQ, ES), (EPS_CB, E3), (EPS_1, E1), (EPS_M, EPS / 2.25),
                                 (ONE, 1.0)):
                        last = nc.gpsimd.memset(eps_col[:, k:k + 1], v)
                    last.then_inc(p_mem, 1)
                    for h in range(HEADS):
                        gp.wait_ge(p_mem, 2 + h)
                        nc.gpsimd.memset(head_ones[h * HD:(h + 1) * HD, h * HD:(h + 1) * HD], 1.0).then_inc(p_mem, 1)
                    gp.wait_ge(p_mem, 2 + HEADS)
                    nc.gpsimd.memset(spread[:], 1.0).then_inc(p_mem, 1)
                    gp.wait_ge(p_mem, 3 + HEADS)
                    nc.gpsimd.affine_select(out=spread[:], in_=spread[:], compare_op=ALU.is_ge, fill=0.0,
                                            base=0, pattern=[[1, D]], channel_multiplier=-HD).then_inc(p_mem, 1)
                    gp.wait_ge(p_mem, 4 + HEADS)
                    nc.gpsimd.affine_select(out=spread[:], in_=spread[:], compare_op=ALU.is_ge, fill=0.0,
                                            base=HD - 1, pattern=[[-1, D]], channel_multiplier=HD).then_inc(p_mem, 1)

                @block.vector
                def _(dve):
                    ch = Chain(dve, dve_done)
                    V = nc.vector
                    dve.wait_ge(p_w, 16 * (2 * NTYPES + HEADS + 5))
                    for t in range(1, NTYPES):
                        V.tensor_tensor(wk[:, t, :], wk[:, t, :], wk[:, 0, :], ALU.subtract)
                        V.tensor_tensor(wa[:, t, :], wa[:, t, :], wa[:, 0, :], ALU.subtract)
                    for t in range(1, ETYPES):
                        V.tensor_tensor(ra[:, t, :], ra[:, t, :], ra[:, 0, :], ALU.subtract)
                    dve.wait_ge(p_b2, 16)
                    for k in range(3):
                        ch.link(V.tensor_copy(b2h[:, k, :], b2r[:, k, :]))
                        if k < 2:
                            ch.link(V.tensor_tensor(b2r[:, k + 1, :], b2r[:, k, :], b2h[:, k, :], ALU.subtract))
                    V.nop().then_inc(p_b2c, 1)
                    dve.wait_ge(p_mem, 2 + HEADS)
                    dve.wait_ge(p_tab, 16)
                    V.tensor_copy(tab[:, :, 1], tab_nt[:]).then_inc(p_tabd, 1)
                    dve.wait_ge(p_ld, 16 * 12)
                    V.tensor_copy(fA[:], raw[:])
                    V.tensor_copy(pos[:], pos_i[:])
                    ch.link(V.tensor_copy(etA[:], raw_et[:]))
                    SRC, DST, NEXT, PREV = range(4)
                    V.tensor_tensor(first[:], fA[:, DST], fA[:, PREV], ALU.not_equal)
                    V.tensor_tensor(t1[:], fA[:, DST], fA[:, NEXT], ALU.not_equal)
                    V.tensor_scalar(t2[:], fA[:, DST], float(N), None, ALU.is_lt)
                    V.tensor_scalar(dclA[:], fA[:, DST], float(N - 1), None, ALU.min)
                    ch.link(V.tensor_scalar(outA[:], fA[:, DST], float(FAR), None, ALU.add))
                    ch.link(V.tensor_tensor(last_[:], t1[:], t2[:], ALU.mult))
                    V.scalar_tensor_tensor(out=t3[:], in0=last_[:], scalar=-float(FAR), in1=outA[:], op0=ALU.mult,
                                           op1=ALU.add)
                    ch.link(V.tensor_tensor(t1[:], pos[:], first[:], ALU.mult))
                    for h in range(2):
                        last = V.tensor_tensor_scan(starts[:, h, :], zero_keep[0:HALF, 0:P], t1[:, h, :], 0.0,
                                                    ALU.add, ALU.max)
                    last.then_inc(p_tot, 1)
                    take(dve, p_scan)
                    V.tensor_tensor_scan(run_rows[:, 1:NT + 1], zero_keep[0:1, :], ps[0][0:1, 0:NT], 0.0,
                                         ALU.add, ALU.max).then_inc(p_carry, 1)
                    take(dve, p_scan)
                    ch.link(V.tensor_copy(carry[:], ps[1][0:HALF, 0:2]))
                    for h in range(2):
                        last = V.tensor_scalar(starts[:, h, :], starts[:, h, :], carry[:, h:h + 1], None, ALU.max)
                    ch.link(last)
                    ch.link(V.tensor_tensor(t2[:], pos[:], starts[:], ALU.subtract))
                    V.tensor_scalar(t1[:], t2[:], 3.0, 3.0, ALU.mult, ALU.add)
                    ch.link(V.tensor_scalar(cnt[:], t2[:], 1.0, None, ALU.add))
                    V.nop().then_inc(p_root, 1)
                    V.reciprocal(thirdA[:], t1[:])
                    V.tensor_scalar(bfA[:, KEEP], first[:], -1.0, 1.0, ALU.mult, ALU.add)
                    V.tensor_scalar(bfA[:, NFIRST], first[:], -BIG, None, ALU.mult)
                    V.tensor_scalar(bfA[:, NOTLAST], last_[:], -1.0, 1.0, ALU.mult, ALU.add)
                    V.tensor_scalar(bfA[:, NLAST], last_[:], -BIG, None, ALU.mult)
                    V.tensor_copy(bfA[:, ET], etA[:])
                    for t in range(ETYPES):
                        V.tensor_scalar(ohA[:, t], etA[:], float(t), None, ALU.is_equal)
                    take(dve, p_rooted)
                    ch.link(V.reciprocal(dinvA[:], rootA[:]))
                    V.nop().then_inc(p_seq, 1)
                    V.nop().then_inc(p_field, 1)
                    outs = (i_src, i_dst, i_out, c_last, c_third, c_dinv, c_root)
                    take(dve, p_turn)
                    for n, o in enumerate(outs):
                        V.tensor_copy(o[:, 0:NT], ps[n][:, 0:NT])
                    V.tensor_scalar(pri[:], ps[7][0:ETYPES, 0:D], HD ** -0.5, None, ALU.mult)
                    V.tensor_copy(b1s[:], ps[7][:, D:D + 2])
                    ch.close()

                @block.scalar
                def _(act):
                    nc.scalar.preload_act_table(ACT.Sqrt)
                    take(act, p_root)
                    nc.scalar.activation(rootA[:], cnt[:], ACT.Sqrt, bias=eps_col[0:HALF, ONE:ONE + 1])\
                        .then_inc(p_rooted, 1)

                @block.tensor
                def _(pe):
                    pe.wait_ge(p_ident, 1)
                    take(pe, p_tot)
                    for h in range(2):
                        last = nc.tensor.matmul(ps[0][0:1, h * HALF:(h + 1) * HALF], starts[:, h, P - 1:P],
                                                ident[0:HALF, 0:HALF], start=True, stop=True)
                    last.then_inc(p_scan, 1)
                    take(pe, p_carry)
                    for h in range(2):
                        last = nc.tensor.matmul(ps[1][0:HALF, h:h + 1], run_rows[0:1, h * HALF:(h + 1) * HALF],
                                                one[:], start=True, stop=True)
                    last.then_inc(p_scan, 1)
                    take(pe, p_field)
                    for n, f in enumerate((fA[:, 0], dclA, t3, last_, thirdA, dinvA, rootA)):
                        for h in range(2):
                            last = nc.tensor.transpose(ps[n][:, h * HALF:(h + 1) * HALF], f[:, h, :],
                                                       ident[0:HALF, 0:HALF])
                    pe.wait_ge(p_w, 16 * (2 * NTYPES + HEADS + 5))
                    pe.wait_ge(p_mem, 5 + HEADS)
                    nc.tensor.matmul(ps[7][0:ETYPES, 0:D], pri_h[:], spread[:], start=True, stop=True)
                    last = nc.tensor.transpose(ps[7][:, D:D + 2], b1r[:], ident[0:2, 0:2])
                    last.then_inc(p_turn, 1)

        dense_psum = ExitStack()
        main.push(dense_psum)
        ps_dt = pb(dense_psum, "ps_dt")
        ps_dh = two(pb, dense_psum, "ps_dh")
        ps_do = pb(dense_psum, "ps_do")

        def table_phase(tag, k0, jobs):
            with Phase(nc) as st:
                stage = [two(sb, st, f"{tag}_stage{n}", [P, TG], I32) for n in range(len(jobs))]
                moved = [two(sb, st, f"{tag}_moved{n}", [P, TG, job[4]], I32) for n, job in enumerate(jobs)]
                staged = sem(st, f"{tag}_staged")
                done = two(sem, st, f"{tag}_done")
                per = 64 * len(jobs)
                with nc.Block() as block:
                    @block.gpsimd
                    def _(gp):
                        bounds = [gp.to_reg(job[0].shape[0] - 1) for job in jobs]
                        with gp.Fori(0, BODIES) as i:
                            for s in range(2):
                                take(gp, staged)
                                for n, (table, _, _, _, _, rows, _) in enumerate(jobs):
                                    for j in range(TG):
                                        at = bass.IndirectOffsetOnAxis(ap=stage[n][s][:, j:j + 1], axis=0)
                                        if rows is None:
                                            gp.indirect_dma_start(moved[n][s][:, j, :], None, table, at,
                                                                  bounds_check=bounds[n], oob_is_err=False)\
                                                .then_inc(done[s], 16)
                                        else:
                                            gp.indirect_dma_start(table, at, moved[n][s][:, j, :], None,
                                                                  bounds_check=bounds[n], oob_is_err=False)\
                                                .then_inc(done[s], 16)

                    @block.vector
                    def _(dve):
                        ch = Chain(dve, dve_done)
                        V = nc.vector

                        def put(s, tile):
                            reg = not isinstance(tile, int)
                            for n, (_, index, times, plus, _, rows, _) in enumerate(jobs):
                                if rows is not None:
                                    V.tensor_copy(moved[n][s][:], sl(rows, tile, reg))
                                last = V.tensor_scalar(stage[n][s][:], sl(index, tile, reg), float(times),
                                                       float(plus), ALU.mult, ALU.add)
                            last.then_inc(staged, 1)

                        def used(s, tile, reg):
                            last = None
                            for n, job in enumerate(jobs):
                                if job[6] is not None:
                                    last = job[6](V, moved[n][s], tile, reg)
                            if last is not None:
                                ch.link(last)

                        put(0, 0)
                        put(1, TG)
                        n0 = k0 // 2

                        def step(i, s, dense, more, put_next):
                            reg = not isinstance(i, int)
                            if dense:
                                dense_dve_a(dve, ch, s, i + n0, more)
                            dve.wait_ge(done[s], per * i + per)
                            used(s, i * (2 * TG) + s * TG, reg)
                            if put_next:
                                put(s, i * (2 * TG) + (2 + s) * TG)
                            if dense:
                                dense_dve_b(dve, ch, s, more)

                        def behind(i, s):
                            return min(2, NGROUPS - 1 - (k0 + 2 * i + s))

                        loop_end = min(BODIES - 1, (NGROUPS - k0) // 2 - 2)
                        with dve.Fori(0, loop_end) as i:
                            for s in range(2):
                                step(i, s, True, 2, True)
                            ch.close()
                        for i in range(loop_end, BODIES):
                            for s in range(2):
                                step(i, s, k0 + 2 * i + s < NGROUPS, behind(i, s), i < BODIES - 1)
                            ch.close()

                    dense_beside(block, k0)

        def dense_beside(block, k0):
            last_body = min(BODIES, (NGROUPS - k0) // 2)
            is_last = k0 + 2 * last_body == NGROUPS
            loop_end = last_body - 2 if is_last else last_body

            @block.sync
            def _(sp):
                if k0 == 0:
                    sp.dma_start(dx[0][:], node_rows(x, 0)).then_inc(d_loaded[0], 16)
                    sp.dma_start(dx[1][:], node_rows(x, 1)).then_inc(d_loaded[1], 16)
                    for s in range(2):
                        sp.nop().then_inc(d_stored[s], 16)
                with sp.Fori(0, loop_end) as i:
                    for s in range(2):
                        d_load(sp, i * 2 + (k0 + 2 + s), s)
                        d_store(sp, i * 2 + (k0 + s), s)
                for k in range(k0 + 2 * loop_end, k0 + 2 * last_body):
                    if k + 2 < NGROUPS:
                        d_load(sp, k + 2, k % 2)
                    if k == NGROUPS - 1:
                        sp.wait_ge(d_stored[1 - k % 2], 16 * (1 + (k + 1) // 2))
                    d_store(sp, k, k % 2)
                if is_last:
                    for s in range(2):
                        sp.wait_ge(d_stored[s], 16 * (1 + NGROUPS // 2))

            @block.scalar
            def _(act):
                nc.scalar.preload_act_table(ACT.Sqrt)
                if k0 == 0:
                    for s in range(2):
                        d_root1(act, s)
                    d_norm1(act, 0)
                    d_copy(act, 0)
                    d_hid(act, 0)
                with act.Fori(0, loop_end) as i:
                    for s in range(2):
                        dense_act(act, s)
                for k in range(k0 + 2 * loop_end, k0 + 2 * last_body):
                    dense_act(act, k % 2, min(2, NGROUPS - 1 - k))

            @block.tensor
            def _(pe):
                if k0 == 0:
                    d_turn(pe, 0)
                    d_first(pe, 0)
                with pe.Fori(0, loop_end) as i:
                    for s in range(2):
                        dense_pe(pe, s)
                for k in range(k0 + 2 * loop_end, k0 + 2 * last_body):
                    dense_pe(pe, k % 2, min(2, NGROUPS - 1 - k))

        def dense_act(act, s, more=2):
            if more:
                d_norm1(act, 1 - s)
                d_copy(act, 1 - s)
            if more > 1:
                d_root1(act, s)
            if more:
                d_hid(act, 1 - s)
            d_root2(act, s)

        def dense_pe(pe, s, more=2):
            d_second(pe, s)
            if more:
                d_turn(pe, 1 - s)
                d_first(pe, 1 - s)

        def sl(t, tile, reg, k=TG):
            return t[:, bass.ds(tile, k)] if reg else t[:, tile:tile + k]

        LOW_BITS = 9
        BINS = 1 << LOW_BITS
        HIGH_BINS = (N >> LOW_BITS) + 1
        PAD_EDGES = EP - E

        def radix_phase(tag, k0, first_pass, bins, load, target, target_row):
            with Phase(nc) as st:
                rec = sb(st, f"{tag}_rec", [P, NT + 2 * TG, 4], I32)
                raw = sb(st, f"{tag}_raw", [P, 3, NT], I32)
                digit_i = sb(st, f"{tag}_digit_i", [P, NT + 2 * TG], I32)
                digit = sb(st, f"{tag}_digit", [P, NT + 2 * TG])
                number_i = sb(st, f"{tag}_number_i", [P, bins], I32)
                number = sb(st, f"{tag}_number", [P, bins])
                count = sb(st, f"{tag}_count", [P, bins])
                before = sb(st, f"{tag}_before", [P, bins])
                total = sb(st, f"{tag}_total", [P, bins])
                hit = sb(st, f"{tag}_hit", [P, bins])
                zeros = sb(st, f"{tag}_zeros", [P, bins])
                lower = sb(st, f"{tag}_lower", [P, P])
                ones = sb(st, f"{tag}_ones", [P, P])
                place = two(sb, st, f"{tag}_place", [P, TG])
                stage = two(sb, st, f"{tag}_stage", [P, TG], I32)
                moved = two(sb, st, f"{tag}_moved", [P, TG, 4], I32)
                ps_lower, ps_total = pb(st, f"{tag}_pslower"), pb(st, f"{tag}_pstotal")
                loaded, ready, cleared, triangle, counted, summed, staged = [sem(st, f"{tag}_{n}") for n in (
                    "loaded", "ready", "cleared", "triangle", "counted", "summed", "staged")]
                sent = two(sem, st, f"{tag}_sent")
                with nc.Block() as block:
                    @block.gpsimd
                    def _(gp):
                        nc.gpsimd.memset(rec[:], 0)
                        nc.gpsimd.memset(raw[:], 0).then_inc(ready, 1)
                        gp.wait_ge(ready, 1)
                        nc.gpsimd.memset(raw[96:P, 0, :], N).then_inc(ready, 1)
                        gp.wait_ge(ready, 2)
                        nc.gpsimd.iota(number_i[:], pattern=[[1, bins]], base=0, channel_multiplier=0)
                        nc.gpsimd.memset(zeros[:], 0.0)
                        nc.gpsimd.memset(count[:], 0.0)
                        nc.gpsimd.memset(ones[:], 1.0)
                        nc.gpsimd.memset(lower[:], 1.0).then_inc(cleared, 1)
                        gp.wait_ge(cleared, 1)
                        nc.gpsimd.affine_select(out=lower[:], in_=lower[:], compare_op=ALU.is_gt, fill=0.0,
                                                base=0, pattern=[[1, P]], channel_multiplier=-1).then_inc(triangle, 1)
                        if first_pass:
                            nc.gpsimd.iota(rec[:, 0:NT, 3], pattern=[[1, NT]], base=0, channel_multiplier=NT)\
                                .then_inc(triangle, 1)

                    @block.sync
                    def _(sp):
                        sp.wait_ge(ready, 2)
                        if first_pass:
                            for n, a in enumerate((src, dst, weight.bitcast(I32))):
                                sp.dma_start(raw[0:E // NT, n, :], a.rearrange("(p t) -> p t", t=NT))\
                                    .then_inc(loaded, 16)
                        else:
                            sp.dma_start(rec[:, 0:NT, :], load.rearrange("(p t) k -> p t k", p=P)).then_inc(loaded, 16)

                    @block.vector
                    def _(dve):
                        ch = Chain(dve, dve_done)
                        V = nc.vector
                        dve.wait_ge(loaded, 48 if first_pass else 16)
                        if first_pass:
                            dve.wait_ge(triangle, 2)
                            for n in range(3):
                                last = V.tensor_copy(rec[:, 0:NT, n], raw[:, n, :])
                            ch.link(last)
                        else:
                            dve.wait_ge(triangle, 1)
                        if first_pass:
                            ch.link(V.tensor_scalar(digit_i[:], rec[:, :, 0], bins - 1, None, ALU.bitwise_and))
                        else:
                            ch.link(V.tensor_scalar(digit_i[:], rec[:, :, 0], LOW_BITS, None, ALU.logical_shift_right))
                        V.tensor_copy(digit[:], digit_i[:])
                        ch.link(V.tensor_copy(number[:], number_i[:]))
                        ch.close()
                        with dve.Fori(0, BODIES) as i:
                            for j in range(2 * TG):
                                t = i * (2 * TG) + j
                                ch.link(V.scalar_tensor_tensor(out=count[:], in0=number[:], scalar=digit[:, bass.ds(t, 1)],
                                                               in1=count[:], op0=ALU.is_equal, op1=ALU.add))
                            ch.close()
                        V.nop().then_inc(counted, 1)
                        take(dve, summed)
                        ch.link(V.tensor_copy(total[:], ps_total[:, 0:bins]))
                        ch.link(V.tensor_tensor_scan(before[:], zeros[:], total[:], 0.0, ALU.add, ALU.add))
                        ch.link(V.tensor_tensor(before[:], before[:], total[:], ALU.subtract))
                        ch.link(V.tensor_tensor(before[:], ps_lower[:, 0:bins], before[:], ALU.add))
                        ch.close()

                    @block.tensor
                    def _(pe):
                        pe.wait_ge(triangle, 1)
                        take(pe, counted)
                        nc.tensor.matmul(ps_lower[:, 0:bins], lower[:], count[:], start=True, stop=True)
                        nc.tensor.matmul(ps_total[:, 0:bins], ones[:], count[:], start=True, stop=True).then_inc(summed, 1)

                with nc.Block() as block:
                    @block.gpsimd
                    def _(gp):
                        bound = gp.to_reg(EP - 1 + target_row)
                        with gp.Fori(0, BODIES) as i:
                            for s in range(2):
                                take(gp, staged)
                                for j in range(TG):
                                    gp.indirect_dma_start(
                                        target, bass.IndirectOffsetOnAxis(ap=stage[s][:, j:j + 1], axis=0),
                                        moved[s][:, j, :], None, bounds_check=bound, oob_is_err=False)\
                                        .then_inc(sent[s], 16)

                    @block.vector
                    def _(dve):
                        ch = Chain(dve, dve_done)
                        V = nc.vector

                        def put(s, tile):
                            for j in range(TG):
                                d = digit[:, bass.ds(tile + j, 1)]
                                V.scalar_tensor_tensor(out=hit[:], in0=number[:], scalar=d, in1=before[:],
                                                       op0=ALU.is_equal, op1=ALU.mult, accum_out=place[s][:, j:j + 1])\
                                    .then_inc(dve_done, 1)
                                ch.n += 1
                                dve.wait_ge(dve_done, ch.n)
                                ch.link(V.scalar_tensor_tensor(out=before[:], in0=number[:], scalar=d, in1=before[:],
                                                               op0=ALU.is_equal, op1=ALU.add))
                            V.tensor_copy(moved[s][:], rec[:, bass.ds(tile, TG), :])
                            V.tensor_scalar(stage[s][:], place[s][:], float(target_row), None, ALU.add)\
                                .then_inc(staged, 1)

                        put(0, 0)
                        put(1, TG)
                        ch.close()
                        n0 = k0 // 2
                        if k0 == 0:
                            V.nop().then_inc(d_taken, 1)
                            for s in range(2):
                                d_stats1(dve, ch, s, 0)
                            for s in range(2):
                                d_affine1_of(dve, ch, s)
                            ch.close()

                        def step(i, s, more):
                            dense_dve_a(dve, ch, s, i + n0)
                            dve.wait_ge(sent[s], 64 * i + 64)
                            if more:
                                put(s, i * (2 * TG) + (2 + s) * TG)
                            dense_dve_b(dve, ch, s)

                        with dve.Fori(0, BODIES - 1) as i:
                            for s in range(2):
                                step(i, s, True)
                            ch.close()
                        for s in range(2):
                            step(BODIES - 1, s, False)
                        ch.close()

                    dense_beside(block, k0)

        assert E % NT == 0 and E // NT >= 96
        radix_phase("ra", 0, True, BINS, None, rec_low, 0)
        radix_phase("rb", 2 * BODIES, False, HIGH_BINS, rec_low, rec_src, 1)

        with Phase(nc) as st:
            recA = [sb(st, f"g_rec{n}", [HALF, 2, P, 4], I32) for n in range(3)]
            kA = [sb(st, f"g_key{n}", [HALF, 2, P]) for n in range(3)]
            first, last_, t1, outA, srcA, dstA, numA, wA = [sb(st, f"g_{n}", [HALF, 2, P]) for n in (
                "first", "last", "t1", "out", "src", "dst", "num", "w")]
            keepA = sb(st, "g_keep", [HALF, 2, P], BF16)
            edge_pads = sb(st, "g_pads", [1, 4], I32)
            g_pad, g_padded, g_ld, g_own, g_field, g_turn, g_keep_ok, g_st = [sem(st, f"g_{n}") for n in (
                "pad", "padded", "ld", "own", "field", "turn", "keep_ok", "stored")]
            psg = [pb(st, f"g_ps{n}") for n in range(3)]
            with nc.Block() as block:
                @block.gpsimd
                def _(gp):
                    nc.gpsimd.memset(edge_pads[:], -1).then_inc(g_pad, 1)
                    nc.gpsimd.iota(entry_src[:, 0:NT, 0], pattern=[[P, NT]], base=1, channel_multiplier=1)

                @block.sync
                def _(sp):
                    take(sp, g_pad)
                    for r in (0, EP + 1):
                        sp.dma_start(rec_src[r:r + 1, :], edge_pads[:]).then_inc(g_padded, 16)
                    sp.wait_ge(g_padded, 32)
                    for n in range(3):
                        for h in range(2):
                            sp.dma_start(recA[n][:, h], rec_src[n + h * HALF * P:n + (h + 1) * HALF * P, :]
                                         .rearrange("(t c) k -> t c k", c=P)).then_inc(g_ld, 16)
                    take(sp, g_keep_ok)
                    sp.dma_start(keep_src[0].rearrange("(h t c) -> t h c", h=2, c=P), keepA[:]).then_inc(g_st, 16)
                    sp.wait_ge(g_st, 16)

                @block.vector
                def _(dve):
                    ch = Chain(dve, dve_done)
                    V = nc.vector
                    dve.wait_ge(g_ld, 16 * 6)
                    for n in range(3):
                        V.tensor_copy(kA[n][:], recA[n][:, :, :, 0])
                    V.tensor_copy(t1[:], recA[1][:, :, :, 1])
                    V.tensor_copy(wA[:].bitcast(I32), recA[1][:, :, :, 2])
                    ch.link(V.tensor_copy(numA[:], recA[1][:, :, :, 3]))
                    V.tensor_scalar(dstA[:], t1[:], float(N - 1), None, ALU.min)
                    V.tensor_scalar(srcA[:], kA[1][:], float(N - 1), None, ALU.min)
                    V.tensor_tensor(first[:], kA[1][:], kA[0][:], ALU.not_equal)
                    V.tensor_tensor(last_[:], kA[1][:], kA[2][:], ALU.not_equal)
                    ch.link(V.tensor_scalar(outA[:], kA[1][:], float(FAR), None, ALU.add))
                    V.tensor_scalar(keepA[:], first[:], -1.0, 1.0, ALU.mult, ALU.add).then_inc(g_keep_ok, 1)
                    V.scalar_tensor_tensor(out=outA[:], in0=last_[:], scalar=-float(FAR), in1=outA[:], op0=ALU.mult,
                                           op1=ALU.add).then_inc(g_field, 1)
                    take(dve, g_turn)
                    V.tensor_copy(k_src[:, 0:NT], psg[0][:, 0:NT])
                    V.tensor_copy(k_dst[:, 0:NT], psg[0][:, NT:2 * NT])
                    V.tensor_copy(k_out[:, 0:NT], psg[1][:, 0:NT])
                    V.tensor_copy(k_w[:], psg[1][:, NT:2 * NT])
                    V.tensor_scalar(entry_src[:, 0:NT, 1], psg[2][:, 0:NT], 1.0, None, ALU.add)
                    ch.close()

                @block.tensor
                def _(pe):
                    take(pe, g_field)
                    for n, f in enumerate((srcA, dstA, outA, wA, numA)):
                        for h in range(2):
                            c = (n % 2) * NT + h * HALF
                            last = nc.tensor.transpose(psg[n // 2][:, c:c + HALF], f[:, h, :], ident[0:HALF, 0:HALF])
                    last.then_inc(g_turn, 1)

        c_got = [sb(main, f"c_got{n}", [P, NT]) for n in range(2)]
        c_got_dst = sb(main, "c_got_dst", [P, NT])
        c_num = sb(main, "c_num", [P, NT])

        def of_edge_src(V, moved, tile, reg):
            return V.tensor_copy(sl(k_pick, tile, reg), moved[:, :, 2])

        def of_src(V, moved, tile, reg):
            V.tensor_copy(sl(c_got[0], tile, reg), moved[:, :, 0])
            V.tensor_copy(sl(c_nts, tile, reg), moved[:, :, 1])
            V.tensor_copy(sl(c_got[1], tile, reg), moved[:, :, 2])
            return V.tensor_copy(sl(c_num, tile, reg), moved[:, :, 3])

        def of_dst(V, moved, tile, reg):
            V.tensor_copy(sl(c_ntd, tile, reg), moved[:, :, 1])
            return V.tensor_copy(sl(c_got_dst, tile, reg), moved[:, :, 2])

        halves_of_nodes = node_table.rearrange("n (h k) -> (n h) k", k=2)
        cells_of_nodes = node_table.rearrange("n (c k) -> (n c) k", k=1)
        table_phase("tp", 4 * BODIES, [(cells_of_nodes, i_out, 4, 0, 1, entry_dst, None),
                                       (halves_of_nodes, k_out, 2, 1, 2, entry_src, None)])
        table_phase("tg", 6 * BODIES, [(node_table, k_dst, 1, 0, 4, None, of_edge_src),
                                       (node_table, i_src, 1, 0, 4, None, of_src),
                                       (node_table, i_dst, 1, 0, 4, None, of_dst)])

        with Phase(nc) as st:
            pf = sb(st, "pf", [P, NT])
            t1, t2, t3 = [sb(st, f"q_t{n}", [P, NT]) for n in range(3)]
            codes = sb(st, "codes", [HALF, 2, 2, P], BF16)
            q_turn, q_code, q_st = [sem(st, f"q_{n}") for n in ("turn", "code", "st")]
            psq = two(pb, st, "psq", (P, GE))
            with nc.Block() as block:
                @block.vector
                def _(dve):
                    ch = Chain(dve, dve_done)
                    V = nc.vector
                    ch.link(V.tensor_copy(pf[:], k_pick[:, 0:NT]))
                    for got, to in ((pf, k_pick), (c_got[0], i_pick)):
                        ch.link(V.tensor_scalar(t1[:], got[:], 0.0, float(NONE + 1), ALU.is_equal, ALU.mult))
                        ch.link(V.scalar_tensor_tensor(out=to[:, 0:NT], in0=got[:], scalar=-1.0, in1=t1[:],
                                                       op0=ALU.add, op1=ALU.add))
                    V.tensor_scalar(t1[:], c_got_dst[:], 0.0, None, ALU.is_equal)
                    ch.link(V.tensor_scalar(t2[:], c_last[:], -1.0, 1.0, ALU.mult, ALU.add))
                    ch.link(V.tensor_tensor(t1[:], t1[:], t2[:], ALU.max))
                    ch.link(V.tensor_scalar(t1[:], t1[:], float(NONE + 1), None, ALU.mult))
                    ch.link(V.scalar_tensor_tensor(out=i_dst1[:, 0:NT], in0=c_got_dst[:], scalar=-1.0, in1=t1[:],
                                                   op0=ALU.add, op1=ALU.add))
                    V.tensor_scalar(i_node1[:, 0:NT], c_got[1][:], -1.0, 0.0, ALU.add, ALU.max)
                    V.tensor_copy(t1[:], entry_dst[:, 0:NT, 0])
                    V.tensor_scalar(t2[:], c_got[0][:], 0.0, None, ALU.is_equal)
                    ch.link(V.tensor_copy(t3[:], i_src[:, 0:NT]))
                    ch.link(V.tensor_tensor(t1[:], t1[:], c_num[:], ALU.is_equal))
                    ch.link(V.tensor_tensor(t1[:], t1[:], t2[:], ALU.mult))
                    ch.link(V.tensor_scalar(t1[:], t1[:], -float(FAR), float(FAR), ALU.mult, ALU.add))
                    ch.link(V.tensor_tensor(i_srcout[:, 0:NT], t1[:], t3[:], ALU.add))
                    take(dve, q_turn)
                    for n in range(2):
                        last = V.tensor_copy(codes[:, n], psq[n][0:HALF, 0:2 * P].rearrange("t (h c) -> t h c", h=2))
                    last.then_inc(q_code, 1)
                    ch.close()

                @block.tensor
                def _(pe):
                    for n, c in enumerate((c_nts, c_ntd)):
                        for h in range(2):
                            last = nc.tensor.transpose(psq[n][0:HALF, h * P:(h + 1) * P],
                                                       c[:, h * HALF:(h + 1) * HALF], ident[:])
                    last.then_inc(q_turn, 1)

                @block.sync
                def _(sp):
                    take(sp, q_code)
                    for n, k in enumerate((NTS, NTD)):
                        sp.dma_start(seq_rows[k].rearrange("(h t c) -> t h c", h=2, c=P), codes[:, n]).then_inc(q_st, 16)
                    sp.wait_ge(q_st, 32)

        def bodies(eng, order, step, ch=None):
            with eng.Fori(0, BODIES - 1) as i:
                for o, s in enumerate(order):
                    step(i, o, s, True)
                if ch:
                    ch.close()
            for o, s in enumerate(order):
                step(BODIES - 1, o, s, False)
            if ch:
                ch.close()

        def skewed(eng, order, first, both, ch=None, peel=1, head=0):
            first(order[0])
            if ch:
                ch.close()
            for i in range(head):
                for o, s in enumerate(order):
                    both(i, o, s, 1 - s, 2 * peel - 1)
                if ch:
                    ch.close()
            with eng.Fori(head, BODIES - peel) as i:
                for o, s in enumerate(order):
                    both(i, o, s, 1 - s, 2 * peel - 1)
                if ch:
                    ch.close()
            for i in range(BODIES - peel, BODIES):
                for o, s in enumerate(order):
                    behind = 2 * (BODIES - 1 - i) + 1 - o
                    both(i, o, s, 1 - s if behind else None, max(behind - 1, 0))
                if ch:
                    ch.close()

        def hop_phase(tag, table, index, first_hop, last_hop):
            with Phase(nc) as st:
                stage = two(sb, st, f"{tag}_stage", [P, TG], I32)
                rows = two(sb, st, f"{tag}_rows", [P, TG, D])
                scaled = two(sb, st, f"{tag}_scaled", [P, TG, D])
                keep = two(sb, st, f"{tag}_keep", [P, 1, GE], BF16)
                sums = two(sb, st, f"{tag}_sums", [P, GE])
                outr = two(sb, st, f"{tag}_outr", [P, TG, D])
                ps_m = two(pb, st, f"{tag}_psm")
                ps_r = two(pb, st, f"{tag}_psr")
                gathered = two(sem, st, f"{tag}_gathered")
                kept = two(sem, st, f"{tag}_kept")
                stored = two(sem, st, f"{tag}_stored")
                staged, freed, rdy, turned, scanned, scan_sp, back, copied = [sem(st, f"{tag}_{n}") for n in (
                    "staged", "freed", "rdy", "turned", "scanned", "scan_sp", "back", "copied")]
                if last_hop:
                    stage2 = two(sb, st, f"{tag}_stage2", [P, TG], I32)
                    brow = two(sb, st, f"{tag}_brow", [P, TG, D])
                    e1r = two(sb, st, f"{tag}_e1r", [P, TG, D])
                    e2r = two(sb, st, f"{tag}_e2r", [P, TG, D])
                    acc = two(sb, st, f"{tag}_acc", [P, TG, D])
                    stt = two(sb, st, f"{tag}_stt", [P, TG, 6])
                    mv = two(sb, st, f"{tag}_mv", [P, TG, 2])
                    sd = two(sb, st, f"{tag}_sd", [P, TG])
                    rr = two(sb, st, f"{tag}_rr", [P, TG])
                    bb = two(sb, st, f"{tag}_bb", [P, TG])
                    hops_in = two(sem, st, f"{tag}_hops_in")
                    var, std, affine, loads_free = [sem(st, f"{tag}_{n}") for n in ("var", "std", "affine", "loads_free")]
                per = 128 if last_hop else 64

                with nc.Block() as block:
                    @block.gpsimd
                    def _(gp):
                        bound = gp.to_reg(N - 1 if first_hop else NONE)
                        bound2 = gp.to_reg(N - 1)
                        with gp.Fori(0, BODIES) as i:
                            for s in range(2):
                                take(gp, staged)
                                for j in range(TG):
                                    gp.indirect_dma_start(
                                        rows[s][:, j, :], None, table,
                                        bass.IndirectOffsetOnAxis(ap=stage[s][:, j:j + 1], axis=0),
                                        bounds_check=bound, oob_is_err=False).then_inc(gathered[s], 16)
                                if last_hop:
                                    for j in range(TG):
                                        gp.indirect_dma_start(
                                            brow[s][:, j, :], None, x,
                                            bass.IndirectOffsetOnAxis(ap=stage2[s][:, j:j + 1], axis=0),
                                            bounds_check=bound2, oob_is_err=False).then_inc(gathered[s], 16)

                    @block.sync
                    def _(sp):
                        for s in range(2):
                            sp.nop().then_inc(stored[s], 16)

                        def load(i, s):
                            take(sp, scan_sp)
                            sp.dma_start(keep[s][:], seq_of(keep_src, i, s, 0, 1)).then_inc(kept[s], 16)
                            if last_hop:
                                take(sp, loads_free)
                                sp.dma_start(e1r[s][:], rows_of(e1_rows, i, s)).then_inc(hops_in[s], 16)
                                sp.dma_start(e2r[s][:], rows_of(e2_rows, i, s)).then_inc(hops_in[s], 16)

                        def step(i, o, s, more):
                            if more:
                                load(i + 1, s)
                            sp.wait_ge(copied, 2 * i + (3 + s))
                            sp.dma_start(rows_of(x1_nodes if last_hop else e1_rows if first_hop else e2_rows, i, s),
                                         outr[s][:]).then_inc(stored[s], 16)

                        for s in range(2):
                            load(0, s)
                        bodies(sp, (0, 1), step)
                        for s in range(2):
                            sp.wait_ge(stored[s], 16 * (BODIES + 1))

                    @block.vector
                    def _(dve):
                        ch = Chain(dve, dve_done)
                        V = nc.vector

                        def put(s, tile):
                            reg = not isinstance(tile, int)
                            if last_hop:
                                V.tensor_copy(stage2[s][:], sl(k_src, tile, reg))
                            V.tensor_copy(stage[s][:], sl(index, tile, reg)).then_inc(staged, 1)

                        ch.link(V.memset(sums[1][:], 0.0))
                        ch.close()
                        V.nop().then_inc(scan_sp, 2)
                        if last_hop:
                            V.nop().then_inc(loads_free, 2)
                        put(0, 0)
                        put(1, TG)

                        def front(i, s):
                            tile = i * (2 * TG) + s * TG
                            dve.wait_ge(gathered[s], per * i + per)
                            V.tensor_tensor(scaled[s][:], rows[s][:],
                                            k_w[:, bass.ds(tile, TG)].unsqueeze(2).to_broadcast([P, TG, D]),
                                            ALU.mult).then_inc(rdy, 1)
                            if last_hop:
                                dve.wait_ge(copied, 2 * i + (1 + s))
                                dve.wait_ge(hops_in[s], 32 * i + 32)
                                ch.link(V.tensor_tensor(acc[s][:], e1r[s][:], e2r[s][:], ALU.add))
                                V.nop().then_inc(loads_free, 1)
                                ch.link(V.scalar_tensor_tensor(out=acc[s][:], in0=brow[s][:], scalar=5.0,
                                                               in1=acc[s][:], op0=ALU.mult, op1=ALU.add))
                            dve.wait_ge(kept[s], 16 * i + 16)
                            take(dve, turned)
                            put(s, i * (2 * TG) + (2 + s) * TG)
                            ch.link(V.tensor_tensor_scan(sums[s][:], keep[s][:, 0, :], ps_m[s][:],
                                                         sums[1 - s][:, GE - 1:GE], ALU.mult, ALU.add))
                            V.nop().then_inc(scanned, 1)
                            V.nop().then_inc(scan_sp, 1)

                        def both(i, o, s, nxt, more):
                            if nxt is not None:
                                front(i + o, nxt)
                            if last_hop:
                                take(dve, back)
                                ch.link(V.tensor_tensor(acc[s][:], ps_r[s][:].rearrange("p (j f) -> p j f", j=TG),
                                                        acc[s][:], ALU.add))
                                for j in range(TG):
                                    last = V.bn_stats(stt[s][:, j, :], acc[s][:, j, :])
                                ch.link(last)
                                for j in range(TG):
                                    last = V.bn_aggr(mv[s][:, j, :], stt[s][:, j, :])
                                last.then_inc(var, 1)
                                take(dve, std)
                                ch.link(V.reciprocal(rr[s][:], sd[s][:]))
                                V.scalar_tensor_tensor(out=bb[s][:], in0=mv[s][:, :, 0], scalar=-1.0, in1=rr[s][:],
                                                       op0=ALU.mult, op1=ALU.mult).then_inc(affine, 1)

                        skewed(dve, (0, 1), lambda s: front(0, s), both, ch)

                    @block.scalar
                    def _(act):
                        nc.scalar.preload_act_table(ACT.Sqrt)
                        nc.scalar.nop().then_inc(copied, 2)

                        def step(i, s):
                            if last_hop:
                                act.wait_ge(stored[s], 16 * i + 16)
                                take(act, var)
                                nc.scalar.activation(sd[s][:], mv[s][:, :, 1], ACT.Sqrt,
                                                     bias=eps_col[:, EPS16:EPS16 + 1]).then_inc(std, 1)
                                take(act, affine)
                                for j in range(TG):
                                    last = nc.scalar.activation(outr[s][:, j, :], acc[s][:, j, :], ACT.Identity,
                                                                bias=bb[s][:, j:j + 1], scale=rr[s][:, j:j + 1])
                                last.then_inc(copied, 1)
                            else:
                                act.wait_ge(stored[s], 16 * i + 16)
                                take(act, back)
                                nc.scalar.activation(outr[s][:].rearrange("p j f -> p (j f)"), ps_r[s][:],
                                                     ACT.Copy).then_inc(copied, 1)

                        with act.Fori(0, BODIES) as i:
                            for s in range(2):
                                step(i, s)

                    @block.tensor
                    def _(pe):
                        def front(s):
                            take(pe, rdy)
                            for j in range(TG):
                                last = nc.tensor.transpose(ps_m[s][:, j * P:(j + 1) * P], scaled[s][:, j, :], ident[:])
                            last.then_inc(turned, 1)

                        def both(i, o, s, nxt, more):
                            if nxt is not None:
                                front(nxt)
                            pe.wait_ge(copied, 2 * i + (1 + s))
                            take(pe, scanned)
                            for j in range(TG):
                                last = nc.tensor.transpose(ps_r[s][:, j * P:(j + 1) * P],
                                                           sums[s][:, j * P:(j + 1) * P], ident[:])
                            last.then_inc(back, 1)

                        skewed(pe, (0, 1), front, both)

        dense_psum.close()
        hop_phase("h1", x, k_dst, True, False)
        hop_phase("h2", e1_rows, k_pick, False, False)
        hop_phase("h3", e2_rows, k_pick, False, True)

        def norm_stats(V, ch, y, stt, mv, s, var):
            for j in range(TG):
                last = V.bn_stats(stt[s][:, j, :], y[s][:, j, :])
            ch.link(last)
            for j in range(TG):
                last = V.bn_aggr(mv[s][:, j, :], stt[s][:, j, :])
            last.then_inc(var, 1)

        def norm_rows(act, out_rows, y, rr, bb, s):
            for j in range(TG):
                last = nc.scalar.activation(out_rows[s][:, j, :], y[s][:, j, :], ACT.Identity,
                                            bias=bb[s][:, j:j + 1], scale=rr[s][:, j:j + 1])
            return last

        def turn(out_bank, rows3d):
            for j in range(TG):
                last = nc.tensor.transpose(out_bank[:, j * P:(j + 1) * P], rows3d[:, j, :], ident[:])
            return last

        def tiles(t):
            return t.rearrange("p (j f) -> p j f", j=TG)

        def cols(c, i, s):
            return c[:, bass.ds(i * (2 * TG) + s * TG, TG)].unsqueeze(2).to_broadcast([P, TG, D])

        def local_put(V, which, aff, stage, b, s, aff_ok, staged):
            t = b * (2 * TG) + s * TG
            if which is not None:
                V.tensor_copy(aff[s][:], local[which][:, bass.ds(t, TG), :]).then_inc(aff_ok, 1)
            V.tensor_copy(stage[s][:], i_pick[:, bass.ds(t, TG)]).then_inc(staged, 1)

        def local_rows(act, i, s, a0_in, aff_ok, x_ok, xs, a0r, aff):
            act.wait_ge(a0_in[s], 16 * i + 16)
            take(act, aff_ok)
            for j in range(TG):
                last = nc.scalar.activation(xs[s][:, j, :], a0r[s][:, j, :], ACT.Identity,
                                            bias=aff[s][:, j, 1:2], scale=aff[s][:, j, 0:1])
            last.then_inc(x_ok, 1)

        def picks(gp, bound, table, xs, stage, picked, s):
            for j in range(TG):
                gp.indirect_dma_start(xs[s][:, j, :], None, table,
                                      bass.IndirectOffsetOnAxis(ap=stage[s][:, j:j + 1], axis=0),
                                      bounds_check=bound, oob_is_err=False).then_inc(picked[s], 16)

        with Phase(nc) as st:
            xr, dr, outd = [two(sb, st, n, [P, TG, D]) for n in ("b_xr", "b_dr", "b_out")]
            stage = two(sb, st, "b_stage", [P, 3, TG], I32)
            stt = two(sb, st, "b_stt", [P, TG, 6])
            mv = two(sb, st, "b_mv", [P, TG, 2])
            sd, rr, bb = [two(sb, st, n, [P, TG]) for n in ("b_sd", "b_rr", "b_bb")]
            got, src_got, picked, src_st, dst_st = [two(sem, st, f"b_{n}") for n in (
                "got", "src_got", "picked", "src_st", "dst_st")]
            staged, stats_ok, std, affine, normed = [sem(st, f"b_{n}") for n in (
                "staged", "stats", "std", "affine", "normed")]
            with nc.Block() as block:
                @block.gpsimd
                def _(gp):
                    bound = gp.to_reg(EP - 1)
                    bound_x = gp.to_reg(N - 1)

                    def load(i, s):
                        if not isinstance(i, int) or i:
                            gp.wait_ge(src_st[s], 16 * i)
                        take(gp, staged)
                        for t, k, table, b, q in ((xr, 0, x1_nodes, bound, src_got), (dr, 1, x, bound_x, got)):
                            for j in range(TG):
                                gp.indirect_dma_start(t[s][:, j, :], None, table,
                                                      bass.IndirectOffsetOnAxis(ap=stage[s][:, k, j:j + 1], axis=0),
                                                      bounds_check=b, oob_is_err=False).then_inc(q[s], 16)

                    load(0, 0)
                    load(0, 1)

                    def step(i, o, s, more):
                        take(gp, normed)
                        for j in range(TG):
                            gp.indirect_dma_start(outd[s][:, j, :], None, x1_nodes,
                                                  bass.IndirectOffsetOnAxis(ap=stage[s][:, 2, j:j + 1], axis=0),
                                                  bounds_check=bound, oob_is_err=False).then_inc(picked[s], 16)
                        if more:
                            load(i + 1, s)

                    bodies(gp, (0, 1), step)

                @block.sync
                def _(sp):
                    for s in range(2):
                        sp.nop().then_inc(dst_st[s], 16)

                    def step(i, o, s, more):
                        sp.wait_ge(src_got[s], 64 * i + 64)
                        sp.dma_start(rows_of(src_x1, i, s), xr[s][:]).then_inc(src_st[s], 16)
                        sp.wait_ge(picked[s], 64 * i + 64)
                        sp.dma_start(rows_of(x1_rows, i, s), outd[s][:]).then_inc(dst_st[s], 16)

                    bodies(sp, (0, 1), step)
                    for s in range(2):
                        sp.wait_ge(src_st[s], 16 * BODIES)
                        sp.wait_ge(dst_st[s], 16 * (BODIES + 1))

                @block.vector
                def _(dve):
                    ch = Chain(dve, dve_done)
                    V = nc.vector

                    def put(b, s):
                        t = b * (2 * TG) + s * TG
                        V.tensor_copy(stage[s][:, 0, :], i_node1[:, bass.ds(t, TG)])
                        V.tensor_copy(stage[s][:, 1, :], i_dst[:, bass.ds(t, TG)])
                        V.tensor_copy(stage[s][:, 2, :], i_dst1[:, bass.ds(t, TG)]).then_inc(staged, 1)

                    put(0, 0)
                    put(0, 1)

                    def step(i, o, s, more):
                        t = i * (2 * TG) + s * TG
                        dve.wait_ge(src_got[s], 64 * i + 64)
                        for j in range(TG):
                            last = V.bn_stats(src_stats[:, bass.ds(t + j, 1), :], xr[s][:, j, :])
                        ch.link(last)
                        dve.wait_ge(got[s], 64 * i + 64)
                        norm_stats(V, ch, dr, stt, mv, s, stats_ok)
                        take(dve, std)
                        ch.link(V.reciprocal(rr[s][:], sd[s][:]))
                        ch.link(V.tensor_tensor(rr[s][:], rr[s][:], c_last[:, bass.ds(t, TG)], ALU.mult))
                        V.scalar_tensor_tensor(out=bb[s][:], in0=mv[s][:, :, 0], scalar=-1.0, in1=rr[s][:],
                                               op0=ALU.mult, op1=ALU.mult).then_inc(affine, 1)
                        if more:
                            dve.wait_ge(picked[s], 64 * i + 64)
                            put(i + 1, s)

                    bodies(dve, (0, 1), step, ch)

                @block.scalar
                def _(act):
                    nc.scalar.preload_act_table(ACT.Sqrt)

                    def step(i, o, s, more):
                        take(act, stats_ok)
                        nc.scalar.activation(sd[s][:], mv[s][:, :, 1], ACT.Sqrt, bias=eps_col[:, EPS_1:EPS_1 + 1])\
                            .then_inc(std, 1)
                        act.wait_ge(dst_st[s], 16 * i + 16)
                        take(act, affine)
                        norm_rows(act, outd, dr, rr, bb, s).then_inc(normed, 1)

                    bodies(act, (0, 1), step)

        with Phase(nc) as st:
            mean = sb(st, "l_mean", [P, NT])
            diff = sb(st, "l_diff", [P, NT])
            vv = sb(st, "l_var", [P, NT])
            root = [sb(st, f"l_root{n}", [P, NT]) for n in range(2)]
            l_var, l_root = [sem(st, f"l_{n}s") for n in ("var", "root")]
            with nc.Block() as block:
                @block.vector
                def _(dve):
                    ch = Chain(dve, dve_done)
                    V = nc.vector
                    S = src_stats
                    V.tensor_tensor(mean[:], S[:, :, 1], S[:, :, 4], ALU.add)
                    V.tensor_tensor(diff[:], S[:, :, 1], S[:, :, 4], ALU.subtract)
                    ch.link(V.tensor_tensor(vv[:], S[:, :, 2], S[:, :, 5], ALU.add))
                    V.tensor_scalar(mean[:], mean[:], 0.5, None, ALU.mult)
                    V.tensor_scalar(vv[:], vv[:], 1.0 / D, None, ALU.mult)
                    ch.link(V.tensor_tensor(diff[:], diff[:], diff[:], ALU.mult))
                    V.scalar_tensor_tensor(out=vv[:], in0=diff[:], scalar=0.25, in1=vv[:], op0=ALU.mult,
                                           op1=ALU.add).then_inc(l_var, 1)
                    take(dve, l_root)
                    for n in range(2):
                        last = V.reciprocal(local[n][:, :, 0], root[n][:])
                    ch.link(last)
                    for n in range(2):
                        V.scalar_tensor_tensor(out=local[n][:, :, 1], in0=mean[:], scalar=-1.0,
                                               in1=local[n][:, :, 0], op0=ALU.mult, op1=ALU.mult)
                    ch.close()

                @block.scalar
                def _(act):
                    nc.scalar.preload_act_table(ACT.Sqrt)
                    take(act, l_var)
                    for n, (c, e) in enumerate(((1.0, EPS1), (CS, EPS_SQ))):
                        last = nc.scalar.activation(root[n][:], vv[:], ACT.Sqrt, bias=eps_col[:, e:e + 1], scale=c)
                    last.then_inc(l_root, 1)

        with Phase(nc) as st:
            xs, x1r = [two(sb, st, n, [P, TG, D]) for n in ("a_xs", "a_x1r")]
            masks = two(sb, st, "a_masks", [P, 5, GE], BF16)
            onehot = two(sb, st, "a_onehot", [ETYPES, GE])
            sT, dT = [[sb(st, f"{n}{t}", [P, GE]) for t in range(NTYPES)] for n in ("a_sT", "a_dT")]
            kT = [sb(st, f"a_kT{t}", [P, GE]) for t in range(ETYPES)]
            prod = sb(st, "a_prod", [P, GE])
            pri_e, q_all, lg, mx, msg = [two(sb, st, n, [P, GE]) for n in ("a_pri", "a_q", "a_lg", "a_mx", "a_msg")]
            b_sT, b_k, b_m, b_dT, b_q, b_l, b_p = [pb(st, f"a_ps{n}") for n in range(7)]
            xs_in, x1_in, masks_in, msg_st, lm_st = [two(sem, st, f"a_{n}") for n in (
                "xs_in", "x1_in", "masks_in", "msg_st", "lm_st")]
            (masks_free, xs_free, x1_free, s_turned, s_copied, s_masked, k_ok, k_copied, k_masked, m_ok,
             m_copied, x1_turned, x1_copied, x1_masked, q_ok, prod_ok, l_ok, pri_ok, pri_copied, lg_ok, mx_ok) = [
                sem(st, f"a_{n}") for n in (
                    "masks_free", "xs_free", "x1_free", "s_turned", "s_copied", "s_masked", "k_ok",
                    "k_copied", "k_masked", "m_ok", "m_copied", "x1_turned", "x1_copied", "x1_masked", "q_ok",
                    "prod_ok", "l_ok", "pri_ok", "pri_copied", "lg_ok", "mx_ok")]
            ORDER = (1, 0)

            def body_of(i):
                return (BODIES - 1) - i

            with nc.Block() as block:
                @block.sync
                def _(sp):
                    for s in range(2):
                        sp.nop().then_inc(msg_st[s], 16)
                        sp.nop().then_inc(lm_st[s], 32)

                    def load_xs(b, s):
                        sp.dma_start(xs[s][:], rows_of(src_x1, b, s)).then_inc(xs_in[s], 16)

                    def load_x1(b, s):
                        sp.dma_start(x1r[s][:], rows_of(x1_rows, b, s)).then_inc(x1_in[s], 16)

                    def load_masks(b, s):
                        sp.dma_start(masks[s][:], seq_of(seq_rows, b, s, NOTLAST, NTD + 1)).then_inc(masks_in[s], 16)
                        sp.dma_start(onehot[s][:], onehot_rows[:, bass.ds(b * BODY + s * GE, GE)])\
                            .then_inc(masks_in[s], 16)

                    for s in ORDER:
                        load_x1(BODIES - 1, s)
                        load_xs(BODIES - 1, s)
                        load_masks(BODIES - 1, s)

                    def step(i, o, s, more):
                        b = body_of(i)
                        if more:
                            take(sp, x1_free)
                            load_x1(b - 1, s)
                            take(sp, xs_free)
                            load_xs(b - 1, s)
                        sp.wait_ge(m_copied, 2 * i + (o + 1))
                        sp.dma_start(lrm_of(b, s, 2, 3), msg[s][:].unsqueeze(1)).then_inc(msg_st[s], 16)
                        take(sp, lg_ok)
                        sp.dma_start(lrm_of(b, s, 0, 1), lg[s][:].unsqueeze(1)).then_inc(lm_st[s], 16)
                        take(sp, mx_ok)
                        sp.dma_start(lrm_of(b, s, 1, 2), mx[s][:].unsqueeze(1)).then_inc(lm_st[s], 16)
                        if more:
                            take(sp, masks_free)
                            load_masks(b - 1, s)

                    bodies(sp, ORDER, step)
                    for s in range(2):
                        sp.wait_ge(msg_st[s], 16 * (BODIES + 1))
                        sp.wait_ge(lm_st[s], 32 * (BODIES + 1))

                @block.scalar
                def _(act):
                    def rows_copied():
                        take(act, x1_turned)
                        nc.scalar.activation(dT[0][:], b_dT[:], ACT.Copy).then_inc(x1_copied, 1)
                        take(act, s_turned)
                        nc.scalar.activation(sT[0][:], b_sT[:], ACT.Copy).then_inc(s_copied, 1)

                    def rest_copied(s):
                        take(act, pri_ok)
                        nc.scalar.activation(pri_e[s][:], b_p[:], ACT.Copy).then_inc(pri_copied, 1)
                        take(act, k_ok)
                        nc.scalar.activation(kT[0][:], b_k[:], ACT.Copy).then_inc(k_copied, 1)

                    def first(s):
                        rows_copied()
                        rest_copied(s)

                    def both(i, o, s, nxt, more):
                        if nxt is not None:
                            rows_copied()
                        act.wait_ge(msg_st[s], 16 * i + 16)
                        take(act, m_ok)
                        nc.scalar.activation(msg[s][:], b_m[:], ACT.Copy).then_inc(m_copied, 1)
                        if nxt is not None:
                            rest_copied(nxt)

                    skewed(act, ORDER, first, both)

                @block.vector
                def _(dve):
                    ch = Chain(dve, dve_done)
                    V = nc.vector
                    V.memset(q_all[0][:], 0.0)
                    ch.link(V.memset(mx[0][:], 0.0))
                    ch.close()

                    def queries_masked(i, s):
                        dve.wait_ge(masks_in[s], 32 * i + 32)
                        take(dve, x1_copied)
                        for t in range(1, NTYPES):
                            V.scalar_tensor_tensor(out=dT[t][:], in0=masks[s][:, NTD - NOTLAST, :], scalar=float(t),
                                                   in1=b_dT[:], op0=ALU.is_equal, op1=ALU.mult).then_inc(x1_masked, 1)

                    def sources_masked(s):
                        take(dve, s_copied)
                        for t in range(1, NTYPES):
                            V.scalar_tensor_tensor(out=sT[t][:], in0=masks[s][:, NTS - NOTLAST, :], scalar=float(t),
                                                   in1=b_sT[:], op0=ALU.is_equal, op1=ALU.mult).then_inc(s_masked, 1)

                    def queries_spread(s):
                        take(dve, q_ok)
                        ch.link(V.tensor_tensor_scan(q_all[s][:, ::-1], masks[s][:, 0, ::-1], b_q[:, ::-1],
                                                     q_all[1 - s][:, 0:1], ALU.mult, ALU.add))

                    def edges_masked(s):
                        take(dve, k_copied)
                        for t in range(1, ETYPES):
                            V.scalar_tensor_tensor(out=kT[t][:], in0=masks[s][:, ET - NOTLAST, :], scalar=float(t),
                                                   in1=b_k[:], op0=ALU.is_equal, op1=ALU.mult).then_inc(k_masked, 1)

                    def first(s):
                        queries_masked(0, s)
                        sources_masked(s)
                        queries_spread(s)
                        edges_masked(s)

                    def both(i, o, s, nxt, more):
                        if nxt is not None:
                            queries_masked(i + o, nxt)
                        dve.wait_ge(m_copied, 2 * i + (o + 1))
                        V.tensor_tensor(prod[:], q_all[s][:], b_m[:], ALU.mult).then_inc(prod_ok, 1)
                        if nxt is not None:
                            sources_masked(nxt)
                        take(dve, l_ok)
                        take(dve, pri_copied)
                        dve.wait_ge(lm_st[s], 32 * i + 32)
                        ch.link(V.tensor_tensor(lg[s][:], pri_e[s][:], b_l[:], ALU.mult))
                        V.nop().then_inc(lg_ok, 1)
                        ch.link(V.tensor_tensor_scan(mx[s][:, ::-1], masks[s][:, 1, ::-1], lg[s][:, ::-1],
                                                     mx[1 - s][:, 0:1], ALU.add, ALU.max))
                        V.nop().then_inc(mx_ok, 1)
                        if more:
                            V.nop().then_inc(masks_free, 1)
                        if nxt is not None:
                            queries_spread(nxt)
                            edges_masked(nxt)

                    skewed(dve, ORDER, first, both, ch)

                @block.tensor
                def _(pe):
                    def rows_turned(i, s):
                        pe.wait_ge(x1_in[s], 16 * i + 16)
                        turn(b_dT, x1r[s]).then_inc(x1_turned, 1)
                        pe.wait_ge(xs_in[s], 16 * i + 16)
                        turn(b_sT, xs[s]).then_inc(s_turned, 1)

                    def priorities(i, s):
                        pe.wait_ge(masks_in[s], 32 * i + 32)
                        nc.tensor.matmul(b_p[:], pri[:], onehot[s][:], start=True, stop=True).then_inc(pri_ok, 1)

                    def by_type(bank, weights, parts, ok):
                        for t in range(len(parts)):
                            last = nc.tensor.matmul(bank[:], weights[:, t, :], parts[t][:], start=(t == 0),
                                                    stop=(t == len(parts) - 1))
                        last.then_inc(ok, 1)

                    def queries(free):
                        take(pe, x1_masked, 2)
                        if free:
                            pe.nop().then_inc(x1_free, 1)
                        by_type(b_q, wk, dT, q_ok)

                    def keys(free):
                        take(pe, s_masked, 2)
                        if free:
                            pe.nop().then_inc(xs_free, 1)
                        by_type(b_k, wk, sT, k_ok)

                    def first(s):
                        rows_turned(0, s)
                        priorities(0, s)
                        queries(True)
                        keys(True)

                    def both(i, o, s, nxt, more):
                        if nxt is not None:
                            rows_turned(i + o, nxt)
                        take(pe, k_masked, 3)
                        by_type(b_m, ra, kT, m_ok)
                        if nxt is not None:
                            priorities(i + o, nxt)
                            queries(more)
                        take(pe, prod_ok)
                        nc.tensor.matmul(b_l[:], head_ones[:], prod[:], start=True, stop=True).then_inc(l_ok, 1)
                        if nxt is not None:
                            keys(more)

                    skewed(pe, ORDER, first, both)

        with Phase(nc) as st:
            lr = two(sb, st, "s_lr", [P, 3, GE])
            masks = two(sb, st, "s_masks", [P, 2, GE], BF16)
            code = two(sb, st, "s_code", [P, 1, GE], BF16)
            x1r, hr, y, outr = [two(sb, st, n, [P, TG, D]) for n in ("s_x1r", "s_hr", "s_y", "s_outr")]
            mb, ex, es, nm = [two(sb, st, n, [P, GE]) for n in ("s_mb", "s_ex", "s_es", "s_nm")]
            hT = [[sb(st, f"s_hT{t}_{s}", [P, GE]) for t in range(NTYPES)] for s in range(2)]
            den = two(sb, st, "s_den", [P, TG, HEADS])
            stt = two(sb, st, "s_stt", [P, TG, 6])
            mv = two(sb, st, "s_mv", [P, TG, 2])
            sd, rr, bb = [two(sb, st, n, [P, TG]) for n in ("s_sd", "s_rr", "s_bb")]
            b_es, b_nm = two(pb, st, "s_bes"), two(pb, st, "s_bnm")
            b_h, b_a = two(pb, st, "s_bh"), two(pb, st, "s_ba")
            lr_in, masks_in, x1_in, x2_st = [two(sem, st, f"s_{n}") for n in ("lr_in", "masks_in", "x1_in", "x2_st")]
            (lr_free, x1_free, sub_ok, ex_ok, sums_ok, sums_turned, h_ok, h_turned, h_copied, h_masked, a_ok, var, std,
             affine, x2_ok) = [sem(st, f"s_{n}") for n in (
                "lr_free", "x1_free", "sub_ok", "ex_ok", "sums_ok", "sums_turned", "h_ok", "h_turned", "h_copied", "h_masked",
                "a_ok", "var", "std", "affine", "x2_ok")]
            with nc.Block() as block:
                @block.sync
                def _(sp):
                    for s in range(2):
                        sp.nop().then_inc(x2_st[s], 16)

                    def load_lr(b, s):
                        sp.dma_start(lr[s][:], lrm_of(b, s, 0, 3)).then_inc(lr_in[s], 16)
                        sp.dma_start(masks[s][:], seq_of(seq_rows, b, s, KEEP, NFIRST + 1)).then_inc(masks_in[s], 16)

                    def load_x1(b, s):
                        sp.dma_start(code[s][:], seq_of(seq_rows, b, s, NTD, NTD + 1)).then_inc(x1_in[s], 16)
                        sp.dma_start(x1r[s][:], rows_of(x1_rows, b, s)).then_inc(x1_in[s], 16)

                    for s in range(2):
                        load_lr(0, s)
                    for s in range(2):
                        load_x1(0, s)
                    for s in range(2):
                        take(sp, lr_free)
                        load_lr(1, s)

                    def body(i, more):
                        if more > 1:
                            for s in range(2):
                                take(sp, lr_free)
                                load_lr(i + 2, s)
                        if more:
                            for s in range(2):
                                take(sp, x1_free)
                                load_x1(i + 1, s)
                        for s in range(2):
                            take(sp, x2_ok)
                            sp.dma_start(rows_of(x2_rows, i, s), outr[s][:]).then_inc(x2_st[s], 16)

                    with sp.Fori(0, BODIES - 2) as i:
                        body(i, 2)
                    body(BODIES - 2, 1)
                    body(BODIES - 1, 0)
                    for s in range(2):
                        sp.wait_ge(x2_st[s], 16 * (BODIES + 1))

                @block.scalar
                def _(act):
                    def exponentials():
                        for s in range(2):
                            take(act, sub_ok)
                            nc.scalar.activation(ex[s][:], ex[s][:], ACT.Exp).then_inc(ex_ok, 1)

                    def body(i, more):
                        if more:
                            exponentials()
                        for s in range(2):
                            take(act, h_turned)
                            nc.scalar.activation(hT[s][0][:], b_h[s][:], ACT.Copy).then_inc(h_copied, 1)
                        for s in range(2):
                            take(act, var)
                            nc.scalar.activation(sd[s][:], mv[s][:, :, 1], ACT.Sqrt, bias=eps_col[:, EPS1:EPS1 + 1])\
                                .then_inc(std, 1)
                        for s in range(2):
                            act.wait_ge(x2_st[s], 16 * i + 16)
                            take(act, affine)
                            norm_rows(act, outr, y, rr, bb, s).then_inc(x2_ok, 1)

                    exponentials()
                    with act.Fori(0, BODIES - 1) as i:
                        body(i, True)
                    body(BODIES - 1, False)

                @block.vector
                def _(dve):
                    ch = Chain(dve, dve_done)
                    V = nc.vector
                    for t in (mb, es, nm):
                        last = V.memset(t[1][:], 0.0)
                    ch.link(last)
                    ch.close()

                    def differences(i, s):
                        dve.wait_ge(masks_in[s], 16 * i + 16)
                        dve.wait_ge(lr_in[s], 16 * i + 16)
                        ch.link(V.tensor_tensor_scan(mb[s][:], masks[s][:, 1, :], lr[s][:, 1, :],
                                                     mb[1 - s][:, GE - 1:GE], ALU.add, ALU.max))
                        V.tensor_tensor(ex[s][:], lr[s][:, 0, :], mb[s][:], ALU.subtract).then_inc(sub_ok, 1)

                    def sums(s, free):
                        take(dve, ex_ok)
                        V.tensor_tensor(lr[s][:, 2, :], lr[s][:, 2, :], ex[s][:], ALU.mult).then_inc(dve_done, 1)
                        ch.n += 1
                        V.tensor_tensor_scan(es[s][:], masks[s][:, 0, :], ex[s][:], es[1 - s][:, GE - 1:GE],
                                             ALU.mult, ALU.add)
                        dve.wait_ge(dve_done, ch.n)
                        ch.link(V.tensor_tensor_scan(nm[s][:], masks[s][:, 0, :], lr[s][:, 2, :],
                                                     nm[1 - s][:, GE - 1:GE], ALU.mult, ALU.add))
                        V.nop().then_inc(sums_ok, 1)
                        if free:
                            V.nop().then_inc(lr_free, 1)

                    def quotients(s):
                        take(dve, sums_turned)
                        ch.link(V.tensor_scalar(den[s][:], tiles(b_es[s][:])[:, :, ::HD], 1.0, None, ALU.max))
                        ch.link(V.reciprocal(den[s][:], den[s][:]))
                        V.tensor_tensor(hr[s][:].rearrange("p j (h r) -> p (j h) r", r=HD),
                                        b_nm[s][:].rearrange("p (k r) -> p k r", r=HD),
                                        den[s][:].rearrange("p j h -> p (j h)").unsqueeze(2)
                                        .to_broadcast([P, TG * HEADS, HD]), ALU.mult).then_inc(h_ok, 1)

                    def by_type(i, s):
                        dve.wait_ge(x1_in[s], 32 * i + 32)
                        take(dve, h_copied)
                        for t in range(1, NTYPES):
                            V.scalar_tensor_tensor(out=hT[s][t][:], in0=code[s][:, 0, :], scalar=float(t),
                                                   in1=b_h[s][:], op0=ALU.is_equal, op1=ALU.mult).then_inc(h_masked, 1)

                    def residual(s, free):
                        take(dve, a_ok)
                        ch.link(V.scalar_tensor_tensor(out=y[s][:], in0=tiles(b_a[s][:]), scalar=0.0, in1=x1r[s][:],
                                                       op0=ALU.max, op1=ALU.add))
                        if free:
                            V.nop().then_inc(x1_free, 1)
                        norm_stats(V, ch, y, stt, mv, s, var)

                    def norm(s):
                        take(dve, std)
                        ch.link(V.reciprocal(rr[s][:], sd[s][:]))
                        V.scalar_tensor_tensor(out=bb[s][:], in0=mv[s][:, :, 0], scalar=-1.0, in1=rr[s][:],
                                               op0=ALU.mult, op1=ALU.mult).then_inc(affine, 1)

                    def body(i, more):
                        if more:
                            for s in range(2):
                                differences(i + 1, s)
                        for s in range(2):
                            quotients(s)
                        for s in range(2):
                            by_type(i, s)
                            if more:
                                sums(s, more > 1)
                        for s in range(2):
                            residual(s, more)
                        for s in range(2):
                            norm(s)

                    for s in range(2):
                        differences(0, s)
                    for s in range(2):
                        sums(s, True)
                    ch.close()
                    with dve.Fori(0, BODIES - 2) as i:
                        body(i, 2)
                        ch.close()
                    body(BODIES - 2, 1)
                    body(BODIES - 1, 0)
                    ch.close()

                @block.tensor
                def _(pe):
                    def sums_turn(s):
                        take(pe, sums_ok)
                        turn(b_es[s], tiles(es[s][:]))
                        turn(b_nm[s], tiles(nm[s][:])).then_inc(sums_turned, 1)

                    def body(more):
                        for s in range(2):
                            take(pe, h_ok)
                            turn(b_h[s], hr[s]).then_inc(h_turned, 1)
                        for s in range(2):
                            take(pe, h_masked, 2)
                            for j in range(TG):
                                for t in range(NTYPES):
                                    last = nc.tensor.matmul(b_a[s][:, j * P:(j + 1) * P],
                                                            hT[s][t][:, j * P:(j + 1) * P], wa[:, t, :],
                                                            start=(t == 0), stop=(t == NTYPES - 1))
                            last.then_inc(a_ok, 1)
                            if more:
                                sums_turn(s)

                    for s in range(2):
                        sums_turn(s)
                    with pe.Fori(0, BODIES - 1) as i:
                        body(True)
                    body(False)

        with Phase(nc) as st:
            a0r, xs, x2r, y, outr = [two(sb, st, n, [P, TG, D]) for n in ("m_a0r", "m_xs", "m_x2r", "m_y", "m_outr")]
            aff = two(sb, st, "m_aff", [P, TG, 2])
            stage = two(sb, st, "m_stage", [P, TG], I32)
            keep = two(sb, st, "m_keep", [P, 1, GE], BF16)
            sums = two(sb, st, "m_sums", [P, GE])
            stt = two(sb, st, "m_stt", [P, TG, 6])
            mv = two(sb, st, "m_mv", [P, TG, 2])
            sd, rr, bb = [two(sb, st, n, [P, TG]) for n in ("m_sd", "m_rr", "m_bb")]
            b_s, b_r = two(pb, st, "m_bs"), two(pb, st, "m_br")
            a0_in, d_in, picked, x3_st = [two(sem, st, f"m_{n}") for n in ("a0_in", "d_in", "picked", "x3_st")]
            (aff_ok, x_ok, staged, a0_free, d_free2, turned, scanned, back, var, std, affine, x3_ok) = [
                sem(st, f"m_{n}") for n in ("aff_ok", "x_ok", "staged", "a0_free", "d_free", "turned", "scanned",
                                            "back", "var", "std", "affine", "x3_ok")]
            with nc.Block() as block:
                @block.sync
                def _(sp):
                    for s in range(2):
                        sp.nop().then_inc(x3_st[s], 16)

                    def load_a0(b, s):
                        sp.dma_start(a0r[s][:], rows_of(src_x1, b, s)).then_inc(a0_in[s], 16)

                    def load_rest(b, s):
                        sp.dma_start(x2r[s][:], rows_of(x2_rows, b, s)).then_inc(d_in[s], 16)
                        sp.dma_start(keep[s][:], seq_of(seq_rows, b, s, KEEP, KEEP + 1)).then_inc(d_in[s], 16)

                    for s in range(2):
                        load_a0(0, s)
                        load_rest(0, s)

                    def step(i, o, s, more):
                        if more:
                            take(sp, a0_free)
                            load_a0(i + 1, s)
                            take(sp, d_free2)
                            load_rest(i + 1, s)
                        take(sp, x3_ok)
                        sp.dma_start(rows_of(x3s_rows, i, s), outr[s][:]).then_inc(x3_st[s], 16)

                    bodies(sp, (0, 1), step)
                    for s in range(2):
                        sp.wait_ge(x3_st[s], 16 * (BODIES + 1))

                @block.gpsimd
                def _(gp):
                    bound = gp.to_reg(EP - 1)
                    with gp.Fori(0, BODIES) as i:
                        for s in range(2):
                            take(gp, staged)
                            take(gp, x_ok)
                            picks(gp, bound, x2_rows, xs, stage, picked, s)

                @block.scalar
                def _(act):
                    nc.scalar.preload_act_table(ACT.Sqrt)
                    for s in range(2):
                        local_rows(act, 0, s, a0_in, aff_ok, x_ok, xs, a0r, aff)

                    def step(i, o, s, more):
                        if more:
                            local_rows(act, i + 1, s, a0_in, aff_ok, x_ok, xs, a0r, aff)
                        take(act, var)
                        nc.scalar.activation(sd[s][:], mv[s][:, :, 1], ACT.Sqrt, bias=eps_col[:, EPS_M:EPS_M + 1])\
                            .then_inc(std, 1)
                        act.wait_ge(x3_st[s], 16 * i + 16)
                        take(act, affine)
                        norm_rows(act, outr, y, rr, bb, s).then_inc(x3_ok, 1)

                    bodies(act, (0, 1), step)

                @block.vector
                def _(dve):
                    ch = Chain(dve, dve_done)
                    V = nc.vector
                    ch.link(V.memset(sums[1][:], 0.0))
                    ch.close()
                    for s in range(2):
                        local_put(V, 0, aff, stage, 0, s, aff_ok, staged)

                    def step(i, o, s, more):
                        dve.wait_ge(d_in[s], 32 * i + 32)
                        take(dve, turned)
                        if more:
                            local_put(V, 0, aff, stage, i + 1, s, aff_ok, staged)
                            V.nop().then_inc(a0_free, 1)
                        ch.link(V.tensor_tensor_scan(sums[s][:], keep[s][:, 0, :], b_s[s][:], sums[1 - s][:, GE - 1:GE],
                                                     ALU.mult, ALU.add))
                        V.nop().then_inc(scanned, 1)
                        take(dve, back)
                        ch.link(V.tensor_tensor(y[s][:], tiles(b_r[s][:]), cols(c_third, i, s), ALU.mult))
                        ch.link(V.tensor_tensor(y[s][:], y[s][:], x2r[s][:], ALU.add))
                        V.nop().then_inc(d_free2, 1)
                        norm_stats(V, ch, y, stt, mv, s, var)
                        take(dve, std)
                        ch.link(V.reciprocal(rr[s][:], sd[s][:]))
                        ch.link(V.tensor_tensor(rr[s][:], rr[s][:],
                                                c_dinv[:, bass.ds(i * (2 * TG) + s * TG, TG)], ALU.mult))
                        V.scalar_tensor_tensor(out=bb[s][:], in0=mv[s][:, :, 0], scalar=-1.0, in1=rr[s][:],
                                               op0=ALU.mult, op1=ALU.mult).then_inc(affine, 1)

                    bodies(dve, (0, 1), step, ch)

                @block.tensor
                def _(pe):
                    def step(i, o, s, more):
                        pe.wait_ge(picked[s], 64 * i + 64)
                        turn(b_s[s], xs[s]).then_inc(turned, 1)
                        take(pe, scanned)
                        turn(b_r[s], tiles(sums[s][:])).then_inc(back, 1)

                    bodies(pe, (0, 1), step)

        with Phase(nc) as st:
            a0r, xs, x3r, h2l, h2s, zr = [two(sb, st, n, [P, TG, D]) for n in (
                "c_a0r", "c_xs", "c_x3r", "c_h2l", "c_h2s", "c_zr")]
            tmp = sb(st, "c_tmp", [P, TG, D])
            y, outr = [two(sb, st, n, [P, TG, D]) for n in ("c_y", "c_outr")]
            stage_out = two(sb, st, "c_stage_out", [P, TG], I32)
            stt = two(sb, st, "c_stt", [P, TG, 6])
            mv = two(sb, st, "c_mv", [P, TG, 2])
            sd, rr, bb = [two(sb, st, n, [P, TG]) for n in ("c_sd", "c_rr", "c_bb")]
            aff = two(sb, st, "c_aff", [P, TG, 2])
            stage = two(sb, st, "c_stage", [P, TG], I32)
            keep = two(sb, st, "c_keep", [P, 1, GE], BF16)
            dinv_b = two(sb, st, "c_dinv_b", [P, 1, GE])
            sums = two(sb, st, "c_sums", [P, GE])
            uT, xsT = two(sb, st, "c_uT", [P, GE]), two(sb, st, "c_xsT", [P, GE])
            hs, hd = two(sb, st, "c_hs", [P, GE]), two(sb, st, "c_hd", [P, GE])
            b_s, b_d = pb(st, "c_bs"), pb(st, "c_bd")
            b_hs, b_hd = two(pb, st, "c_bhs"), two(pb, st, "c_bhd")
            b_os, b_od = pb(st, "c_bos"), pb(st, "c_bod")
            a0_in, d_in, picked, h2l_st, h2s_st, z_st, sent = [two(sem, st, f"c_{n}") for n in (
                "a0_in", "d_in", "picked", "h2l_st", "h2s_st", "z_st", "sent")]
            var, std, affine, out_ok, y_ok = [sem(st, f"c_{n}") for n in ("var", "std", "affine", "out_ok", "y_ok")]
            (aff_ok, x_ok, staged, a0_free, d_free2, s_turned, s_copied, x3_turned, u_ok, hs_ok, hs_relu, hd_ok,
             hd_relu, os_ok, os_copied, od_ok, h2s_ok, z_ok) = [sem(st, f"c_{n}") for n in (
                "aff_ok", "x_ok", "staged", "a0_free", "d_free", "s_turned", "s_copied", "x3_turned", "u_ok", "hs_ok",
                "hs_relu", "hd_ok", "hd_relu", "os_ok", "os_copied", "od_ok", "h2s_ok", "z_ok")]
            with nc.Block() as block:
                @block.sync
                def _(sp):
                    for s in range(2):
                        for q in (h2l_st, h2s_st, z_st):
                            sp.nop().then_inc(q[s], 16)

                    def load_a0(b, s):
                        sp.dma_start(a0r[s][:], rows_of(src_x1, b, s)).then_inc(a0_in[s], 16)

                    def load_rest(b, s):
                        sp.dma_start(x3r[s][:], rows_of(x3s_rows, b, s)).then_inc(d_in[s], 16)
                        sp.dma_start(keep[s][:], seq_of(seq_rows, b, s, KEEP, KEEP + 1)).then_inc(d_in[s], 16)
                        sp.dma_start(dinv_b[s][:], seq_of(dinv_row, b, s, 0, 1)).then_inc(d_in[s], 16)

                    for s in range(2):
                        load_a0(0, s)
                        load_rest(0, s)

                    def first(s):
                        take(sp, a0_free)
                        load_a0(1, s)

                    def both(i, o, s, nxt, more):
                        if more:
                            take(sp, d_free2)
                            load_rest(i + 1, s)
                        if more > 1:
                            take(sp, a0_free)
                            load_a0(i + (1 + o), nxt)
                        take(sp, os_copied)
                        sp.dma_start(rows_of(h2_src, i, s), h2l[s][:]).then_inc(h2l_st[s], 16)
                        take(sp, h2s_ok)
                        sp.dma_start(rows_of(h2s_rows, i, s), h2s[s][:]).then_inc(h2s_st[s], 16)
                        take(sp, z_ok)
                        sp.dma_start(rows_of(z_rows, i, s), zr[s][:]).then_inc(z_st[s], 16)

                    skewed(sp, (0, 1), first, both, peel=2)
                    for s in range(2):
                        for q in (h2l_st, h2s_st, z_st):
                            sp.wait_ge(q[s], 16 * (BODIES + 1))

                @block.gpsimd
                def _(gp):
                    bound = gp.to_reg(EP - 1)
                    bound_out = gp.to_reg(N - 1)

                    def pick(s):
                        take(gp, staged)
                        take(gp, x_ok)
                        picks(gp, bound, x3s_rows, xs, stage, picked, s)

                    def first(s):
                        for n in (0, 1, s):
                            pick(n)

                    def both(i, o, s, nxt, more):
                        if more > 1:
                            pick(nxt)
                        take(gp, out_ok)
                        for j in range(TG):
                            gp.indirect_dma_start(out, bass.IndirectOffsetOnAxis(ap=stage_out[s][:, j:j + 1], axis=0),
                                                  outr[s][:, j, :], None, bounds_check=bound_out, oob_is_err=False)\
                                .then_inc(sent[s], 16)

                    skewed(gp, (0, 1), first, both, peel=2)
                    for s in range(2):
                        gp.wait_ge(sent[s], 64 * BODIES)

                @block.scalar
                def _(act):
                    nc.scalar.preload_act_table(ACT.Sqrt)
                    for s in range(2):
                        local_rows(act, 0, s, a0_in, aff_ok, x_ok, xs, a0r, aff)

                    def front(b, s, more):
                        take(act, s_turned)
                        nc.scalar.activation(xsT[s][:], b_s[:], ACT.Copy).then_inc(s_copied, 1)
                        if more:
                            local_rows(act, b + 1, s, a0_in, aff_ok, x_ok, xs, a0r, aff)

                    def both(i, o, s, nxt, more):
                        for half, ok, bank, relu in ((hs, hs_ok, b_hs, hs_relu), (hd, hd_ok, b_hd, hd_relu)):
                            for c in range(2):
                                take(act, ok)
                                nc.scalar.activation(half[c][:], bank[c][:], ACT.Relu, bias=b1s[:, c:c + 1])\
                                    .then_inc(relu, 1)
                        if nxt is not None:
                            front(i + o, nxt, more > 1)
                        act.wait_ge(h2l_st[s], 16 * i + 16)
                        take(act, y_ok)
                        nc.scalar.activation(h2l[s][:], tiles(b_os[:]), ACT.Copy).then_inc(os_copied, 1)
                        take(act, var)
                        nc.scalar.activation(sd[s][:], mv[s][:, :, 1], ACT.Sqrt, bias=eps_col[:, EPS1:EPS1 + 1])\
                            .then_inc(std, 1)
                        take(act, affine)
                        norm_rows(act, outr, y, rr, bb, s).then_inc(out_ok, 1)

                    skewed(act, (0, 1), lambda s: front(0, s, True), both, peel=2)

                @block.vector
                def _(dve):
                    ch = Chain(dve, dve_done)
                    V = nc.vector
                    ch.link(V.memset(sums[1][:], 0.0))
                    ch.close()
                    for s in range(2):
                        local_put(V, 1, aff, stage, 0, s, aff_ok, staged)

                    def front(b, s, more):
                        dve.wait_ge(d_in[s], 48 * b + 48)
                        take(dve, s_copied)
                        ch.link(V.tensor_tensor(y[s][:], xs[s][:], b2_all[:].unsqueeze(1).to_broadcast([P, TG, D]),
                                                ALU.add))
                        if more:
                            local_put(V, 1, aff, stage, b + 1, s, aff_ok, staged)
                            V.nop().then_inc(a0_free, 1)
                        ch.link(V.tensor_tensor_scan(sums[s][:], keep[s][:, 0, :], b_s[:], sums[1 - s][:, GE - 1:GE],
                                                     ALU.mult, ALU.add))
                        take(dve, x3_turned)
                        ch.link(V.tensor_tensor(uT[s][:], sums[s][:], b_d[:], ALU.add))
                        V.tensor_tensor(uT[s][:], uT[s][:], dinv_b[s][:, 0, :], ALU.mult).then_inc(u_ok, 1)

                    def both(i, o, s, nxt, more):
                        ch.link(V.tensor_tensor(tmp[:], x3r[s][:], cols(c_root, i, s), ALU.mult))
                        if more:
                            V.nop().then_inc(d_free2, 1)
                        ch.link(V.tensor_tensor(tmp[:], tmp[:], b2_all[:].unsqueeze(1).to_broadcast([P, TG, D]), ALU.add))
                        if nxt is not None:
                            front(i + o, nxt, more > 1)
                        take(dve, os_ok)
                        ch.link(V.tensor_tensor(y[s][:], tiles(b_os[:]), y[s][:], ALU.add))
                        V.nop().then_inc(y_ok, 1)
                        norm_stats(V, ch, y, stt, mv, s, var)
                        dve.wait_ge(h2s_st[s], 16 * i + 16)
                        take(dve, od_ok)
                        ch.link(V.tensor_tensor(h2s[s][:], tiles(b_od[:]), cols(c_dinv, i, s), ALU.mult))
                        V.nop().then_inc(h2s_ok, 1)
                        dve.wait_ge(z_st[s], 16 * i + 16)
                        ch.link(V.tensor_tensor(zr[s][:], h2s[s][:], cols(c_dinv, i, s), ALU.mult))
                        V.tensor_tensor(zr[s][:], zr[s][:], tmp[:], ALU.add).then_inc(z_ok, 1)
                        take(dve, std)
                        ch.link(V.reciprocal(rr[s][:], sd[s][:]))
                        if not isinstance(i, int) or i:
                            dve.wait_ge(sent[s], 64 * i)
                        V.tensor_copy(stage_out[s][:], i_srcout[:, bass.ds(i * (2 * TG) + s * TG, TG)])
                        V.scalar_tensor_tensor(out=bb[s][:], in0=mv[s][:, :, 0], scalar=-1.0, in1=rr[s][:],
                                               op0=ALU.mult, op1=ALU.mult).then_inc(affine, 1)

                    skewed(dve, (0, 1), lambda s: front(0, s, True), both, ch, peel=2, head=1)

                @block.tensor
                def _(pe):
                    def first(banks, t, ok):
                        for c in range(2):
                            nc.tensor.matmul(banks[c][:], w1s[:, c * D:(c + 1) * D], t[:], start=True, stop=True)\
                                .then_inc(ok, 1)

                    def second(bank, h):
                        for j in range(TG):
                            for c in range(2):
                                last = nc.tensor.matmul(bank[:, j * P:(j + 1) * P], h[c][:, j * P:(j + 1) * P],
                                                        w2s[:, c, :], start=(c == 0), stop=(c == 1))
                        return last

                    def rows_turned(b, s):
                        pe.wait_ge(d_in[s], 48 * b + 48)
                        turn(b_d, x3r[s]).then_inc(x3_turned, 1)
                        pe.wait_ge(picked[s], 64 * b + 64)
                        turn(b_s, xs[s]).then_inc(s_turned, 1)

                    def both(i, o, s, nxt, more):
                        take(pe, u_ok)
                        first(b_hs, xsT[s], hs_ok)
                        first(b_hd, uT[s], hd_ok)
                        if nxt is not None:
                            rows_turned(i + o, nxt)
                        take(pe, hs_relu, 2)
                        second(b_os, hs).then_inc(os_ok, 1)
                        take(pe, hd_relu, 2)
                        second(b_od, hd).then_inc(od_ok, 1)

                    skewed(pe, (0, 1), lambda s: rows_turned(0, s), both)

        with Phase(nc) as st:
            xs, zr, y, outr = [two(sb, st, n, [P, TG, D]) for n in ("f_xs", "f_zr", "f_y", "f_outr")]
            stage = two(sb, st, "f_stage", [P, TG], I32)
            stage_out = two(sb, st, "f_stage_out", [P, TG], I32)
            keep = two(sb, st, "f_keep", [P, 1, GE], BF16)
            sums = two(sb, st, "f_sums", [P, GE])
            stt = two(sb, st, "f_stt", [P, TG, 6])
            mv = two(sb, st, "f_mv", [P, TG, 2])
            sd, rr, bb = [two(sb, st, n, [P, TG]) for n in ("f_sd", "f_rr", "f_bb")]
            b_s, b_r = two(pb, st, "f_bs"), two(pb, st, "f_br")
            h2_in, d_in, picked, sent = [two(sem, st, f"f_{n}") for n in ("h2_in", "d_in", "picked", "sent")]
            (staged, xs_free, d_free2, turned, scanned, back, var, std, affine, out_ok) = [
                sem(st, f"f_{n}") for n in ("staged", "xs_free", "d_free", "turned", "scanned", "back", "var", "std",
                                            "affine", "out_ok")]
            with nc.Block() as block:
                @block.sync
                def _(sp):
                    def load_h2(b, s):
                        sp.dma_start(xs[s][:], rows_of(h2_src, b, s)).then_inc(h2_in[s], 16)

                    def load_rest(b, s):
                        sp.dma_start(zr[s][:], rows_of(z_rows, b, s)).then_inc(d_in[s], 16)
                        sp.dma_start(keep[s][:], seq_of(seq_rows, b, s, KEEP, KEEP + 1)).then_inc(d_in[s], 16)

                    for s in range(2):
                        load_h2(0, s)
                        load_rest(0, s)
                    with sp.Fori(0, BODIES - 1) as i:
                        for s in range(2):
                            take(sp, xs_free)
                            load_h2(i + 1, s)
                            take(sp, d_free2)
                            load_rest(i + 1, s)

                @block.gpsimd
                def _(gp):
                    bound = gp.to_reg(EP - 1)
                    bound_out = gp.to_reg(N - 1)

                    def pick(i, s):
                        gp.wait_ge(h2_in[s], 16 * i + 16)
                        take(gp, staged)
                        picks(gp, bound, h2s_rows, xs, stage, picked, s)

                    for s in range(2):
                        pick(0, s)

                    def step(i, o, s, more):
                        take(gp, out_ok)
                        for j in range(TG):
                            gp.indirect_dma_start(out, bass.IndirectOffsetOnAxis(ap=stage_out[s][:, j:j + 1], axis=0),
                                                  outr[s][:, j, :], None, bounds_check=bound_out, oob_is_err=False)\
                                .then_inc(sent[s], 16)
                        if more:
                            pick(i + 1, s)

                    bodies(gp, (0, 1), step)
                    for s in range(2):
                        gp.wait_ge(sent[s], 64 * BODIES)

                @block.scalar
                def _(act):
                    nc.scalar.preload_act_table(ACT.Sqrt)
                    with act.Fori(0, BODIES) as i:
                        for s in range(2):
                            take(act, var)
                            nc.scalar.activation(sd[s][:], mv[s][:, :, 1], ACT.Sqrt, bias=eps_col[:, EPS1:EPS1 + 1])\
                                .then_inc(std, 1)
                            take(act, affine)
                            norm_rows(act, outr, y, rr, bb, s).then_inc(out_ok, 1)

                @block.vector
                def _(dve):
                    ch = Chain(dve, dve_done)
                    V = nc.vector
                    ch.link(V.memset(sums[1][:], 0.0))
                    ch.close()
                    for s in range(2):
                        local_put(V, None, None, stage, 0, s, None, staged)

                    def step(i, o, s, more):
                        dve.wait_ge(d_in[s], 32 * i + 32)
                        take(dve, turned)
                        if more:
                            local_put(V, None, None, stage, i + 1, s, None, staged)
                            V.nop().then_inc(xs_free, 1)
                        ch.link(V.tensor_tensor_scan(sums[s][:], keep[s][:, 0, :], b_s[s][:], sums[1 - s][:, GE - 1:GE],
                                                     ALU.mult, ALU.add))
                        V.nop().then_inc(scanned, 1)
                        take(dve, back)
                        ch.link(V.tensor_tensor(y[s][:], tiles(b_r[s][:]), cols(c_dinv, i, s), ALU.mult))
                        ch.link(V.tensor_tensor(y[s][:], y[s][:], zr[s][:], ALU.add))
                        V.nop().then_inc(d_free2, 1)
                        norm_stats(V, ch, y, stt, mv, s, var)
                        take(dve, std)
                        ch.link(V.reciprocal(rr[s][:], sd[s][:]))
                        if not isinstance(i, int) or i:
                            dve.wait_ge(sent[s], 64 * i)
                        V.tensor_copy(stage_out[s][:], i_out[:, bass.ds(i * (2 * TG) + s * TG, TG)])
                        V.scalar_tensor_tensor(out=bb[s][:], in0=mv[s][:, :, 0], scalar=-1.0, in1=rr[s][:],
                                               op0=ALU.mult, op1=ALU.mult).then_inc(affine, 1)

                    for s in range(2):
                        step(0, s, s, True)
                    ch.close()
                    with dve.Fori(1, BODIES - 1) as i:
                        for s in range(2):
                            step(i, s, s, True)
                        ch.close()
                    for s in range(2):
                        step(BODIES - 1, s, s, False)
                    ch.close()

                @block.tensor
                def _(pe):
                    def step(i, o, s, more):
                        pe.wait_ge(picked[s], 64 * i + 64)
                        turn(b_s[s], xs[s]).then_inc(turned, 1)
                        take(pe, scanned)
                        turn(b_r[s], tiles(sums[s][:])).then_inc(back, 1)

                    bodies(pe, (0, 1), step)


_INS = ["x", "src", "dst", "edge_type_4", "edge_weight", "node_type_3", "L1_gnn_W_kqv", "L1_gnn_W_a",
        "L1_gnn_rel_pri", "L1_gnn_rel_att", "L3_gnn_W1", "L3_gnn_b1", "L3_gnn_W2", "L3_gnn_b2"]


def kernel(**inputs):
    import numpy as _np
    import concourse.bacc as _bacc
    from concourse.bass_utils import run_bass_kernel_spmd as _run

    nc = _bacc.Bacc("TRN2", target_bir_lowering=False, num_devices=1)
    arrays, args = {}, []
    for name in _INS:
        a = _np.ascontiguousarray(inputs[name])
        arrays[f"in_{name}"] = a
        args.append(nc.dram_tensor(f"in_{name}", a.shape, mybir.dt.from_np(a.dtype), kind="ExternalInput").ap())
    x = inputs["x"]
    args.append(nc.dram_tensor("out_0", x.shape, F32, kind="ExternalOutput").ap())
    gnn_kernel(nc, *args)
    r = _run(nc, [arrays], core_ids=[0])
    return r.results[0]["out_0"]
```

```python
import concourse.bass as bass
from concourse import mybir
from contextlib import ExitStack

ALU = mybir.AluOpType
ACT = mybir.ActivationFunctionType
F32 = mybir.dt.float32
BF16 = mybir.dt.bfloat16
I32 = mybir.dt.int32

P = 128
D = 128
TG = 4
GE = TG * P
BODY = 2 * GE
HEADS, HD = 4, 32
EPS = 1e-5
BIG = 1e30
FAR = 1 << 20


class Phase(ExitStack):

    def __init__(self, nc):
        super().__init__()
        self.nc, self.sems = nc, []

    def __exit__(self, *problem):
        if self.sems and problem[0] is None:
            self.nc.clear_and_free_semaphores(self.sems)
            self.nc.all_engine_barrier()
        return super().__exit__(*problem)


class Chain:

    def __init__(self, eng, sem):
        self.eng, self.sem, self.n = eng, sem, 0

    def link(self, ins):
        self.n += 1
        ins.then_inc(self.sem, 1)
        self.eng.wait_ge(self.sem, self.n)

    def mark(self, ins):
        self.n += 1
        ins.then_inc(self.sem, 1)
        return self.n

    def until(self, mark):
        self.eng.wait_ge(self.sem, mark)

    def close(self):
        if self.n:
            self.eng.sem_inc(self.sem, -self.n)
        self.n = 0


def take(eng, sem, n=1):
    eng.wait_ge(sem, n)
    eng.sem_inc(sem, -n)


def gnn_kernel(nc, x, src, dst, etype, weight, ntype, w_kqv, w_a, rel_pri, rel_att, w1, b1, w2, b2, out):
    N = x.shape[0]
    E = src.shape[0]
    NTYPES, ETYPES = w_kqv.shape[0], rel_att.shape[1]
    BODIES = -(-E // BODY)
    EP = BODIES * BODY
    NT = EP // P
    HALF = NT // 2
    NONE = EP
    assert D == P and NT % 2 == 0 and HALF <= P and NTYPES == 3 and ETYPES == 4
    NGROUPS = -(-N // GE)
    NODE_P = 125
    assert N % NODE_P == 0

    main = ExitStack()
    with main:
        def sb(stack, name, shape, dt=F32):
            return stack.enter_context(nc.sbuf_tensor(name, shape, dt))

        def pb(stack, name, shape=(P, GE), dt=F32):
            return stack.enter_context(nc.psum_tensor(name, list(shape), dt))

        def sem(stack, name):
            handle = nc.alloc_semaphore(name=name)
            if stack is not main:
                stack.sems.append(handle)
            return handle

        def two(make, stack, name, *a):
            return [make(stack, f"{name}{s}", *a) for s in range(2)]

        def dram(name, shape, dt=F32):
            return nc.dram_tensor(name, shape, dt, kind="Internal").ap()

        node_table = dram("node_table", (N, 4), I32)
        rec_low = dram("rec_low", (EP, 4), I32)
        rec_src = dram("rec_src", (EP + 2, 4), I32)
        keep_src = dram("keep_src", (1, EP), BF16)
        edge_dst = dram("edge_dst", (EP + 2,), I32)
        seq_rows = dram("seq_rows", (7, EP), BF16)
        onehot_rows = dram("onehot_rows", (ETYPES, EP))
        dinv_row = dram("dinv_row", (1, EP))
        src_x1 = dram("src_x1", (EP, D))
        x1_nodes = dram("x1_nodes", (EP, D))
        e1_rows = dram("e1_rows", (EP + 1, D))
        e2_rows = dram("e2_rows", (EP + 1, D))
        x1_rows = dram("x1_rows", (EP, D))
        x2_rows = dram("x2_rows", (EP, D))
        x3s_rows = dram("x3s_rows", (EP, D))
        lrm = dram("lrm", (EP // GE, P, 3, GE))
        h2_src = dram("h2_src", (EP, D))
        h2s_rows = dram("h2s_rows", (EP, D))
        z_rows = dram("z_rows", (EP, D))
        KEEP, NFIRST, NOTLAST, NLAST, ET, NTS, NTD = range(7)

        def rows_of(table, i, s):
            v = table[0:EP, :].rearrange("(b s j p) f -> b s p j f", s=2, j=TG, p=P)
            return v[bass.ds(i, 1), s].rearrange("o p j f -> (o p) j f")

        def seq_of(table, i, s, a, b):
            return table[a:b, bass.ds(i * BODY + s * GE, GE)].partition_broadcast(P)

        def lrm_of(i, s, a, b):
            v = lrm.rearrange("(b s) p k e -> b s p k e", s=2)
            return v[bass.ds(i, 1), s, :, a:b].rearrange("o p k e -> (o p) k e")

        ident = sb(main, "ident", [P, P])
        head_ones = sb(main, "head_ones", [P, P])
        wk = sb(main, "wk", [P, NTYPES, D])
        wa = sb(main, "wa", [P, NTYPES, D])
        ra = sb(main, "ra", [P, ETYPES, D])
        pri = sb(main, "pri", [ETYPES, D])
        w1s = sb(main, "w1s", [P, 2 * D])
        w2s = sb(main, "w2s", [P, 2, D])
        b1s = sb(main, "b1s", [P, 2])
        b2_all = sb(main, "b2_all", [P, D])
        b2_parts = sb(main, "b2_parts", [3, GE], BF16)
        ones3 = sb(main, "ones3", [3, P], BF16)
        eps_col = sb(main, "eps_col", [P, 7])
        EPS1, EPS16, EPS_SQ, EPS_CB, EPS_1, EPS_M, ONE = range(7)
        i_src = sb(main, "i_src", [P, NT + 2 * TG], I32)
        i_dst = sb(main, "i_dst", [P, NT + 2 * TG], I32)
        i_out = sb(main, "i_out", [P, NT + 2 * TG], I32)
        i_pick = sb(main, "i_pick", [P, NT + 2 * TG], I32)
        i_node1 = sb(main, "i_node1", [P, NT + 2 * TG], I32)
        i_dst1 = sb(main, "i_dst1", [P, NT + 2 * TG], I32)
        i_srcout = sb(main, "i_srcout", [P, NT + 2 * TG], I32)
        entry_dst = sb(main, "entry_dst", [P, NT + 2 * TG, 1], I32)
        k_src = sb(main, "k_src", [P, NT + 2 * TG], I32)
        k_out = sb(main, "k_out", [P, NT + 2 * TG], I32)
        k_dst = sb(main, "k_dst", [P, NT + 2 * TG], I32)
        k_pick = sb(main, "k_pick", [P, NT + 2 * TG], I32)
        k_w = sb(main, "k_w", [P, NT])
        entry_src = sb(main, "entry_src", [P, NT + 2 * TG, 2], I32)
        c_last = sb(main, "c_last", [P, NT])
        c_third = sb(main, "c_third", [P, NT])
        c_dinv = sb(main, "c_dinv", [P, NT])
        c_root = sb(main, "c_root", [P, NT])
        c_nts = sb(main, "c_nts", [P, NT])
        c_ntd = sb(main, "c_ntd", [P, NT])
        src_stats = sb(main, "src_stats", [P, NT, 6])
        local = [sb(main, f"local{n}", [P, NT, 2]) for n in range(2)]

        dx = two(sb, main, "dx", [P, TG, D])
        dn = two(sb, main, "dn", [P, TG, D])
        dxT = two(sb, main, "dxT", [P, GE])
        dh = two(sb, main, "dh", [P, 2, GE])
        dy = two(sb, main, "dy", [P, TG, D])
        dst1 = two(sb, main, "dst1", [P, TG, 6])
        dst2 = two(sb, main, "dst2", [P, TG, 6])
        dmv1 = two(sb, main, "dmv1", [P, TG, 2])
        dmv2 = two(sb, main, "dmv2", [P, TG, 2])
        dsd1 = two(sb, main, "dsd1", [P, TG])
        dsd2 = two(sb, main, "dsd2", [P, TG])
        dr1 = two(sb, main, "dr1", [P, TG])
        dr2 = two(sb, main, "dr2", [P, TG])
        db1 = two(sb, main, "db1", [P, TG])
        db2 = two(sb, main, "db2", [P, TG])
        d_loaded = two(sem, main, "d_loaded")
        d_stored = two(sem, main, "d_stored")
        (d_var1, d_std1, d_affine1, d_normed, d_free, d_turned, d_copied, d_hidden, d_relu, d_summed, d_taken,
         d_var2, d_std2, d_out) = [sem(main, f"d_{n}") for n in (
            "var1", "std1", "affine1", "normed", "free", "turned", "copied", "hidden", "relu", "summed",
            "taken", "var2", "std2", "out")]
        dve_done = sem(main, "dve_done")

        def node_rows(table, k):
            start = min(k * GE, N - GE) if isinstance(k, int) else k * GE
            v = table[bass.ds(start, GE), :] if not isinstance(start, int) else table[start:start + GE, :]
            return v.rearrange("(p j) f -> p j f", j=TG)

        def d_load(sp, k, s):
            take(sp, d_free)
            sp.dma_start(dx[s][:], node_rows(x, k)).then_inc(d_loaded[s], 16)

        def d_store(sp, k, s):
            take(sp, d_out)
            sp.dma_start(node_rows(out, k), dy[s][:]).then_inc(d_stored[s], 16)

        def d_stats1(dve, ch, s, n):
            dve.wait_ge(d_loaded[s], 16 * n + 16)
            for j in range(TG):
                last = nc.vector.bn_stats(dst1[s][:, j, :], dx[s][:, j, :])
            ch.link(last)
            for j in range(TG):
                last = nc.vector.bn_aggr(dmv1[s][:, j, :], dst1[s][:, j, :])
            last.then_inc(d_var1, 1)

        def d_affine1_of(dve, ch, s):
            take(dve, d_std1)
            ch.link(nc.vector.reciprocal(dr1[s][:], dsd1[s][:]))
            nc.vector.scalar_tensor_tensor(out=db1[s][:], in0=dmv1[s][:, :, 0], scalar=-1.0, in1=dr1[s][:],
                                           op0=ALU.mult, op1=ALU.mult).then_inc(d_affine1, 1)

        def dense_dve_a(dve, ch, s, n, more=2):
            if more > 1:
                dve.wait_ge(d_loaded[s], 16 * (n + 1) + 16)
                for j in range(TG):
                    last = nc.vector.bn_stats(dst1[s][:, j, :], dx[s][:, j, :])
                stats = ch.mark(last)
            take(dve, d_summed)
            dve.wait_ge(d_stored[s], 16 * n + 16)
            added = ch.mark(nc.vector.tensor_tensor(dy[s][:], ps_do[:].rearrange("p (j f) -> p j f", j=TG),
                                                    dn[s][:], ALU.add))
            if more > 1:
                ch.until(stats)
                for j in range(TG):
                    last = nc.vector.bn_aggr(dmv1[s][:, j, :], dst1[s][:, j, :])
                last.then_inc(d_var1, 1)
            ch.until(added)
            nc.vector.nop().then_inc(d_taken, 1)
            for j in range(TG):
                last = nc.vector.bn_stats(dst2[s][:, j, :], dy[s][:, j, :])
            return ch.mark(last)

        def dense_dve_m(dve, ch, s, stats):
            ch.until(stats)
            for j in range(TG):
                last = nc.vector.bn_aggr(dmv2[s][:, j, :], dst2[s][:, j, :])
            last.then_inc(d_var2, 1)

        def dense_dve_b(dve, ch, s, more=2):
            if more > 1:
                take(dve, d_std1)
                first = ch.mark(nc.vector.reciprocal(dr1[s][:], dsd1[s][:]))
            take(dve, d_std2)
            second = ch.mark(nc.vector.reciprocal(dr2[s][:], dsd2[s][:]))
            if more > 1:
                ch.until(first)
                nc.vector.scalar_tensor_tensor(out=db1[s][:], in0=dmv1[s][:, :, 0], scalar=-1.0, in1=dr1[s][:],
                                               op0=ALU.mult, op1=ALU.mult).then_inc(d_affine1, 1)
            ch.until(second)
            ch.link(nc.vector.scalar_tensor_tensor(out=db2[s][:], in0=dmv2[s][:, :, 0], scalar=-1.0, in1=dr2[s][:],
                                                   op0=ALU.mult, op1=ALU.mult))
            for j in range(TG):
                last = nc.vector.tensor_scalar(dy[s][:, j, :], dy[s][:, j, :], dr2[s][:, j:j + 1],
                                               db2[s][:, j:j + 1], ALU.mult, ALU.add)
            last.then_inc(d_out, 1)

        def dense_start(dve, ch):
            nc.vector.nop().then_inc(d_taken, 1)
            for s in range(2):
                d_stats1(dve, ch, s, 0)
            for s in range(2):
                d_affine1_of(dve, ch, s)

        def groups_behind(k0, i, s):
            return 2 if not isinstance(i, int) else min(2, NGROUPS - 1 - (k0 + 2 * i + s))

        def d_root1(act, s):
            take(act, d_var1)
            nc.scalar.activation(dsd1[s][:], dmv1[s][:, :, 1], ACT.Sqrt, bias=eps_col[:, EPS_CB:EPS_CB + 1],
                                 scale=C3).then_inc(d_std1, 1)

        def d_root2(act, s):
            take(act, d_var2)
            nc.scalar.activation(dsd2[s][:], dmv2[s][:, :, 1], ACT.Sqrt, bias=eps_col[:, EPS1:EPS1 + 1])\
                .then_inc(d_std2, 1)

        def d_norm1(act, s):
            take(act, d_affine1)
            for j in range(TG):
                last = nc.scalar.activation(dn[s][:, j, :], dx[s][:, j, :], ACT.Identity, bias=db1[s][:, j:j + 1],
                                            scale=dr1[s][:, j:j + 1])
            last.then_inc(d_normed, 1)

        def d_copy(act, s):
            take(act, d_turned)
            nc.scalar.activation(dxT[s][:], ps_dt[:], ACT.Copy).then_inc(d_copied, 1)

        def d_hid(act, s):
            for c in range(2):
                take(act, d_hidden)
                nc.scalar.activation(dh[s][:, c, :], ps_dh[c][:], ACT.Relu, bias=b1s[:, c:c + 1])\
                    .then_inc(d_relu, 1)

        def d_turn(pe, s):
            take(pe, d_normed)
            nc.tensor.nop().then_inc(d_free, 1)
            for j in range(TG):
                last = nc.tensor.transpose(ps_dt[:, j * P:(j + 1) * P], dn[s][:, j, :], ident[:])
            last.then_inc(d_turned, 1)

        def d_first(pe, s):
            take(pe, d_copied)
            for c in range(2):
                nc.tensor.matmul(ps_dh[c][:], w1s[:, c * D:(c + 1) * D], dxT[s][:], start=True, stop=True)\
                    .then_inc(d_hidden, 1)

        def d_second(pe, s):
            take(pe, d_relu, 2)
            take(pe, d_taken)
            nc.tensor.matmul(ps_do[:], ones3[:], b2_parts[:], start=True, stop=False, skip_group_check=True)
            for j in range(TG):
                for c in range(2):
                    last = nc.tensor.matmul(ps_do[:, j * P:(j + 1) * P], dh[s][:, c, j * P:(j + 1) * P],
                                            w2s[:, c, :], start=False, stop=(j == TG - 1 and c == 1),
                                            skip_group_check=True)
            last.then_inc(d_summed, 1)

        E1 = EPS / 1.5625
        CS = 1 + EPS / 2.25
        ES = EPS * EPS / 2.25
        C3 = (2.25 * 1.5625 + EPS * 1.5625 * (1 + EPS)) / (2.25 * 1.5625)
        E3 = EPS ** 3 / (2.25 * 1.5625)

        LOW_BITS = 9
        BINS = 1 << LOW_BITS
        HIGH_BINS = (N >> LOW_BITS) + 1

        def radix_phase(tag, fields, key, bins, load, target, target_row):
            first_pass = fields is not None
            with Phase(nc) as st:
                rec = sb(st, f"{tag}_rec", [P, NT + 2 * TG, 4], I32)
                raw = sb(st, f"{tag}_raw", [P, 4, NT], I32)
                digit_i = sb(st, f"{tag}_digit_i", [P, NT + 2 * TG], I32)
                digit = sb(st, f"{tag}_digit", [P, NT + 2 * TG])
                number_i = sb(st, f"{tag}_number_i", [P, bins], I32)
                number = sb(st, f"{tag}_number", [P, bins])
                count = two(sb, st, f"{tag}_count", [P, bins])
                before = two(sb, st, f"{tag}_before", [P, bins])
                earlier = sb(st, f"{tag}_earlier", [P, NT + 2 * TG])
                same = sb(st, f"{tag}_same", [P, NT // TG + 2])
                total = sb(st, f"{tag}_total", [P, bins])
                hit = two(sb, st, f"{tag}_hit", [P, bins])
                zeros = sb(st, f"{tag}_zeros", [P, bins])
                lower = sb(st, f"{tag}_lower", [P, P])
                ones = sb(st, f"{tag}_ones", [P, P])
                place = two(sb, st, f"{tag}_place", [P, TG])
                stage = two(sb, st, f"{tag}_stage", [P, TG], I32)
                moved = two(sb, st, f"{tag}_moved", [P, TG, 4], I32)
                ps_lower, ps_total = pb(st, f"{tag}_pslower"), pb(st, f"{tag}_pstotal")
                loaded, ready, cleared, triangle, counted, summed, staged = [sem(st, f"{tag}_{n}") for n in (
                    "loaded", "ready", "cleared", "triangle", "counted", "summed", "staged")]
                sent = two(sem, st, f"{tag}_sent")
                with nc.Block() as block:
                    @block.gpsimd
                    def _(gp):
                        nc.gpsimd.memset(rec[:], 0)
                        nc.gpsimd.memset(raw[:], 0).then_inc(ready, 1)
                        gp.wait_ge(ready, 1)
                        nc.gpsimd.memset(raw[96:P, key, :], N).then_inc(ready, 1)
                        gp.wait_ge(ready, 2)
                        nc.gpsimd.iota(number_i[:], pattern=[[1, bins]], base=0, channel_multiplier=0)
                        nc.gpsimd.memset(zeros[:], 0.0)
                        nc.gpsimd.memset(count[0][:], 0.0)
                        nc.gpsimd.memset(count[1][:], 0.0)
                        nc.gpsimd.memset(earlier[:], 0.0)
                        nc.gpsimd.memset(ones[:], 1.0)
                        nc.gpsimd.memset(lower[:], 1.0).then_inc(cleared, 1)
                        gp.wait_ge(cleared, 1)
                        nc.gpsimd.affine_select(out=lower[:], in_=lower[:], compare_op=ALU.is_gt, fill=0.0,
                                                base=0, pattern=[[1, P]], channel_multiplier=-1).then_inc(triangle, 1)
                        if first_pass and len(fields) == 3:
                            nc.gpsimd.iota(rec[:, 0:NT, 3], pattern=[[1, NT]], base=0, channel_multiplier=NT)\
                                .then_inc(triangle, 1)

                    @block.sync
                    def _(sp):
                        sp.wait_ge(ready, 2)
                        if first_pass:
                            for n, a in enumerate(fields):
                                sp.dma_start(raw[0:E // NT, n, :], a.rearrange("(p t) -> p t", t=NT))\
                                    .then_inc(loaded, 16)
                        else:
                            sp.dma_start(rec[:, 0:NT, :], load.rearrange("(p t) k -> p t k", p=P)).then_inc(loaded, 16)

                    @block.vector
                    def _(dve):
                        ch = Chain(dve, dve_done)
                        V = nc.vector
                        dve.wait_ge(loaded, 16 * len(fields) if first_pass else 16)
                        if first_pass:
                            dve.wait_ge(triangle, 5 - len(fields))
                            for n in range(len(fields)):
                                last = V.tensor_copy(rec[:, 0:NT, n], raw[:, n, :])
                            ch.link(last)
                        else:
                            dve.wait_ge(triangle, 1)
                        if first_pass:
                            ch.link(V.tensor_scalar(digit_i[:], rec[:, :, key], bins - 1, None, ALU.bitwise_and))
                        else:
                            ch.link(V.tensor_scalar(digit_i[:], rec[:, :, key], LOW_BITS, None, ALU.logical_shift_right))
                        V.tensor_copy(digit[:], digit_i[:])
                        ch.link(V.tensor_copy(number[:], number_i[:]))
                        ch.close()
                        with dve.Fori(0, BODIES) as i:
                            for j in range(2 * TG):
                                t = i * (2 * TG) + j
                                if j >= 2:
                                    dve.wait_ge(dve_done, ch.n - 1)
                                V.scalar_tensor_tensor(out=count[j % 2][:], in0=number[:],
                                                       scalar=digit[:, bass.ds(t, 1)], in1=count[j % 2][:],
                                                       op0=ALU.is_equal, op1=ALU.add).then_inc(dve_done, 1)
                                ch.n += 1
                            dve.wait_ge(dve_done, ch.n)
                            ch.close()
                        ch.link(V.tensor_tensor(count[0][:], count[0][:], count[1][:], ALU.add))
                        V.nop().then_inc(counted, 1)
                        groups = digit[:].rearrange("p (g j) -> p g j", j=TG)
                        earliers = earlier[:].rearrange("p (g j) -> p g j", j=TG)
                        for j in range(1, TG):
                            for j0 in range(j):
                                ch.link(V.tensor_tensor(same[:], groups[:, :, j], groups[:, :, j0], ALU.is_equal))
                                ch.link(V.tensor_tensor(earliers[:, :, j], earliers[:, :, j], same[:], ALU.add))
                        take(dve, summed)
                        ch.link(V.tensor_copy(total[:], ps_total[:, 0:bins]))
                        ch.link(V.tensor_tensor_scan(before[0][:], zeros[:], total[:], 0.0, ALU.add, ALU.add))
                        ch.link(V.tensor_tensor(before[0][:], before[0][:], total[:], ALU.subtract))
                        ch.link(V.tensor_tensor(before[0][:], ps_lower[:, 0:bins], before[0][:], ALU.add))
                        ch.close()

                    @block.tensor
                    def _(pe):
                        pe.wait_ge(triangle, 1)
                        take(pe, counted)
                        nc.tensor.matmul(ps_lower[:, 0:bins], lower[:], count[0][:], start=True, stop=True)
                        nc.tensor.matmul(ps_total[:, 0:bins], ones[:], count[0][:], start=True, stop=True).then_inc(summed, 1)

                with nc.Block() as block:
                    @block.gpsimd
                    def _(gp):
                        bound = gp.to_reg(EP - 1 + target_row)
                        with gp.Fori(0, BODIES) as i:
                            for s in range(2):
                                take(gp, staged)
                                for j in range(TG):
                                    gp.indirect_dma_start(
                                        target, bass.IndirectOffsetOnAxis(ap=stage[s][:, j:j + 1], axis=0),
                                        moved[s][:, j, :], None, bounds_check=bound, oob_is_err=False)\
                                        .then_inc(sent[s], 16)

                    @block.vector
                    def _(dve):
                        ch = Chain(dve, dve_done)
                        V = nc.vector

                        def put(s, tile):
                            for j in range(TG):
                                d = digit[:, bass.ds(tile + j, 1)]
                                V.scalar_tensor_tensor(out=before[1 - s][:], in0=number[:], scalar=d,
                                                       in1=before[1 - s if j else s][:], op0=ALU.is_equal,
                                                       op1=ALU.add).then_inc(dve_done, 1)
                                ch.n += 1
                                V.scalar_tensor_tensor(out=hit[j % 2][:], in0=number[:], scalar=d, in1=before[s][:],
                                                       op0=ALU.is_equal, op1=ALU.mult, accum_out=place[s][:, j:j + 1])\
                                    .then_inc(dve_done, 1)
                                ch.n += 1
                                dve.wait_ge(dve_done, ch.n if j == TG - 1 else ch.n - 1)
                            V.tensor_copy(moved[s][:], rec[:, bass.ds(tile, TG), :])
                            V.scalar_tensor_tensor(out=stage[s][:], in0=place[s][:], scalar=float(target_row),
                                                   in1=earlier[:, bass.ds(tile, TG)], op0=ALU.add, op1=ALU.add)\
                                .then_inc(staged, 1)

                        put(0, 0)
                        put(1, TG)
                        ch.close()
                        with dve.Fori(0, BODIES - 1) as i:
                            for s in range(2):
                                dve.wait_ge(sent[s], 64 * i + 64)
                                put(s, i * (2 * TG) + (2 + s) * TG)
                            ch.close()
                        for s in range(2):
                            dve.wait_ge(sent[s], 64 * BODIES)

        assert E % NT == 0 and E // NT >= 96
        EDGE_P = E // NT
        unsorted = sb(main, "unsorted", [1, 1], I32)
        edges = [dram(f"edges_{n}", (EP,), I32) for n in ("src", "dst", "type", "weight")]
        given = [src, dst, etype, weight.bitcast(I32)]
        with Phase(nc) as st:
            here, after = [sb(st, f"o_{n}", [EDGE_P, NT], I32) for n in ("here", "after")]
            here_f, after_f, falls = [sb(st, f"o_{n}", [EDGE_P, NT]) for n in ("here_f", "after_f", "falls")]
            count, ones = sb(st, "o_count", [EDGE_P, 1]), sb(st, "o_ones", [EDGE_P, 1])
            ps_count = pb(st, "o_ps", (1, 1))
            cleared, loaded, copied, made, counted, summed = [sem(st, f"o_{n}") for n in (
                "cleared", "loaded", "copied", "made", "counted", "summed")]
            with nc.Block() as block:
                @block.gpsimd
                def _(gp):
                    nc.gpsimd.memset(after[:], N)
                    nc.gpsimd.memset(ones[:], 1.0).then_inc(cleared, 1)

                @block.sync
                def _(sp):
                    for a, to in zip(given, edges):
                        sp.dma_start(to[0:E], a).then_inc(copied, 16)
                    take(sp, cleared)
                    sp.dma_start(here[:], dst.rearrange("(p t) -> p t", t=NT)).then_inc(loaded, 16)
                    sp.dma_start(after[0:EDGE_P - 1, :], dst[1:E - NT + 1].rearrange("(p t) -> p t", t=NT))\
                        .then_inc(loaded, 16)
                    sp.dma_start(after[EDGE_P - 1:EDGE_P, 0:NT - 1],
                                 dst[E - NT + 1:E].rearrange("(p t) -> p t", p=1)).then_inc(loaded, 16)
                    sp.wait_ge(copied, 16 * len(given))

                @block.vector
                def _(dve):
                    ch = Chain(dve, dve_done)
                    V = nc.vector
                    dve.wait_ge(loaded, 48)
                    V.tensor_copy(here_f[:], here[:])
                    ch.link(V.tensor_copy(after_f[:], after[:]))
                    V.scalar_tensor_tensor(out=falls[:], in0=here_f[:], scalar=1.0, in1=after_f[:], op0=ALU.mult,
                                           op1=ALU.is_gt, accum_out=count[:]).then_inc(counted, 1)
                    take(dve, summed)
                    ch.link(V.tensor_copy(unsorted[:], ps_count[:]))
                    ch.close()

                @block.tensor
                def _(pe):
                    take(pe, counted)
                    nc.tensor.matmul(ps_count[:], count[:], ones[:], start=True, stop=True).then_inc(summed, 1)

        falls_found = nc.values_load(unsorted[0:1, 0:1], min_val=0, max_val=E)
        with nc.If(falls_found > 0):
            rec_a, rec_b = [dram(f"rec_dst_{n}", (EP, 4), I32) for n in "ab"]
            radix_phase("oa", given, 1, BINS, None, rec_a, 0)
            radix_phase("ob", None, 1, HIGH_BINS, rec_a, rec_b, 0)
            with Phase(nc) as st:
                rec = sb(st, "v_rec", [P, NT, 4], I32)
                field = sb(st, "v_field", [P, 4, NT], I32)
                loaded, split, written = [sem(st, f"v_{n}") for n in ("loaded", "split", "written")]
                with nc.Block() as block:
                    @block.sync
                    def _(sp):
                        sp.dma_start(rec[:], rec_b.rearrange("(p t) k -> p t k", p=P)).then_inc(loaded, 16)
                        take(sp, split)
                        for n, to in enumerate(edges):
                            sp.dma_start(to.rearrange("(p t) -> p t", p=P), field[:, n, :]).then_inc(written, 16)
                        sp.wait_ge(written, 16 * len(edges))

                    @block.vector
                    def _(dve):
                        dve.wait_ge(loaded, 16)
                        for n in range(4):
                            last = nc.vector.tensor_copy(field[:, n, :], rec[:, :, n])
                        last.then_inc(split, 1)
        with nc.Else():
            nc.all_engine_barrier()
        nc.all_engine_barrier()
        src, dst, etype, weight = [e[0:E] for e in edges]

        with Phase(nc) as st:
            raw = sb(st, "raw_edges", [HALF, 4, 2, P], I32)
            raw_et = sb(st, "raw_et", [HALF, 2, P], I32)
            pads = sb(st, "pads", [1, EP + 2 - E], I32)
            tab = sb(st, "tab", [NODE_P, N // NODE_P, 4], I32)
            tab_nt = sb(st, "tab_nt", [NODE_P, N // NODE_P], I32)
            fA = sb(st, "fA", [HALF, 4, 2, P])
            etA = sb(st, "etA", [HALF, 2, P])
            pos_i = sb(st, "pos_i", [HALF, 2, P], I32)
            pos = sb(st, "pos", [HALF, 2, P])
            first = sb(st, "first", [HALF, 2, P])
            last_ = sb(st, "last_", [HALF, 2, P])
            t1 = sb(st, "t1", [HALF, 2, P])
            t2 = sb(st, "t2", [HALF, 2, P])
            t3 = sb(st, "t3", [HALF, 2, P])
            cnt = sb(st, "cnt", [HALF, 2, P])
            rootA = sb(st, "rootA", [HALF, 2, P])
            dinvA = sb(st, "dinvA", [HALF, 2, P])
            thirdA = sb(st, "thirdA", [HALF, 2, P])
            dclA = sb(st, "dclA", [HALF, 2, P])
            outA = sb(st, "outA", [HALF, 2, P])
            starts = sb(st, "starts", [HALF, 2, P])
            bfA = sb(st, "bfA", [HALF, 5, 2, P], BF16)
            ohA = sb(st, "ohA", [HALF, ETYPES, 2, P])
            zero_keep = sb(st, "zero_keep", [P, NT])
            run_rows = sb(st, "run_rows", [1, NT + 1])
            carry = sb(st, "carry", [HALF, 2])
            one = sb(st, "one", [1, 1])
            b2r = sb(st, "b2r", [1, 3, D])
            pri_h = sb(st, "pri_h", [HEADS, ETYPES])
            spread = sb(st, "spread", [HEADS, D])
            b1r = sb(st, "b1r", [2, P])
            b2h = sb(st, "b2h", [1, 3, D], BF16)
            zrow = sb(st, "zrow", [1, D])
            ps = [pb(st, f"pp{n}") for n in range(8)]
            p_pad, p_dst, p_w, p_ld, p_tab, p_b2, p_z, p_st, p_b2c = [sem(st, f"p_{n}") for n in (
                "pad", "dst", "w", "ld", "tab", "b2", "z", "st", "b2c")]
            p_mem, p_own, p_ident, p_tot, p_scan, p_carry, p_root, p_rooted, p_field, p_turn, p_seq, p_tabd, p_raw = [
                sem(st, f"p_{n}") for n in ("mem", "own", "ident", "tot", "scan", "carry", "root", "rooted",
                                            "field", "turn", "seq", "tabd", "raw")]
            FULL = E // P - HALF
            REST = E - (HALF + FULL) * P

            def halves(view_out, flat, n):
                whole = n // P - HALF
                rest = n - (HALF + whole) * P
                got = [(view_out[:, 0, :], flat[0:HALF * P].rearrange("(t c) -> t c", c=P)),
                       (view_out[0:whole, 1, :], flat[HALF * P:(HALF + whole) * P].rearrange("(t c) -> t c", c=P))]
                if rest:
                    got.append((view_out[whole:whole + 1, 1, 0:rest],
                                flat[(HALF + whole) * P:n].rearrange("(a c) -> a c", a=1)))
                return got

            with nc.Block() as block:
                @block.sync
                def _(sp):
                    take(sp, p_pad)
                    sp.dma_start(edge_dst[1:E + 1], dst).then_inc(p_dst, 16)
                    sp.dma_start(edge_dst[E + 1:EP + 2].rearrange("(a c) -> a c", a=1), pads[0:1, 1:]).then_inc(p_dst, 16)
                    sp.dma_start(edge_dst[0:1].rearrange("(a c) -> a c", a=1), pads[0:1, 0:1]).then_inc(p_dst, 16)
                    take(sp, p_raw)
                    for t in range(NTYPES):
                        sp.dma_start(wk[:, t, :], w_kqv[t]).then_inc(p_w, 16)
                        sp.dma_start(wa[:, t, :], w_a[t]).then_inc(p_w, 16)
                    for h in range(HEADS):
                        sp.dma_start(ra[h * HD:(h + 1) * HD, :, h * HD:(h + 1) * HD],
                                     rel_att[h].rearrange("t d f -> d t f")).then_inc(p_w, 16)
                    sp.dma_start(pri_h[:], rel_pri).then_inc(p_w, 16)
                    sp.dma_start(w1s[:], w1).then_inc(p_w, 16)
                    sp.dma_start(w2s[:], w2.rearrange("(c p) f -> p c f", p=P)).then_inc(p_w, 16)
                    sp.dma_start(b1r[:], b1.rearrange("(c p) -> c p", p=P)).then_inc(p_w, 16)
                    sp.dma_start(b2_all[:], b2.rearrange("(a f) -> a f", a=1).to_broadcast([P, D])).then_inc(p_w, 16)
                    sp.dma_start(b2r[:, 0, :], b2.rearrange("(a f) -> a f", a=1)).then_inc(p_b2, 16)
                    sp.dma_start(tab_nt[:], ntype.rearrange("(p c) -> p c", p=NODE_P)).then_inc(p_tab, 16)
                    for o, f in halves(raw[:, 0], src, E) + halves(raw_et[:], etype, E):
                        sp.dma_start(o, f).then_inc(p_ld, 16)
                    sp.wait_ge(p_dst, 48)
                    for k, off in ((1, 1), (2, 2), (3, 0)):
                        for h in range(2):
                            sp.dma_start(raw[:, k, h, :], edge_dst[off + h * HALF * P:off + (h + 1) * HALF * P]
                                         .rearrange("(t c) -> t c", c=P)).then_inc(p_ld, 16)
                    sp.dma_start(e1_rows[EP:EP + 1, :], zrow[:]).then_inc(p_z, 16)
                    sp.dma_start(e2_rows[EP:EP + 1, :], zrow[:]).then_inc(p_z, 16)
                    take(sp, p_tabd)
                    sp.dma_start(node_table.rearrange("(p c) k -> p c k", p=NODE_P), tab[:]).then_inc(p_st, 16)
                    take(sp, p_b2c)
                    for k in range(3):
                        for j in range(TG):
                            sp.dma_start(b2_parts[k:k + 1, j * D:(j + 1) * D], b2h[0:1, k, :]).then_inc(p_st, 16)
                    take(sp, p_seq)
                    for k in range(5):
                        sp.dma_start(seq_rows[k].rearrange("(h t c) -> t h c", h=2, c=P), bfA[:, k]).then_inc(p_st, 16)
                    for k in range(ETYPES):
                        sp.dma_start(onehot_rows[k].rearrange("(h t c) -> t h c", h=2, c=P), ohA[:, k])\
                            .then_inc(p_st, 16)
                    sp.dma_start(dinv_row[0].rearrange("(h t c) -> t h c", h=2, c=P), dinvA[:]).then_inc(p_st, 16)
                    sp.wait_ge(p_z, 32)
                    sp.wait_ge(p_st, 16 * (1 + 3 * TG + 5 + ETYPES + 1))

                @block.gpsimd
                def _(gp):
                    nc.gpsimd.memset(pads[:], 2 * FAR)
                    nc.gpsimd.memset(zrow[:], 0.0)
                    nc.gpsimd.memset(ident[:], 0.0).then_inc(p_own, 1)
                    gp.wait_ge(p_own, 1)
                    nc.gpsimd.memset(pads[0:1, 0:1], -1).then_inc(p_pad, 1)
                    nc.gpsimd.memset(raw_et[:], 0)
                    nc.gpsimd.memset(raw[:, 0], 0)
                    nc.gpsimd.memset(ra[:], 0.0).then_inc(p_raw, 1)
                    nc.gpsimd.affine_select(out=ident[:], in_=ident[:], compare_op=ALU.not_equal, fill=1.0,
                                            base=0, pattern=[[-1, P]], channel_multiplier=1).then_inc(p_ident, 1)
                    nc.gpsimd.memset(tab[:], 0)
                    nc.gpsimd.iota(pos_i[:], pattern=[[HALF * P, 2], [1, P]], base=1, channel_multiplier=P)
                    nc.gpsimd.memset(entry_dst[:], 0)
                    nc.gpsimd.memset(entry_src[:], 0)
                    nc.gpsimd.memset(head_ones[:], 0.0).then_inc(p_mem, 1)
                    gp.wait_ge(p_mem, 1)
                    nc.gpsimd.iota(entry_dst[:, 0:NT, 0], pattern=[[P, NT]], base=1, channel_multiplier=1)
                    for t in (i_src, i_dst, i_out, i_pick, i_node1, i_dst1, i_srcout, k_src, k_out, k_dst, k_pick):
                        nc.gpsimd.memset(t[:, NT:NT + 2 * TG], 0)
                    nc.gpsimd.memset(one[:], 1.0)
                    nc.gpsimd.memset(run_rows[:], 0.0)
                    nc.gpsimd.memset(zero_keep[:], 0.0)
                    nc.gpsimd.memset(ones3[:], 1.0)
                    for k, v in ((EPS1, EPS), (EPS16, 16 * EPS), (EPS_SQ, ES), (EPS_CB, E3), (EPS_1, E1), (EPS_M, EPS / 2.25),
                                 (ONE, 1.0)):
                        last = nc.gpsimd.memset(eps_col[:, k:k + 1], v)
                    last.then_inc(p_mem, 1)
                    for h in range(HEADS):
                        gp.wait_ge(p_mem, 2 + h)
                        nc.gpsimd.memset(head_ones[h * HD:(h + 1) * HD, h * HD:(h + 1) * HD], 1.0).then_inc(p_mem, 1)
                    gp.wait_ge(p_mem, 2 + HEADS)
                    nc.gpsimd.memset(spread[:], 1.0).then_inc(p_mem, 1)
                    gp.wait_ge(p_mem, 3 + HEADS)
                    nc.gpsimd.affine_select(out=spread[:], in_=spread[:], compare_op=ALU.is_ge, fill=0.0,
                                            base=0, pattern=[[1, D]], channel_multiplier=-HD).then_inc(p_mem, 1)
                    gp.wait_ge(p_mem, 4 + HEADS)
                    nc.gpsimd.affine_select(out=spread[:], in_=spread[:], compare_op=ALU.is_ge, fill=0.0,
                                            base=HD - 1, pattern=[[-1, D]], channel_multiplier=HD).then_inc(p_mem, 1)

                @block.vector
                def _(dve):
                    ch = Chain(dve, dve_done)
                    V = nc.vector
                    dve.wait_ge(p_w, 16 * (2 * NTYPES + HEADS + 5))
                    for t in range(1, NTYPES):
                        V.tensor_tensor(wk[:, t, :], wk[:, t, :], wk[:, 0, :], ALU.subtract)
                        V.tensor_tensor(wa[:, t, :], wa[:, t, :], wa[:, 0, :], ALU.subtract)
                    for t in range(1, ETYPES):
                        V.tensor_tensor(ra[:, t, :], ra[:, t, :], ra[:, 0, :], ALU.subtract)
                    dve.wait_ge(p_b2, 16)
                    for k in range(3):
                        ch.link(V.tensor_copy(b2h[:, k, :], b2r[:, k, :]))
                        if k < 2:
                            ch.link(V.tensor_tensor(b2r[:, k + 1, :], b2r[:, k, :], b2h[:, k, :], ALU.subtract))
                    V.nop().then_inc(p_b2c, 1)
                    dve.wait_ge(p_mem, 2 + HEADS)
                    dve.wait_ge(p_tab, 16)
                    V.tensor_copy(tab[:, :, 1], tab_nt[:]).then_inc(p_tabd, 1)
                    dve.wait_ge(p_ld, 16 * 12)
                    V.tensor_copy(fA[:], raw[:])
                    V.tensor_copy(pos[:], pos_i[:])
                    ch.link(V.tensor_copy(etA[:], raw_et[:]))
                    SRC, DST, NEXT, PREV = range(4)
                    V.tensor_tensor(first[:], fA[:, DST], fA[:, PREV], ALU.not_equal)
                    V.tensor_tensor(t1[:], fA[:, DST], fA[:, NEXT], ALU.not_equal)
                    V.tensor_scalar(t2[:], fA[:, DST], float(N), None, ALU.is_lt)
                    V.tensor_scalar(dclA[:], fA[:, DST], float(N - 1), None, ALU.min)
                    ch.link(V.tensor_scalar(outA[:], fA[:, DST], float(FAR), None, ALU.add))
                    ch.link(V.tensor_tensor(last_[:], t1[:], t2[:], ALU.mult))
                    V.scalar_tensor_tensor(out=t3[:], in0=last_[:], scalar=-float(FAR), in1=outA[:], op0=ALU.mult,
                                           op1=ALU.add)
                    ch.link(V.tensor_tensor(t1[:], pos[:], first[:], ALU.mult))
                    for h in range(2):
                        last = V.tensor_tensor_scan(starts[:, h, :], zero_keep[0:HALF, 0:P], t1[:, h, :], 0.0,
                                                    ALU.add, ALU.max)
                    last.then_inc(p_tot, 1)
                    take(dve, p_scan)
                    V.tensor_tensor_scan(run_rows[:, 1:NT + 1], zero_keep[0:1, :], ps[0][0:1, 0:NT], 0.0,
                                         ALU.add, ALU.max).then_inc(p_carry, 1)
                    take(dve, p_scan)
                    ch.link(V.tensor_copy(carry[:], ps[1][0:HALF, 0:2]))
                    for h in range(2):
                        last = V.tensor_scalar(starts[:, h, :], starts[:, h, :], carry[:, h:h + 1], None, ALU.max)
                    ch.link(last)
                    ch.link(V.tensor_tensor(t2[:], pos[:], starts[:], ALU.subtract))
                    V.tensor_scalar(t1[:], t2[:], 3.0, 3.0, ALU.mult, ALU.add)
                    ch.link(V.tensor_scalar(cnt[:], t2[:], 1.0, None, ALU.add))
                    V.nop().then_inc(p_root, 1)
                    V.reciprocal(thirdA[:], t1[:])
                    V.tensor_scalar(bfA[:, KEEP], first[:], -1.0, 1.0, ALU.mult, ALU.add)
                    V.tensor_scalar(bfA[:, NFIRST], first[:], -BIG, None, ALU.mult)
                    V.tensor_scalar(bfA[:, NOTLAST], last_[:], -1.0, 1.0, ALU.mult, ALU.add)
                    V.tensor_scalar(bfA[:, NLAST], last_[:], -BIG, None, ALU.mult)
                    V.tensor_copy(bfA[:, ET], etA[:])
                    for t in range(ETYPES):
                        V.tensor_scalar(ohA[:, t], etA[:], float(t), None, ALU.is_equal)
                    take(dve, p_rooted)
                    ch.link(V.reciprocal(dinvA[:], rootA[:]))
                    V.nop().then_inc(p_seq, 1)
                    V.nop().then_inc(p_field, 1)
                    outs = (i_src, i_dst, i_out, c_last, c_third, c_dinv, c_root)
                    take(dve, p_turn)
                    for n, o in enumerate(outs):
                        V.tensor_copy(o[:, 0:NT], ps[n][:, 0:NT])
                    V.tensor_scalar(pri[:], ps[7][0:ETYPES, 0:D], HD ** -0.5, None, ALU.mult)
                    V.tensor_copy(b1s[:], ps[7][:, D:D + 2])
                    ch.close()

                @block.scalar
                def _(act):
                    nc.scalar.preload_act_table(ACT.Sqrt)
                    take(act, p_root)
                    nc.scalar.activation(rootA[:], cnt[:], ACT.Sqrt, bias=eps_col[0:HALF, ONE:ONE + 1])\
                        .then_inc(p_rooted, 1)

                @block.tensor
                def _(pe):
                    pe.wait_ge(p_ident, 1)
                    take(pe, p_tot)
                    for h in range(2):
                        last = nc.tensor.matmul(ps[0][0:1, h * HALF:(h + 1) * HALF], starts[:, h, P - 1:P],
                                                ident[0:HALF, 0:HALF], start=True, stop=True)
                    last.then_inc(p_scan, 1)
                    take(pe, p_carry)
                    for h in range(2):
                        last = nc.tensor.matmul(ps[1][0:HALF, h:h + 1], run_rows[0:1, h * HALF:(h + 1) * HALF],
                                                one[:], start=True, stop=True)
                    last.then_inc(p_scan, 1)
                    take(pe, p_field)
                    for n, f in enumerate((fA[:, 0], dclA, t3, last_, thirdA, dinvA, rootA)):
                        for h in range(2):
                            last = nc.tensor.transpose(ps[n][:, h * HALF:(h + 1) * HALF], f[:, h, :],
                                                       ident[0:HALF, 0:HALF])
                    pe.wait_ge(p_w, 16 * (2 * NTYPES + HEADS + 5))
                    pe.wait_ge(p_mem, 5 + HEADS)
                    nc.tensor.matmul(ps[7][0:ETYPES, 0:D], pri_h[:], spread[:], start=True, stop=True)
                    last = nc.tensor.transpose(ps[7][:, D:D + 2], b1r[:], ident[0:2, 0:2])
                    last.then_inc(p_turn, 1)

        dense_psum = ExitStack()
        main.push(dense_psum)
        ps_dt = pb(dense_psum, "ps_dt")
        ps_dh = two(pb, dense_psum, "ps_dh")
        ps_do = pb(dense_psum, "ps_do")

        def table_phase(tag, k0, jobs):
            with Phase(nc) as st:
                stage = [two(sb, st, f"{tag}_stage{n}", [P, TG], I32) for n in range(len(jobs))]
                moved = [two(sb, st, f"{tag}_moved{n}", [P, TG, job[4]], I32) for n, job in enumerate(jobs)]
                staged = sem(st, f"{tag}_staged")
                done = two(sem, st, f"{tag}_done")
                per = 64 * len(jobs)
                with nc.Block() as block:
                    @block.gpsimd
                    def _(gp):
                        bounds = [gp.to_reg(job[0].shape[0] - 1) for job in jobs]
                        with gp.Fori(0, BODIES) as i:
                            for s in range(2):
                                take(gp, staged)
                                for n, (table, _, _, _, _, rows, _) in enumerate(jobs):
                                    for j in range(TG):
                                        at = bass.IndirectOffsetOnAxis(ap=stage[n][s][:, j:j + 1], axis=0)
                                        if rows is None:
                                            gp.indirect_dma_start(moved[n][s][:, j, :], None, table, at,
                                                                  bounds_check=bounds[n], oob_is_err=False)\
                                                .then_inc(done[s], 16)
                                        else:
                                            gp.indirect_dma_start(table, at, moved[n][s][:, j, :], None,
                                                                  bounds_check=bounds[n], oob_is_err=False)\
                                                .then_inc(done[s], 16)

                    @block.vector
                    def _(dve):
                        ch = Chain(dve, dve_done)
                        V = nc.vector

                        def put(s, tile):
                            reg = not isinstance(tile, int)
                            for n, (_, index, times, plus, _, rows, _) in enumerate(jobs):
                                if rows is not None:
                                    V.tensor_copy(moved[n][s][:], sl(rows, tile, reg))
                                last = V.tensor_scalar(stage[n][s][:], sl(index, tile, reg), float(times),
                                                       float(plus), ALU.mult, ALU.add)
                            last.then_inc(staged, 1)

                        def used(s, tile, reg):
                            last = None
                            for n, job in enumerate(jobs):
                                if job[6] is not None:
                                    last = job[6](V, moved[n][s], tile, reg)
                            if last is not None:
                                ch.link(last)

                        put(0, 0)
                        put(1, TG)
                        n0 = k0 // 2

                        def step(i, s, dense, put_next):
                            reg = not isinstance(i, int)
                            if dense:
                                stats = dense_dve_a(dve, ch, s, i + n0)
                            dve.wait_ge(done[s], per * i + per)
                            used(s, i * (2 * TG) + s * TG, reg)
                            if put_next:
                                put(s, i * (2 * TG) + (2 + s) * TG)
                            if dense:
                                dense_dve_m(dve, ch, s, stats)
                                dense_dve_b(dve, ch, s)

                        begin = max(0, -n0)
                        for i in range(begin):
                            for s in range(2):
                                step(i, s, False, True)
                        if k0 <= 0:
                            dense_start(dve, ch)
                        ch.close()
                        with dve.Fori(begin, BODIES - 1) as i:
                            for s in range(2):
                                step(i, s, True, True)
                            ch.close()
                        for s in range(2):
                            step(BODIES - 1, s, True, False)
                        ch.close()

                    dense_beside(block, k0)

        def dense_beside(block, k0):
            begin = max(0, -k0 // 2)

            @block.sync
            def _(sp):
                if k0 <= 0:
                    for s in range(2):
                        sp.dma_start(dx[s][:], node_rows(x, s)).then_inc(d_loaded[s], 16)
                        sp.nop().then_inc(d_stored[s], 16)
                    d_load(sp, 2, 0)
                with sp.Fori(begin, BODIES) as i:
                    for s in range(2):
                        d_load(sp, i * 2 + (k0 + 3 + s), 1 - s)
                        d_store(sp, i * 2 + (k0 + s), s)

            @block.scalar
            def _(act):
                nc.scalar.preload_act_table(ACT.Sqrt)
                if k0 <= 0:
                    for s in range(2):
                        d_root1(act, s)
                    d_norm1(act, 0)
                    d_copy(act, 0)
                    d_hid(act, 0)
                with act.Fori(begin, BODIES) as i:
                    for s in range(2):
                        dense_act(act, s)

            @block.tensor
            def _(pe):
                if k0 <= 0:
                    d_turn(pe, 0)
                    d_first(pe, 0)
                with pe.Fori(begin, BODIES) as i:
                    for s in range(2):
                        d_second(pe, s)
                        d_turn(pe, 1 - s)
                        d_first(pe, 1 - s)

        def dense_act(act, s, more=2, beside=None):
            if more:
                d_norm1(act, 1 - s)
                d_copy(act, 1 - s)
            if beside:
                beside()
            if more > 1:
                d_root1(act, s)
            if more:
                d_hid(act, 1 - s)
            d_root2(act, s)

        def sl(t, tile, reg, k=TG):
            return t[:, bass.ds(tile, k)] if reg else t[:, tile:tile + k]

        assert E % NT == 0 and E // NT >= 96
        radix_phase("ra", (src, dst, weight), 0, BINS, None, rec_low, 0)
        radix_phase("rb", None, 0, HIGH_BINS, rec_low, rec_src, 1)

        with Phase(nc) as st:
            recA = [sb(st, f"g_rec{n}", [HALF, 2, P, 4], I32) for n in range(3)]
            kA = [sb(st, f"g_key{n}", [HALF, 2, P]) for n in range(3)]
            first, last_, t1, outA, srcA, dstA, numA, wA = [sb(st, f"g_{n}", [HALF, 2, P]) for n in (
                "first", "last", "t1", "out", "src", "dst", "num", "w")]
            keepA = sb(st, "g_keep", [HALF, 2, P], BF16)
            edge_pads = sb(st, "g_pads", [1, 4], I32)
            g_pad, g_padded, g_ld, g_field, g_turn, g_keep_ok, g_st = [sem(st, f"g_{n}") for n in (
                "pad", "padded", "ld", "field", "turn", "keep_ok", "stored")]
            psg = [pb(st, f"g_ps{n}") for n in range(3)]
            with nc.Block() as block:
                @block.gpsimd
                def _(gp):
                    nc.gpsimd.memset(edge_pads[:], -1).then_inc(g_pad, 1)
                    nc.gpsimd.iota(entry_src[:, 0:NT, 0], pattern=[[P, NT]], base=1, channel_multiplier=1)

                @block.sync
                def _(sp):
                    take(sp, g_pad)
                    for r in (0, EP + 1):
                        sp.dma_start(rec_src[r:r + 1, :], edge_pads[:]).then_inc(g_padded, 16)
                    sp.wait_ge(g_padded, 32)
                    for n in range(3):
                        for h in range(2):
                            sp.dma_start(recA[n][:, h], rec_src[n + h * HALF * P:n + (h + 1) * HALF * P, :]
                                         .rearrange("(t c) k -> t c k", c=P)).then_inc(g_ld, 16)
                    take(sp, g_keep_ok)
                    sp.dma_start(keep_src[0].rearrange("(h t c) -> t h c", h=2, c=P), keepA[:]).then_inc(g_st, 16)
                    sp.wait_ge(g_st, 16)

                @block.vector
                def _(dve):
                    ch = Chain(dve, dve_done)
                    V = nc.vector
                    dve.wait_ge(g_ld, 16 * 6)
                    for n in range(3):
                        V.tensor_copy(kA[n][:], recA[n][:, :, :, 0])
                    V.tensor_copy(t1[:], recA[1][:, :, :, 1])
                    V.tensor_copy(wA[:].bitcast(I32), recA[1][:, :, :, 2])
                    ch.link(V.tensor_copy(numA[:], recA[1][:, :, :, 3]))
                    V.tensor_scalar(dstA[:], t1[:], float(N - 1), None, ALU.min)
                    V.tensor_scalar(srcA[:], kA[1][:], float(N - 1), None, ALU.min)
                    V.tensor_tensor(first[:], kA[1][:], kA[0][:], ALU.not_equal)
                    V.tensor_tensor(last_[:], kA[1][:], kA[2][:], ALU.not_equal)
                    ch.link(V.tensor_scalar(outA[:], kA[1][:], float(FAR), None, ALU.add))
                    V.tensor_scalar(keepA[:], first[:], -1.0, 1.0, ALU.mult, ALU.add).then_inc(g_keep_ok, 1)
                    V.scalar_tensor_tensor(out=outA[:], in0=last_[:], scalar=-float(FAR), in1=outA[:], op0=ALU.mult,
                                           op1=ALU.add).then_inc(g_field, 1)
                    take(dve, g_turn)
                    V.tensor_copy(k_src[:, 0:NT], psg[0][:, 0:NT])
                    V.tensor_copy(k_dst[:, 0:NT], psg[0][:, NT:2 * NT])
                    V.tensor_copy(k_out[:, 0:NT], psg[1][:, 0:NT])
                    V.tensor_copy(k_w[:], psg[1][:, NT:2 * NT])
                    V.tensor_scalar(entry_src[:, 0:NT, 1], psg[2][:, 0:NT], 1.0, None, ALU.add)
                    ch.close()

                @block.tensor
                def _(pe):
                    take(pe, g_field)
                    for n, f in enumerate((srcA, dstA, outA, wA, numA)):
                        for h in range(2):
                            c = (n % 2) * NT + h * HALF
                            last = nc.tensor.transpose(psg[n // 2][:, c:c + HALF], f[:, h, :], ident[0:HALF, 0:HALF])
                    last.then_inc(g_turn, 1)

        c_got = [sb(main, f"c_got{n}", [P, NT]) for n in range(2)]
        c_got_dst = sb(main, "c_got_dst", [P, NT])
        c_num = sb(main, "c_num", [P, NT])

        def of_edge_src(V, moved, tile, reg):
            return V.tensor_copy(sl(k_pick, tile, reg), moved[:, :, 2])

        def of_src(V, moved, tile, reg):
            V.tensor_copy(sl(c_got[0], tile, reg), moved[:, :, 0])
            V.tensor_copy(sl(c_nts, tile, reg), moved[:, :, 1])
            V.tensor_copy(sl(c_got[1], tile, reg), moved[:, :, 2])
            return V.tensor_copy(sl(c_num, tile, reg), moved[:, :, 3])

        def of_dst(V, moved, tile, reg):
            V.tensor_copy(sl(c_ntd, tile, reg), moved[:, :, 1])
            return V.tensor_copy(sl(c_got_dst, tile, reg), moved[:, :, 2])

        halves_of_nodes = node_table.rearrange("n (h k) -> (n h) k", k=2)
        cells_of_nodes = node_table.rearrange("n (c k) -> (n c) k", k=1)
        DENSE0 = NGROUPS - 8 * BODIES
        assert -2 * BODIES < DENSE0 <= 0 and DENSE0 % 2 == 0
        table_phase("tp", DENSE0, [(cells_of_nodes, i_out, 4, 0, 1, entry_dst, None),
                                       (halves_of_nodes, k_out, 2, 1, 2, entry_src, None)])
        table_phase("tg", DENSE0 + 2 * BODIES, [(node_table, k_dst, 1, 0, 4, None, of_edge_src),
                                       (node_table, i_src, 1, 0, 4, None, of_src),
                                       (node_table, i_dst, 1, 0, 4, None, of_dst)])

        with Phase(nc) as st:
            pf = sb(st, "pf", [P, NT])
            t1, t2, t3 = [sb(st, f"q_t{n}", [P, NT]) for n in range(3)]
            codes = sb(st, "codes", [HALF, 2, 2, P], BF16)
            q_turn, q_code, q_st = [sem(st, f"q_{n}") for n in ("turn", "code", "st")]
            psq = two(pb, st, "psq", (P, GE))
            with nc.Block() as block:
                @block.vector
                def _(dve):
                    ch = Chain(dve, dve_done)
                    V = nc.vector
                    ch.link(V.tensor_copy(pf[:], k_pick[:, 0:NT]))
                    for got, to in ((pf, k_pick), (c_got[0], i_pick)):
                        ch.link(V.tensor_scalar(t1[:], got[:], 0.0, float(NONE + 1), ALU.is_equal, ALU.mult))
                        ch.link(V.scalar_tensor_tensor(out=to[:, 0:NT], in0=got[:], scalar=-1.0, in1=t1[:],
                                                       op0=ALU.add, op1=ALU.add))
                    V.tensor_scalar(t1[:], c_got_dst[:], 0.0, None, ALU.is_equal)
                    ch.link(V.tensor_scalar(t2[:], c_last[:], -1.0, 1.0, ALU.mult, ALU.add))
                    ch.link(V.tensor_tensor(t1[:], t1[:], t2[:], ALU.max))
                    ch.link(V.tensor_scalar(t1[:], t1[:], float(NONE + 1), None, ALU.mult))
                    ch.link(V.scalar_tensor_tensor(out=i_dst1[:, 0:NT], in0=c_got_dst[:], scalar=-1.0, in1=t1[:],
                                                   op0=ALU.add, op1=ALU.add))
                    V.tensor_scalar(i_node1[:, 0:NT], c_got[1][:], -1.0, 0.0, ALU.add, ALU.max)
                    V.tensor_copy(t1[:], entry_dst[:, 0:NT, 0])
                    V.tensor_scalar(t2[:], c_got[0][:], 0.0, None, ALU.is_equal)
                    ch.link(V.tensor_copy(t3[:], i_src[:, 0:NT]))
                    ch.link(V.tensor_tensor(t1[:], t1[:], c_num[:], ALU.is_equal))
                    ch.link(V.tensor_tensor(t1[:], t1[:], t2[:], ALU.mult))
                    ch.link(V.tensor_scalar(t1[:], t1[:], -float(FAR), float(FAR), ALU.mult, ALU.add))
                    ch.link(V.tensor_tensor(i_srcout[:, 0:NT], t1[:], t3[:], ALU.add))
                    take(dve, q_turn)
                    for n in range(2):
                        last = V.tensor_copy(codes[:, n], psq[n][0:HALF, 0:2 * P].rearrange("t (h c) -> t h c", h=2))
                    last.then_inc(q_code, 1)
                    ch.close()

                @block.tensor
                def _(pe):
                    for n, c in enumerate((c_nts, c_ntd)):
                        for h in range(2):
                            last = nc.tensor.transpose(psq[n][0:HALF, h * P:(h + 1) * P],
                                                       c[:, h * HALF:(h + 1) * HALF], ident[:])
                    last.then_inc(q_turn, 1)

                @block.sync
                def _(sp):
                    take(sp, q_code)
                    for n, k in enumerate((NTS, NTD)):
                        sp.dma_start(seq_rows[k].rearrange("(h t c) -> t h c", h=2, c=P), codes[:, n]).then_inc(q_st, 16)
                    sp.wait_ge(q_st, 32)

        def bodies(eng, order, step, ch=None):
            with eng.Fori(0, BODIES - 1) as i:
                for o, s in enumerate(order):
                    step(i, o, s, True)
                if ch:
                    ch.close()
            for o, s in enumerate(order):
                step(BODIES - 1, o, s, False)
            if ch:
                ch.close()

        def is_first(i, o):
            return isinstance(i, int) and i == 0 and o == 0

        def skewed(eng, order, first, both, ch=None, peel=1, head=0):
            first(order[0])
            if ch:
                ch.close()
            for i in range(head):
                for o, s in enumerate(order):
                    both(i, o, s, 1 - s, 2 * peel - 1)
                if ch:
                    ch.close()
            with eng.Fori(head, BODIES - peel) as i:
                for o, s in enumerate(order):
                    both(i, o, s, 1 - s, 2 * peel - 1)
                if ch:
                    ch.close()
            for i in range(BODIES - peel, BODIES):
                for o, s in enumerate(order):
                    behind = 2 * (BODIES - 1 - i) + 1 - o
                    both(i, o, s, 1 - s if behind else None, max(behind - 1, 0))
                if ch:
                    ch.close()

        def hop_phase(tag, table, index, first_hop, last_hop, k0):
            dense = k0 is not None
            with Phase(nc) as st:
                stage = two(sb, st, f"{tag}_stage", [P, TG], I32)
                rows = two(sb, st, f"{tag}_rows", [P, TG, D])
                scaled = two(sb, st, f"{tag}_scaled", [P, TG, D])
                keep = two(sb, st, f"{tag}_keep", [P, 1, GE], BF16)
                sums = two(sb, st, f"{tag}_sums", [P, GE])
                outr = two(sb, st, f"{tag}_outr", [P, TG, D])
                ps_m = two(pb, st, f"{tag}_psm")
                ps_r = two(pb, st, f"{tag}_psr")
                gathered = two(sem, st, f"{tag}_gathered")
                kept = two(sem, st, f"{tag}_kept")
                stored = two(sem, st, f"{tag}_stored")
                staged, freed, rdy, turned, scanned, scan_sp, back, copied = [sem(st, f"{tag}_{n}") for n in (
                    "staged", "freed", "rdy", "turned", "scanned", "scan_sp", "back", "copied")]
                if last_hop:
                    stage2 = two(sb, st, f"{tag}_stage2", [P, TG], I32)
                    brow = two(sb, st, f"{tag}_brow", [P, TG, D])
                    e1r = two(sb, st, f"{tag}_e1r", [P, TG, D])
                    e2r = two(sb, st, f"{tag}_e2r", [P, TG, D])
                    acc = two(sb, st, f"{tag}_acc", [P, TG, D])
                    stt = two(sb, st, f"{tag}_stt", [P, TG, 6])
                    mv = two(sb, st, f"{tag}_mv", [P, TG, 2])
                    sd = two(sb, st, f"{tag}_sd", [P, TG])
                    rr = two(sb, st, f"{tag}_rr", [P, TG])
                    bb = two(sb, st, f"{tag}_bb", [P, TG])
                    hops_in = two(sem, st, f"{tag}_hops_in")
                    var, std, affine, loads_free = [sem(st, f"{tag}_{n}") for n in ("var", "std", "affine", "loads_free")]
                per = 128 if last_hop else 64

                with nc.Block() as block:
                    @block.gpsimd
                    def _(gp):
                        bound = gp.to_reg(N - 1 if first_hop else NONE)
                        bound2 = gp.to_reg(N - 1)
                        with gp.Fori(0, BODIES) as i:
                            for s in range(2):
                                take(gp, staged)
                                for j in range(TG):
                                    gp.indirect_dma_start(
                                        rows[s][:, j, :], None, table,
                                        bass.IndirectOffsetOnAxis(ap=stage[s][:, j:j + 1], axis=0),
                                        bounds_check=bound, oob_is_err=False).then_inc(gathered[s], 16)
                                if last_hop:
                                    for j in range(TG):
                                        gp.indirect_dma_start(
                                            brow[s][:, j, :], None, x,
                                            bass.IndirectOffsetOnAxis(ap=stage2[s][:, j:j + 1], axis=0),
                                            bounds_check=bound2, oob_is_err=False).then_inc(gathered[s], 16)

                    @block.sync
                    def _(sp):
                        for s in range(2):
                            sp.nop().then_inc(stored[s], 16)

                        def load(i, s):
                            take(sp, scan_sp)
                            sp.dma_start(keep[s][:], seq_of(keep_src, i, s, 0, 1)).then_inc(kept[s], 16)
                            if last_hop:
                                take(sp, loads_free)
                                sp.dma_start(e1r[s][:], rows_of(e1_rows, i, s)).then_inc(hops_in[s], 16)
                                sp.dma_start(e2r[s][:], rows_of(e2_rows, i, s)).then_inc(hops_in[s], 16)

                        def both(i, o, s, nxt, more):
                            if more:
                                load(i + 1, s)
                            if dense:
                                k = i * 2 + (k0 + s)
                                d_load(sp, k + 3, 1 - s)
                                d_store(sp, k, s)
                            sp.wait_ge(copied, 2 * i + (3 + s))
                            sp.dma_start(rows_of(x1_nodes if last_hop else e1_rows if first_hop else e2_rows, i, s),
                                         outr[s][:]).then_inc(stored[s], 16)

                        for s in range(2):
                            load(0, s)
                        skewed(sp, (0, 1), lambda s: None, both, peel=2)
                        for s in range(2):
                            sp.wait_ge(stored[s], 16 * (BODIES + 1))

                    @block.vector
                    def _(dve):
                        ch = Chain(dve, dve_done)
                        V = nc.vector

                        def put(s, tile):
                            reg = not isinstance(tile, int)
                            if last_hop:
                                V.tensor_copy(stage2[s][:], sl(k_src, tile, reg))
                            V.tensor_copy(stage[s][:], sl(index, tile, reg)).then_inc(staged, 1)

                        ch.link(V.memset(sums[1][:], 0.0))
                        ch.close()
                        V.nop().then_inc(scan_sp, 2)
                        if last_hop:
                            V.nop().then_inc(loads_free, 2)
                        put(0, 0)
                        put(1, TG)

                        def front(i, s, beside=None):
                            tile = i * (2 * TG) + s * TG
                            dve.wait_ge(gathered[s], per * i + per)
                            V.tensor_tensor(scaled[s][:], rows[s][:],
                                            k_w[:, bass.ds(tile, TG)].unsqueeze(2).to_broadcast([P, TG, D]),
                                            ALU.mult).then_inc(rdy, 1)
                            if last_hop:
                                dve.wait_ge(copied, 2 * i + (1 + s))
                                dve.wait_ge(hops_in[s], 32 * i + 32)
                                ch.link(V.tensor_tensor(acc[s][:], e1r[s][:], e2r[s][:], ALU.add))
                                V.nop().then_inc(loads_free, 1)
                                ch.link(V.scalar_tensor_tensor(out=acc[s][:], in0=brow[s][:], scalar=5.0,
                                                               in1=acc[s][:], op0=ALU.mult, op1=ALU.add))
                            put(s, i * (2 * TG) + (2 + s) * TG)
                            if beside:
                                beside()
                            dve.wait_ge(kept[s], 16 * i + 16)
                            take(dve, turned)
                            ch.link(V.tensor_tensor_scan(sums[s][:], keep[s][:, 0, :], ps_m[s][:],
                                                         sums[1 - s][:, GE - 1:GE], ALU.mult, ALU.add))
                            V.nop().then_inc(scanned, 1)
                            V.nop().then_inc(scan_sp, 1)

                        def both(i, o, s, nxt, more):
                            behind = groups_behind(k0, i, s) if dense else 0
                            stats = []

                            def beside():
                                stats.append(dense_dve_a(dve, ch, s, i + k0 // 2, behind))

                            if nxt is not None:
                                front(i + o, nxt, beside if dense else None)
                            elif dense:
                                beside()
                            if dense:
                                dense_dve_m(dve, ch, s, stats[0])
                                dense_dve_b(dve, ch, s, behind)
                            if last_hop:
                                take(dve, back)
                                ch.link(V.tensor_tensor(acc[s][:], ps_r[s][:].rearrange("p (j f) -> p j f", j=TG),
                                                        acc[s][:], ALU.add))
                                for j in range(TG):
                                    last = V.bn_stats(stt[s][:, j, :], acc[s][:, j, :])
                                ch.link(last)
                                for j in range(TG):
                                    last = V.bn_aggr(mv[s][:, j, :], stt[s][:, j, :])
                                last.then_inc(var, 1)
                                take(dve, std)
                                ch.link(V.reciprocal(rr[s][:], sd[s][:]))
                                V.scalar_tensor_tensor(out=bb[s][:], in0=mv[s][:, :, 0], scalar=-1.0, in1=rr[s][:],
                                                       op0=ALU.mult, op1=ALU.mult).then_inc(affine, 1)

                        skewed(dve, (0, 1), lambda s: front(0, s), both, ch, peel=2)

                    @block.scalar
                    def _(act):
                        nc.scalar.preload_act_table(ACT.Sqrt)
                        nc.scalar.nop().then_inc(copied, 2)

                        def step(i, o, s, nxt, more):
                            if dense:
                                dense_act(act, s, groups_behind(k0, i, s))
                            if last_hop:
                                act.wait_ge(stored[s], 16 * i + 16)
                                take(act, var)
                                nc.scalar.activation(sd[s][:], mv[s][:, :, 1], ACT.Sqrt,
                                                     bias=eps_col[:, EPS16:EPS16 + 1]).then_inc(std, 1)
                                take(act, affine)
                                for j in range(TG):
                                    last = nc.scalar.activation(outr[s][:, j, :], acc[s][:, j, :], ACT.Identity,
                                                                bias=bb[s][:, j:j + 1], scale=rr[s][:, j:j + 1])
                                last.then_inc(copied, 1)
                            else:
                                act.wait_ge(stored[s], 16 * i + 16)
                                take(act, back)
                                nc.scalar.activation(outr[s][:].rearrange("p j f -> p (j f)"), ps_r[s][:],
                                                     ACT.Copy).then_inc(copied, 1)

                        skewed(act, (0, 1), lambda s: None, step, peel=2)

                    @block.tensor
                    def _(pe):
                        def front(s):
                            take(pe, rdy)
                            for j in range(TG):
                                last = nc.tensor.transpose(ps_m[s][:, j * P:(j + 1) * P], scaled[s][:, j, :], ident[:])
                            last.then_inc(turned, 1)

                        def both(i, o, s, nxt, more):
                            behind = groups_behind(k0, i, s) if dense else 0
                            if dense:
                                d_second(pe, s)
                            if behind:
                                d_turn(pe, 1 - s)
                            if nxt is not None:
                                front(nxt)
                            if behind:
                                d_first(pe, 1 - s)
                            pe.wait_ge(copied, 2 * i + (1 + s))
                            take(pe, scanned)
                            for j in range(TG):
                                last = nc.tensor.transpose(ps_r[s][:, j * P:(j + 1) * P],
                                                           sums[s][:, j * P:(j + 1) * P], ident[:])
                            last.then_inc(back, 1)

                        skewed(pe, (0, 1), front, both, peel=2)

        hop_phase("h1", x, k_dst, True, False, None)
        hop_phase("h2", e1_rows, k_pick, False, False, DENSE0 + 4 * BODIES)
        hop_phase("h3", e2_rows, k_pick, False, True, None)

        def norm_stats(V, ch, y, stt, mv, s, var):
            for j in range(TG):
                last = V.bn_stats(stt[s][:, j, :], y[s][:, j, :])
            ch.link(last)
            for j in range(TG):
                last = V.bn_aggr(mv[s][:, j, :], stt[s][:, j, :])
            last.then_inc(var, 1)

        def norm_rows(act, out_rows, y, rr, bb, s):
            for j in range(TG):
                last = nc.scalar.activation(out_rows[s][:, j, :], y[s][:, j, :], ACT.Identity,
                                            bias=bb[s][:, j:j + 1], scale=rr[s][:, j:j + 1])
            return last

        def turn(out_bank, rows3d):
            for j in range(TG):
                last = nc.tensor.transpose(out_bank[:, j * P:(j + 1) * P], rows3d[:, j, :], ident[:])
            return last

        def tiles(t):
            return t.rearrange("p (j f) -> p j f", j=TG)

        def cols(c, i, s):
            return c[:, bass.ds(i * (2 * TG) + s * TG, TG)].unsqueeze(2).to_broadcast([P, TG, D])

        def times_col_plus(V, out, in0, c, i, s, plus):
            for j in range(TG):
                last = V.scalar_tensor_tensor(out=out[:, j, :], in0=in0[:, j, :],
                                              scalar=c[:, bass.ds(i * (2 * TG) + (s * TG + j), 1)], in1=plus(j),
                                              op0=ALU.mult, op1=ALU.add)
            return last

        def local_put(V, which, aff, stage, b, s, aff_ok, staged):
            t = b * (2 * TG) + s * TG
            if which is not None:
                V.tensor_copy(aff[s][:], local[which][:, bass.ds(t, TG), :]).then_inc(aff_ok, 1)
            V.tensor_copy(stage[s][:], i_pick[:, bass.ds(t, TG)]).then_inc(staged, 1)

        def local_rows(act, i, s, a0_in, aff_ok, x_ok, xs, a0r, aff):
            act.wait_ge(a0_in[s], 16 * i + 16)
            take(act, aff_ok)
            for j in range(TG):
                last = nc.scalar.activation(xs[s][:, j, :], a0r[s][:, j, :], ACT.Identity,
                                            bias=aff[s][:, j, 1:2], scale=aff[s][:, j, 0:1])
            last.then_inc(x_ok, 1)

        def picks(gp, bound, table, xs, stage, picked, s):
            for j in range(TG):
                gp.indirect_dma_start(xs[s][:, j, :], None, table,
                                      bass.IndirectOffsetOnAxis(ap=stage[s][:, j:j + 1], axis=0),
                                      bounds_check=bound, oob_is_err=False).then_inc(picked[s], 16)

        with Phase(nc) as st:
            xr, dr, outd = [two(sb, st, n, [P, TG, D]) for n in ("b_xr", "b_dr", "b_out")]
            stage = two(sb, st, "b_stage", [P, 3, TG], I32)
            stt = two(sb, st, "b_stt", [P, TG, 6])
            mv = two(sb, st, "b_mv", [P, TG, 2])
            sd, rr, bb = [two(sb, st, n, [P, TG]) for n in ("b_sd", "b_rr", "b_bb")]
            got, src_got, picked, src_st, dst_st = [two(sem, st, f"b_{n}") for n in (
                "got", "src_got", "picked", "src_st", "dst_st")]
            staged, stats_ok, std, affine, normed = [sem(st, f"b_{n}") for n in (
                "staged", "stats", "std", "affine", "normed")]
            K0 = DENSE0 + 6 * BODIES

            def loop(eng, step, ch=None):
                def body(i):
                    for s in range(2):
                        step(i, s, not isinstance(i, int) or i < BODIES - 1)
                    if ch:
                        ch.close()

                body(0)
                with eng.Fori(1, BODIES - 2) as i:
                    body(i)
                body(BODIES - 2)
                body(BODIES - 1)

            with nc.Block() as block:
                @block.gpsimd
                def _(gp):
                    bound = gp.to_reg(EP - 1)
                    bound_x = gp.to_reg(N - 1)

                    def load(i, s):
                        if not isinstance(i, int) or i:
                            gp.wait_ge(src_st[s], 16 * i)
                        take(gp, staged)
                        for t, k, table, b, q in ((xr, 0, x1_nodes, bound, src_got), (dr, 1, x, bound_x, got)):
                            for j in range(TG):
                                gp.indirect_dma_start(t[s][:, j, :], None, table,
                                                      bass.IndirectOffsetOnAxis(ap=stage[s][:, k, j:j + 1], axis=0),
                                                      bounds_check=b, oob_is_err=False).then_inc(q[s], 16)

                    load(0, 0)
                    load(0, 1)

                    def step(i, s, more):
                        take(gp, normed)
                        for j in range(TG):
                            gp.indirect_dma_start(outd[s][:, j, :], None, x1_nodes,
                                                  bass.IndirectOffsetOnAxis(ap=stage[s][:, 2, j:j + 1], axis=0),
                                                  bounds_check=bound, oob_is_err=False).then_inc(picked[s], 16)
                        if more:
                            load(i + 1, s)

                    loop(gp, step)

                @block.sync
                def _(sp):
                    for s in range(2):
                        sp.nop().then_inc(dst_st[s], 16)

                    def step(i, s, more):
                        k = i * 2 + (K0 + s)
                        sp.wait_ge(src_got[s], 64 * i + 64)
                        sp.dma_start(rows_of(src_x1, i, s), xr[s][:]).then_inc(src_st[s], 16)
                        if not isinstance(k, int) or k + 3 < NGROUPS:
                            d_load(sp, k + 3, 1 - s)
                        sp.wait_ge(picked[s], 64 * i + 64)
                        sp.dma_start(rows_of(x1_rows, i, s), outd[s][:]).then_inc(dst_st[s], 16)
                        if isinstance(k, int) and k == NGROUPS - 1:
                            sp.wait_ge(d_stored[1 - s], 16 * (1 + (k + 1) // 2))
                        d_store(sp, k, s)

                    loop(sp, step)
                    for s in range(2):
                        sp.wait_ge(d_stored[s], 16 * (1 + NGROUPS // 2))
                        sp.wait_ge(src_st[s], 16 * BODIES)
                        sp.wait_ge(dst_st[s], 16 * (BODIES + 1))

                @block.vector
                def _(dve):
                    ch = Chain(dve, dve_done)
                    V = nc.vector

                    def put(b, s):
                        t = b * (2 * TG) + s * TG
                        V.tensor_copy(stage[s][:, 0, :], i_node1[:, bass.ds(t, TG)])
                        V.tensor_copy(stage[s][:, 1, :], i_dst[:, bass.ds(t, TG)]).then_inc(staged, 1)

                    put(0, 0)
                    put(0, 1)

                    def step(i, s, more):
                        t = i * (2 * TG) + s * TG
                        dve.wait_ge(src_got[s], 64 * i + 64)
                        for j in range(TG):
                            last = V.bn_stats(src_stats[:, bass.ds(t + j, 1), :], xr[s][:, j, :])
                        ch.mark(last)
                        dve.wait_ge(got[s], 64 * i + 64)
                        if more:
                            put(i + 1, s)
                        if not isinstance(i, int) or i:
                            dve.wait_ge(picked[s], 64 * i)
                        V.tensor_copy(stage[s][:, 2, :], i_dst1[:, bass.ds(t, TG)])
                        norm_stats(V, ch, dr, stt, mv, s, stats_ok)
                        behind = groups_behind(K0, i, s)
                        dense_stats = dense_dve_a(dve, ch, s, i + K0 // 2, behind)
                        take(dve, std)
                        ch.link(V.reciprocal(rr[s][:], sd[s][:]))
                        ch.link(V.tensor_tensor(rr[s][:], rr[s][:], c_last[:, bass.ds(t, TG)], ALU.mult))
                        V.scalar_tensor_tensor(out=bb[s][:], in0=mv[s][:, :, 0], scalar=-1.0, in1=rr[s][:],
                                               op0=ALU.mult, op1=ALU.mult).then_inc(affine, 1)
                        dense_dve_m(dve, ch, s, dense_stats)
                        dense_dve_b(dve, ch, s, behind)

                    loop(dve, step, ch)

                @block.scalar
                def _(act):
                    nc.scalar.preload_act_table(ACT.Sqrt)

                    def step(i, s, more):
                        take(act, stats_ok)
                        nc.scalar.activation(sd[s][:], mv[s][:, :, 1], ACT.Sqrt, bias=eps_col[:, EPS_1:EPS_1 + 1])\
                            .then_inc(std, 1)

                        def destination_rows():
                            act.wait_ge(dst_st[s], 16 * i + 16)
                            take(act, affine)
                            norm_rows(act, outd, dr, rr, bb, s).then_inc(normed, 1)

                        dense_act(act, s, groups_behind(K0, i, s), destination_rows)

                    loop(act, step)

                @block.tensor
                def _(pe):
                    def step(i, s, more):
                        d_second(pe, s)
                        if groups_behind(K0, i, s):
                            d_turn(pe, 1 - s)
                            d_first(pe, 1 - s)

                    loop(pe, step)

        dense_psum.close()

        with Phase(nc) as st:
            mean = sb(st, "l_mean", [P, NT])
            diff = sb(st, "l_diff", [P, NT])
            vv = sb(st, "l_var", [P, NT])
            root = [sb(st, f"l_root{n}", [P, NT]) for n in range(2)]
            l_var, l_root = [sem(st, f"l_{n}s") for n in ("var", "root")]
            with nc.Block() as block:
                @block.vector
                def _(dve):
                    ch = Chain(dve, dve_done)
                    V = nc.vector
                    S = src_stats
                    V.tensor_tensor(mean[:], S[:, :, 1], S[:, :, 4], ALU.add)
                    V.tensor_tensor(diff[:], S[:, :, 1], S[:, :, 4], ALU.subtract)
                    ch.link(V.tensor_tensor(vv[:], S[:, :, 2], S[:, :, 5], ALU.add))
                    V.tensor_scalar(mean[:], mean[:], 0.5, None, ALU.mult)
                    V.tensor_scalar(vv[:], vv[:], 1.0 / D, None, ALU.mult)
                    ch.link(V.tensor_tensor(diff[:], diff[:], diff[:], ALU.mult))
                    V.scalar_tensor_tensor(out=vv[:], in0=diff[:], scalar=0.25, in1=vv[:], op0=ALU.mult,
                                           op1=ALU.add).then_inc(l_var, 1)
                    take(dve, l_root)
                    for n in range(2):
                        last = V.reciprocal(local[n][:, :, 0], root[n][:])
                    ch.link(last)
                    for n in range(2):
                        V.scalar_tensor_tensor(out=local[n][:, :, 1], in0=mean[:], scalar=-1.0,
                                               in1=local[n][:, :, 0], op0=ALU.mult, op1=ALU.mult)
                    ch.close()

                @block.scalar
                def _(act):
                    nc.scalar.preload_act_table(ACT.Sqrt)
                    take(act, l_var)
                    for n, (c, e) in enumerate(((1.0, EPS1), (CS, EPS_SQ))):
                        last = nc.scalar.activation(root[n][:], vv[:], ACT.Sqrt, bias=eps_col[:, e:e + 1], scale=c)
                    last.then_inc(l_root, 1)

        with Phase(nc) as st:
            xs, x1r = [two(sb, st, n, [P, TG, D]) for n in ("a_xs", "a_x1r")]
            masks = two(sb, st, "a_masks", [P, 5, GE], BF16)
            onehot = two(sb, st, "a_onehot", [ETYPES, GE])
            sT, dT = [[sb(st, f"{n}{t}", [P, GE]) for t in range(NTYPES)] for n in ("a_sT", "a_dT")]
            kT = [sb(st, f"a_kT{t}", [P, GE]) for t in range(ETYPES)]
            prod = sb(st, "a_prod", [P, GE])
            pri_e, q_all, lg, mx, msg = [two(sb, st, n, [P, GE]) for n in ("a_pri", "a_q", "a_lg", "a_mx", "a_msg")]
            b_sT, b_k, b_m, b_dT, b_q, b_l, b_p = [pb(st, f"a_ps{n}") for n in range(7)]
            xs_in, x1_in, masks_in, msg_st, lm_st = [two(sem, st, f"a_{n}") for n in (
                "xs_in", "x1_in", "masks_in", "msg_st", "lm_st")]
            (masks_free, xs_free, x1_free, s_turned, s_copied, s_masked, k_ok, k_copied, k_masked, m_ok,
             m_copied, x1_turned, x1_copied, x1_masked, q_ok, prod_ok, l_ok, pri_ok, pri_copied, lg_ok, mx_ok) = [
                sem(st, f"a_{n}") for n in (
                    "masks_free", "xs_free", "x1_free", "s_turned", "s_copied", "s_masked", "k_ok",
                    "k_copied", "k_masked", "m_ok", "m_copied", "x1_turned", "x1_copied", "x1_masked", "q_ok",
                    "prod_ok", "l_ok", "pri_ok", "pri_copied", "lg_ok", "mx_ok")]
            ORDER = (1, 0)

            def body_of(i):
                return (BODIES - 1) - i

            with nc.Block() as block:
                @block.sync
                def _(sp):
                    for s in range(2):
                        sp.nop().then_inc(msg_st[s], 16)
                        sp.nop().then_inc(lm_st[s], 32)

                    def load_xs(b, s):
                        sp.dma_start(xs[s][:], rows_of(src_x1, b, s)).then_inc(xs_in[s], 16)

                    def load_x1(b, s):
                        sp.dma_start(x1r[s][:], rows_of(x1_rows, b, s)).then_inc(x1_in[s], 16)

                    def load_masks(b, s):
                        sp.dma_start(masks[s][:], seq_of(seq_rows, b, s, NOTLAST, NTD + 1)).then_inc(masks_in[s], 16)
                        sp.dma_start(onehot[s][:], onehot_rows[:, bass.ds(b * BODY + s * GE, GE)])\
                            .then_inc(masks_in[s], 16)

                    for s in ORDER:
                        load_x1(BODIES - 1, s)
                        load_xs(BODIES - 1, s)
                        load_masks(BODIES - 1, s)

                    def step(i, o, s, more):
                        b = body_of(i)
                        if more:
                            take(sp, x1_free)
                            load_x1(b - 1, s)
                            take(sp, xs_free)
                            load_xs(b - 1, s)
                        sp.wait_ge(m_copied, 2 * i + (o + 1))
                        sp.dma_start(lrm_of(b, s, 2, 3), msg[s][:].unsqueeze(1)).then_inc(msg_st[s], 16)
                        take(sp, lg_ok)
                        sp.dma_start(lrm_of(b, s, 0, 1), lg[s][:].unsqueeze(1)).then_inc(lm_st[s], 16)
                        take(sp, mx_ok)
                        sp.dma_start(lrm_of(b, s, 1, 2), mx[s][:].unsqueeze(1)).then_inc(lm_st[s], 16)
                        if more:
                            take(sp, masks_free)
                            load_masks(b - 1, s)

                    bodies(sp, ORDER, step)
                    for s in range(2):
                        sp.wait_ge(msg_st[s], 16 * (BODIES + 1))
                        sp.wait_ge(lm_st[s], 32 * (BODIES + 1))

                @block.scalar
                def _(act):
                    def rows_copied():
                        take(act, x1_turned)
                        nc.scalar.activation(dT[0][:], b_dT[:], ACT.Copy).then_inc(x1_copied, 1)
                        take(act, s_turned)
                        nc.scalar.activation(sT[0][:], b_sT[:], ACT.Copy).then_inc(s_copied, 1)

                    def rest_copied(s):
                        take(act, pri_ok)
                        nc.scalar.activation(pri_e[s][:], b_p[:], ACT.Copy).then_inc(pri_copied, 1)
                        take(act, k_ok)
                        nc.scalar.activation(kT[0][:], b_k[:], ACT.Copy).then_inc(k_copied, 1)

                    def first(s):
                        rows_copied()
                        rest_copied(s)

                    def both(i, o, s, nxt, more):
                        if nxt is not None:
                            rows_copied()
                        act.wait_ge(msg_st[s], 16 * i + 16)
                        take(act, m_ok)
                        nc.scalar.activation(msg[s][:], b_m[:], ACT.Copy).then_inc(m_copied, 1)
                        if nxt is not None:
                            rest_copied(nxt)

                    skewed(act, ORDER, first, both)

                @block.vector
                def _(dve):
                    ch = Chain(dve, dve_done)
                    V = nc.vector
                    V.memset(q_all[0][:], 0.0)
                    ch.link(V.memset(mx[0][:], 0.0))
                    ch.close()

                    def queries_masked(i, s):
                        dve.wait_ge(masks_in[s], 32 * i + 32)
                        take(dve, x1_copied)
                        for t in range(1, NTYPES):
                            V.scalar_tensor_tensor(out=dT[t][:], in0=masks[s][:, NTD - NOTLAST, :], scalar=float(t),
                                                   in1=b_dT[:], op0=ALU.is_equal, op1=ALU.mult).then_inc(x1_masked, 1)

                    def sources_masked(s):
                        take(dve, s_copied)
                        for t in range(1, NTYPES):
                            V.scalar_tensor_tensor(out=sT[t][:], in0=masks[s][:, NTS - NOTLAST, :], scalar=float(t),
                                                   in1=b_sT[:], op0=ALU.is_equal, op1=ALU.mult).then_inc(s_masked, 1)

                    def queries_spread(s):
                        take(dve, q_ok)
                        ch.link(V.tensor_tensor_scan(q_all[s][:, ::-1], masks[s][:, 0, ::-1], b_q[:, ::-1],
                                                     q_all[1 - s][:, 0:1], ALU.mult, ALU.add))

                    def edges_masked(s):
                        take(dve, k_copied)
                        for t in range(1, ETYPES):
                            V.scalar_tensor_tensor(out=kT[t][:], in0=masks[s][:, ET - NOTLAST, :], scalar=float(t),
                                                   in1=b_k[:], op0=ALU.is_equal, op1=ALU.mult).then_inc(k_masked, 1)

                    def first(s):
                        queries_masked(0, s)
                        sources_masked(s)
                        queries_spread(s)
                        edges_masked(s)

                    def both(i, o, s, nxt, more):
                        if nxt is not None:
                            queries_masked(i + o, nxt)
                        dve.wait_ge(m_copied, 2 * i + (o + 1))
                        V.tensor_tensor(prod[:], q_all[s][:], b_m[:], ALU.mult).then_inc(prod_ok, 1)
                        if nxt is not None:
                            sources_masked(nxt)
                        take(dve, l_ok)
                        take(dve, pri_copied)
                        dve.wait_ge(lm_st[s], 32 * i + 32)
                        ch.link(V.tensor_tensor(lg[s][:], pri_e[s][:], b_l[:], ALU.mult))
                        V.nop().then_inc(lg_ok, 1)
                        ch.link(V.tensor_tensor_scan(mx[s][:, ::-1], masks[s][:, 1, ::-1], lg[s][:, ::-1],
                                                     mx[1 - s][:, 0:1], ALU.add, ALU.max))
                        V.nop().then_inc(mx_ok, 1)
                        if more:
                            V.nop().then_inc(masks_free, 1)
                        if nxt is not None:
                            queries_spread(nxt)
                            edges_masked(nxt)

                    skewed(dve, ORDER, first, both, ch)

                @block.tensor
                def _(pe):
                    def rows_turned(i, s):
                        pe.wait_ge(x1_in[s], 16 * i + 16)
                        turn(b_dT, x1r[s]).then_inc(x1_turned, 1)
                        pe.wait_ge(xs_in[s], 16 * i + 16)
                        turn(b_sT, xs[s]).then_inc(s_turned, 1)

                    def priorities(i, s):
                        pe.wait_ge(masks_in[s], 32 * i + 32)
                        nc.tensor.matmul(b_p[:], pri[:], onehot[s][:], start=True, stop=True).then_inc(pri_ok, 1)

                    def by_type(bank, weights, parts, ok):
                        for t in range(len(parts)):
                            last = nc.tensor.matmul(bank[:], weights[:, t, :], parts[t][:], start=(t == 0),
                                                    stop=(t == len(parts) - 1))
                        last.then_inc(ok, 1)

                    def queries(free):
                        take(pe, x1_masked, 2)
                        if free:
                            pe.nop().then_inc(x1_free, 1)
                        by_type(b_q, wk, dT, q_ok)

                    def keys(free):
                        take(pe, s_masked, 2)
                        if free:
                            pe.nop().then_inc(xs_free, 1)
                        by_type(b_k, wk, sT, k_ok)

                    def first(s):
                        rows_turned(0, s)
                        priorities(0, s)
                        queries(True)
                        keys(True)

                    def both(i, o, s, nxt, more):
                        if nxt is not None:
                            rows_turned(i + o, nxt)
                        take(pe, k_masked, 3)
                        by_type(b_m, ra, kT, m_ok)
                        if nxt is not None:
                            priorities(i + o, nxt)
                            queries(more)
                        take(pe, prod_ok)
                        nc.tensor.matmul(b_l[:], head_ones[:], prod[:], start=True, stop=True).then_inc(l_ok, 1)
                        if nxt is not None:
                            keys(more)

                    skewed(pe, ORDER, first, both)

        with Phase(nc) as st:
            lr = two(sb, st, "s_lr", [P, 3, GE])
            masks = two(sb, st, "s_masks", [P, 2, GE], BF16)
            code = two(sb, st, "s_code", [P, 1, GE], BF16)
            x1r, hr, y, outr = [two(sb, st, n, [P, TG, D]) for n in ("s_x1r", "s_hr", "s_y", "s_outr")]
            mb, ex, es, nm = [two(sb, st, n, [P, GE]) for n in ("s_mb", "s_ex", "s_es", "s_nm")]
            hT = [[sb(st, f"s_hT{t}_{s}", [P, GE]) for t in range(NTYPES)] for s in range(2)]
            den = two(sb, st, "s_den", [P, TG, HEADS])
            stt = two(sb, st, "s_stt", [P, TG, 6])
            mv = two(sb, st, "s_mv", [P, TG, 2])
            sd, rr, bb = [two(sb, st, n, [P, TG]) for n in ("s_sd", "s_rr", "s_bb")]
            b_es, b_nm = two(pb, st, "s_bes"), two(pb, st, "s_bnm")
            b_h, b_a = two(pb, st, "s_bh"), two(pb, st, "s_ba")
            lr_in, masks_in, x1_in, x2_st = [two(sem, st, f"s_{n}") for n in ("lr_in", "masks_in", "x1_in", "x2_st")]
            (lr_free, x1_free, sub_ok, ex_ok, sums_ok, sums_turned, h_ok, h_turned, h_copied, h_masked, a_ok, var, std,
             affine, x2_ok) = [sem(st, f"s_{n}") for n in (
                "lr_free", "x1_free", "sub_ok", "ex_ok", "sums_ok", "sums_turned", "h_ok", "h_turned", "h_copied", "h_masked",
                "a_ok", "var", "std", "affine", "x2_ok")]
            with nc.Block() as block:
                @block.sync
                def _(sp):
                    for s in range(2):
                        sp.nop().then_inc(x2_st[s], 16)

                    def load_lr(b, s):
                        sp.dma_start(lr[s][:], lrm_of(b, s, 0, 3)).then_inc(lr_in[s], 16)
                        sp.dma_start(masks[s][:], seq_of(seq_rows, b, s, KEEP, NFIRST + 1)).then_inc(masks_in[s], 16)

                    def load_x1(b, s):
                        sp.dma_start(code[s][:], seq_of(seq_rows, b, s, NTD, NTD + 1)).then_inc(x1_in[s], 16)
                        sp.dma_start(x1r[s][:], rows_of(x1_rows, b, s)).then_inc(x1_in[s], 16)

                    for s in range(2):
                        load_lr(0, s)
                    for s in range(2):
                        load_x1(0, s)
                    for s in range(2):
                        take(sp, lr_free)
                        load_lr(1, s)

                    def body(i, more):
                        if more > 1:
                            for s in range(2):
                                take(sp, lr_free)
                                load_lr(i + 2, s)
                        if more:
                            for s in range(2):
                                take(sp, x1_free)
                                load_x1(i + 1, s)
                        if not isinstance(i, int) or i:
                            store(i - 1)

                    def store(i):
                        for s in range(2):
                            take(sp, x2_ok)
                            sp.dma_start(rows_of(x2_rows, i, s), outr[s][:]).then_inc(x2_st[s], 16)

                    body(0, 2)
                    with sp.Fori(1, BODIES - 2) as i:
                        body(i, 2)
                    body(BODIES - 2, 1)
                    body(BODIES - 1, 0)
                    store(BODIES - 1)
                    for s in range(2):
                        sp.wait_ge(x2_st[s], 16 * (BODIES + 1))

                @block.scalar
                def _(act):
                    def exponentials():
                        for s in range(2):
                            take(act, sub_ok)
                            nc.scalar.activation(ex[s][:], ex[s][:], ACT.Exp).then_inc(ex_ok, 1)

                    def norms(i):
                        for s in range(2):
                            act.wait_ge(x2_st[s], 16 * i + 16)
                            take(act, affine)
                            norm_rows(act, outr, y, rr, bb, s).then_inc(x2_ok, 1)

                    def body(i, more):
                        if more:
                            exponentials()
                        if not isinstance(i, int) or i:
                            norms(i - 1)
                        for s in range(2):
                            take(act, h_turned)
                            nc.scalar.activation(hT[s][0][:], b_h[s][:], ACT.Copy).then_inc(h_copied, 1)
                        for s in range(2):
                            take(act, var)
                            nc.scalar.activation(sd[s][:], mv[s][:, :, 1], ACT.Sqrt, bias=eps_col[:, EPS1:EPS1 + 1])\
                                .then_inc(std, 1)

                    exponentials()
                    body(0, True)
                    with act.Fori(1, BODIES - 1) as i:
                        body(i, True)
                    body(BODIES - 1, False)
                    norms(BODIES - 1)

                @block.vector
                def _(dve):
                    ch = Chain(dve, dve_done)
                    V = nc.vector
                    for t in (mb, es, nm):
                        last = V.memset(t[1][:], 0.0)
                    ch.link(last)
                    ch.close()

                    def differences(i, s):
                        dve.wait_ge(masks_in[s], 16 * i + 16)
                        dve.wait_ge(lr_in[s], 16 * i + 16)
                        ch.link(V.tensor_tensor_scan(mb[s][:], masks[s][:, 1, :], lr[s][:, 1, :],
                                                     mb[1 - s][:, GE - 1:GE], ALU.add, ALU.max))
                        V.tensor_tensor(ex[s][:], lr[s][:, 0, :], mb[s][:], ALU.subtract).then_inc(sub_ok, 1)

                    def sums(s, free):
                        take(dve, ex_ok)
                        V.tensor_tensor(lr[s][:, 2, :], lr[s][:, 2, :], ex[s][:], ALU.mult).then_inc(dve_done, 1)
                        ch.n += 1
                        V.tensor_tensor_scan(es[s][:], masks[s][:, 0, :], ex[s][:], es[1 - s][:, GE - 1:GE],
                                             ALU.mult, ALU.add)
                        dve.wait_ge(dve_done, ch.n)
                        ch.link(V.tensor_tensor_scan(nm[s][:], masks[s][:, 0, :], lr[s][:, 2, :],
                                                     nm[1 - s][:, GE - 1:GE], ALU.mult, ALU.add))
                        V.nop().then_inc(sums_ok, 1)
                        if free:
                            V.nop().then_inc(lr_free, 1)

                    def quotients(s):
                        take(dve, sums_turned)
                        ch.link(V.tensor_scalar(den[s][:], tiles(b_es[s][:])[:, :, ::HD], 1.0, None, ALU.max))
                        ch.link(V.reciprocal(den[s][:], den[s][:]))
                        V.tensor_tensor(hr[s][:].rearrange("p j (h r) -> p (j h) r", r=HD),
                                        b_nm[s][:].rearrange("p (k r) -> p k r", r=HD),
                                        den[s][:].rearrange("p j h -> p (j h)").unsqueeze(2)
                                        .to_broadcast([P, TG * HEADS, HD]), ALU.mult).then_inc(h_ok, 1)

                    def by_type(i, s):
                        dve.wait_ge(x1_in[s], 32 * i + 32)
                        take(dve, h_copied)
                        for t in range(1, NTYPES):
                            V.scalar_tensor_tensor(out=hT[s][t][:], in0=code[s][:, 0, :], scalar=float(t),
                                                   in1=b_h[s][:], op0=ALU.is_equal, op1=ALU.mult).then_inc(h_masked, 1)

                    def residual(s, free):
                        take(dve, a_ok)
                        ch.link(V.scalar_tensor_tensor(out=y[s][:], in0=tiles(b_a[s][:]), scalar=0.0, in1=x1r[s][:],
                                                       op0=ALU.max, op1=ALU.add))
                        if free:
                            V.nop().then_inc(x1_free, 1)
                        norm_stats(V, ch, y, stt, mv, s, var)

                    def norm(s):
                        take(dve, std)
                        ch.link(V.reciprocal(rr[s][:], sd[s][:]))
                        V.scalar_tensor_tensor(out=bb[s][:], in0=mv[s][:, :, 0], scalar=-1.0, in1=rr[s][:],
                                               op0=ALU.mult, op1=ALU.mult).then_inc(affine, 1)

                    def body(i, more):
                        if more:
                            for s in range(2):
                                differences(i + 1, s)
                        if not isinstance(i, int) or i:
                            for s in range(2):
                                norm(s)
                        for s in range(2):
                            quotients(s)
                        for s in range(2):
                            by_type(i, s)
                            if more:
                                sums(s, more > 1)
                        for s in range(2):
                            residual(s, more)

                    for s in range(2):
                        differences(0, s)
                    for s in range(2):
                        sums(s, True)
                    body(0, 2)
                    ch.close()
                    with dve.Fori(1, BODIES - 2) as i:
                        body(i, 2)
                        ch.close()
                    body(BODIES - 2, 1)
                    body(BODIES - 1, 0)
                    for s in range(2):
                        norm(s)
                    ch.close()

                @block.tensor
                def _(pe):
                    def sums_turn(s):
                        take(pe, sums_ok)
                        turn(b_es[s], tiles(es[s][:]))
                        turn(b_nm[s], tiles(nm[s][:])).then_inc(sums_turned, 1)

                    def body(more):
                        for s in range(2):
                            take(pe, h_ok)
                            turn(b_h[s], hr[s]).then_inc(h_turned, 1)
                        for s in range(2):
                            take(pe, h_masked, 2)
                            for j in range(TG):
                                for t in range(NTYPES):
                                    last = nc.tensor.matmul(b_a[s][:, j * P:(j + 1) * P],
                                                            hT[s][t][:, j * P:(j + 1) * P], wa[:, t, :],
                                                            start=(t == 0), stop=(t == NTYPES - 1))
                            last.then_inc(a_ok, 1)
                            if more:
                                sums_turn(s)

                    for s in range(2):
                        sums_turn(s)
                    with pe.Fori(0, BODIES - 1) as i:
                        body(True)
                    body(False)

        with Phase(nc) as st:
            a0r, xs, x2r, y, outr = [two(sb, st, n, [P, TG, D]) for n in ("m_a0r", "m_xs", "m_x2r", "m_y", "m_outr")]
            aff = two(sb, st, "m_aff", [P, TG, 2])
            stage = two(sb, st, "m_stage", [P, TG], I32)
            keep = two(sb, st, "m_keep", [P, 1, GE], BF16)
            sums = two(sb, st, "m_sums", [P, GE])
            stt = two(sb, st, "m_stt", [P, TG, 6])
            mv = two(sb, st, "m_mv", [P, TG, 2])
            sd, rr, bb = [two(sb, st, n, [P, TG]) for n in ("m_sd", "m_rr", "m_bb")]
            b_s, b_r = two(pb, st, "m_bs"), two(pb, st, "m_br")
            a0_in, d_in, picked, x3_st = [two(sem, st, f"m_{n}") for n in ("a0_in", "d_in", "picked", "x3_st")]
            (aff_ok, x_ok, staged, a0_free, d_free2, turned, scanned, back, var, std, affine, x3_ok) = [
                sem(st, f"m_{n}") for n in ("aff_ok", "x_ok", "staged", "a0_free", "d_free", "turned", "scanned",
                                            "back", "var", "std", "affine", "x3_ok")]
            with nc.Block() as block:
                @block.sync
                def _(sp):
                    for s in range(2):
                        sp.nop().then_inc(x3_st[s], 16)

                    def load_a0(b, s):
                        sp.dma_start(a0r[s][:], rows_of(src_x1, b, s)).then_inc(a0_in[s], 16)

                    def load_rest(b, s):
                        sp.dma_start(x2r[s][:], rows_of(x2_rows, b, s)).then_inc(d_in[s], 16)
                        sp.dma_start(keep[s][:], seq_of(seq_rows, b, s, KEEP, KEEP + 1)).then_inc(d_in[s], 16)

                    for s in range(2):
                        load_a0(0, s)
                        load_rest(0, s)

                    def first(_):
                        for s in range(2):
                            take(sp, a0_free)
                            load_a0(1, s)

                    def both(i, o, s, nxt, more):
                        if not isinstance(i, int):
                            take(sp, a0_free)
                            load_a0(i + 2, s)
                        if more:
                            take(sp, d_free2)
                            load_rest(i + 1, s)
                        take(sp, x3_ok)
                        sp.dma_start(rows_of(x3s_rows, i, s), outr[s][:]).then_inc(x3_st[s], 16)

                    skewed(sp, (0, 1), first, both, peel=2)
                    for s in range(2):
                        sp.wait_ge(x3_st[s], 16 * (BODIES + 1))

                @block.gpsimd
                def _(gp):
                    bound = gp.to_reg(EP - 1)
                    with gp.Fori(0, BODIES) as i:
                        for s in range(2):
                            take(gp, staged)
                            take(gp, x_ok)
                            gp.nop().then_inc(a0_free, 1)
                            picks(gp, bound, x2_rows, xs, stage, picked, s)

                @block.scalar
                def _(act):
                    nc.scalar.preload_act_table(ACT.Sqrt)
                    for s in range(2):
                        local_rows(act, 0, s, a0_in, aff_ok, x_ok, xs, a0r, aff)

                    def both(i, o, s, nxt, more):
                        if more > 1:
                            local_rows(act, i + (1 + o), nxt, a0_in, aff_ok, x_ok, xs, a0r, aff)
                        take(act, var)
                        nc.scalar.activation(sd[s][:], mv[s][:, :, 1], ACT.Sqrt, bias=eps_col[:, EPS_M:EPS_M + 1])\
                            .then_inc(std, 1)
                        act.wait_ge(x3_st[s], 16 * i + 16)
                        take(act, affine)
                        norm_rows(act, outr, y, rr, bb, s).then_inc(x3_ok, 1)

                    skewed(act, (0, 1), lambda s: local_rows(act, 1, s, a0_in, aff_ok, x_ok, xs, a0r, aff), both,
                           peel=2)

                @block.vector
                def _(dve):
                    ch = Chain(dve, dve_done)
                    V = nc.vector
                    ch.link(V.memset(sums[1][:], 0.0))
                    ch.close()
                    for s in range(2):
                        local_put(V, 0, aff, stage, 0, s, aff_ok, staged)

                    def front(b, s, more):
                        dve.wait_ge(d_in[s], 32 * b + 32)
                        take(dve, turned)
                        if more:
                            local_put(V, 0, aff, stage, b + 1, s, aff_ok, staged)
                        summed = ch.mark(V.tensor_tensor_scan(sums[s][:], keep[s][:, 0, :], b_s[s][:],
                                                              sums[1 - s][:, GE - 1:GE], ALU.mult, ALU.add))
                        ch.until(summed)
                        V.nop().then_inc(scanned, 1)

                    def both(i, o, s, nxt, more):
                        take(dve, back)
                        added = ch.mark(times_col_plus(V, y[s], tiles(b_r[s][:]), c_third, i, s,
                                                       lambda j: x2r[s][:, j, :]))
                        if nxt is not None:
                            front(i + o, nxt, more > 1)
                        ch.until(added)
                        if more:
                            V.nop().then_inc(d_free2, 1)
                        norm_stats(V, ch, y, stt, mv, s, var)
                        take(dve, std)
                        ch.link(V.reciprocal(rr[s][:], sd[s][:]))
                        ch.link(V.tensor_tensor(rr[s][:], rr[s][:],
                                                c_dinv[:, bass.ds(i * (2 * TG) + s * TG, TG)], ALU.mult))
                        V.scalar_tensor_tensor(out=bb[s][:], in0=mv[s][:, :, 0], scalar=-1.0, in1=rr[s][:],
                                               op0=ALU.mult, op1=ALU.mult).then_inc(affine, 1)

                    skewed(dve, (0, 1), lambda s: front(0, s, True), both, ch, peel=2)

                @block.tensor
                def _(pe):
                    def front(b, s):
                        pe.wait_ge(picked[s], 64 * b + 64)
                        turn(b_s[s], xs[s]).then_inc(turned, 1)

                    def both(i, o, s, nxt, more):
                        if nxt is not None:
                            front(i + o, nxt)
                        take(pe, scanned)
                        turn(b_r[s], tiles(sums[s][:])).then_inc(back, 1)

                    skewed(pe, (0, 1), lambda s: front(0, s), both)

        with Phase(nc) as st:
            a0r, xs, x3r, h2l, h2s, zr = [two(sb, st, n, [P, TG, D]) for n in (
                "c_a0r", "c_xs", "c_x3r", "c_h2l", "c_h2s", "c_zr")]
            tmp = two(sb, st, "c_tmp", [P, TG, D])
            y, outr = [two(sb, st, n, [P, TG, D]) for n in ("c_y", "c_outr")]
            stage_out = two(sb, st, "c_stage_out", [P, TG], I32)
            stt = two(sb, st, "c_stt", [P, TG, 6])
            mv = two(sb, st, "c_mv", [P, TG, 2])
            sd, rr, bb = [two(sb, st, n, [P, TG]) for n in ("c_sd", "c_rr", "c_bb")]
            aff = two(sb, st, "c_aff", [P, TG, 2])
            stage = two(sb, st, "c_stage", [P, TG], I32)
            keep = two(sb, st, "c_keep", [P, 1, GE], BF16)
            dinv_b = two(sb, st, "c_dinv_b", [P, 1, GE])
            sums = two(sb, st, "c_sums", [P, GE])
            uT, xsT = two(sb, st, "c_uT", [P, GE]), two(sb, st, "c_xsT", [P, GE])
            hs, hd = two(sb, st, "c_hs", [P, GE]), two(sb, st, "c_hd", [P, GE])
            b_s, b_d = pb(st, "c_bs"), pb(st, "c_bd")
            b_hs, b_hd = two(pb, st, "c_bhs"), two(pb, st, "c_bhd")
            b_os, b_od = pb(st, "c_bos"), pb(st, "c_bod")
            a0_in, d_in, picked, h2l_st, h2s_st, z_st, sent = [two(sem, st, f"c_{n}") for n in (
                "a0_in", "d_in", "picked", "h2l_st", "h2s_st", "z_st", "sent")]
            var, std, affine, out_ok, y_ok = [sem(st, f"c_{n}") for n in ("var", "std", "affine", "out_ok", "y_ok")]
            (aff_ok, x_ok, staged, a0_free, d_free2, s_turned, s_copied, x3_turned, u_ok, hs_ok, hs_relu, hd_ok,
             hd_relu, os_ok, os_copied, od_ok, h2s_ok, z_ok) = [sem(st, f"c_{n}") for n in (
                "aff_ok", "x_ok", "staged", "a0_free", "d_free", "s_turned", "s_copied", "x3_turned", "u_ok", "hs_ok",
                "hs_relu", "hd_ok", "hd_relu", "os_ok", "os_copied", "od_ok", "h2s_ok", "z_ok")]
            with nc.Block() as block:
                @block.sync
                def _(sp):
                    for s in range(2):
                        for q in (h2l_st, h2s_st, z_st):
                            sp.nop().then_inc(q[s], 16)

                    def load_a0(b, s):
                        sp.dma_start(a0r[s][:], rows_of(src_x1, b, s)).then_inc(a0_in[s], 16)

                    def load_rest(b, s):
                        sp.dma_start(x3r[s][:], rows_of(x3s_rows, b, s)).then_inc(d_in[s], 16)
                        sp.dma_start(keep[s][:], seq_of(seq_rows, b, s, KEEP, KEEP + 1)).then_inc(d_in[s], 16)
                        sp.dma_start(dinv_b[s][:], seq_of(dinv_row, b, s, 0, 1)).then_inc(d_in[s], 16)

                    for s in range(2):
                        load_a0(0, s)
                        load_rest(0, s)

                    def first(_):
                        for s in range(2):
                            take(sp, a0_free)
                            load_a0(1, s)

                    def both(i, o, s, nxt, more):
                        if more:
                            take(sp, d_free2)
                            load_rest(i + 1, s)
                        if not isinstance(i, int):
                            take(sp, a0_free)
                            load_a0(i + 2, s)
                        take(sp, os_copied)
                        sp.dma_start(rows_of(h2_src, i, s), h2l[s][:]).then_inc(h2l_st[s], 16)
                        take(sp, h2s_ok)
                        sp.dma_start(rows_of(h2s_rows, i, s), h2s[s][:]).then_inc(h2s_st[s], 16)
                        take(sp, z_ok)
                        sp.dma_start(rows_of(z_rows, i, s), zr[s][:]).then_inc(z_st[s], 16)

                    skewed(sp, (0, 1), first, both, peel=2)
                    for s in range(2):
                        for q in (h2l_st, h2s_st, z_st):
                            sp.wait_ge(q[s], 16 * (BODIES + 1))

                @block.gpsimd
                def _(gp):
                    bound = gp.to_reg(EP - 1)
                    bound_out = gp.to_reg(N - 1)

                    def pick(s):
                        take(gp, staged)
                        take(gp, x_ok)
                        gp.nop().then_inc(a0_free, 1)
                        picks(gp, bound, x3s_rows, xs, stage, picked, s)

                    def first(s):
                        for n in (0, 1, s):
                            pick(n)

                    def send(s):
                        take(gp, out_ok)
                        for j in range(TG):
                            gp.indirect_dma_start(out, bass.IndirectOffsetOnAxis(ap=stage_out[s][:, j:j + 1], axis=0),
                                                  outr[s][:, j, :], None, bounds_check=bound_out, oob_is_err=False)\
                                .then_inc(sent[s], 16)

                    def both(i, o, s, nxt, more):
                        if more > 1:
                            pick(nxt)
                        if not is_first(i, o):
                            send(1 - s)

                    skewed(gp, (0, 1), first, both, peel=2, head=1)
                    send(1)
                    for s in range(2):
                        gp.wait_ge(sent[s], 64 * BODIES)

                @block.scalar
                def _(act):
                    nc.scalar.preload_act_table(ACT.Sqrt)
                    for s in range(2):
                        local_rows(act, 0, s, a0_in, aff_ok, x_ok, xs, a0r, aff)

                    def front(b, s, more):
                        take(act, s_turned)
                        nc.scalar.activation(xsT[s][:], b_s[:], ACT.Copy).then_inc(s_copied, 1)
                        if more:
                            local_rows(act, b + 1, s, a0_in, aff_ok, x_ok, xs, a0r, aff)

                    def relus(half, ok, bank, relu):
                        for c in range(2):
                            take(act, ok)
                            nc.scalar.activation(half[c][:], bank[c][:], ACT.Relu, bias=b1s[:, c:c + 1])\
                                .then_inc(relu, 1)

                    def root(s):
                        take(act, var)
                        nc.scalar.activation(sd[s][:], mv[s][:, :, 1], ACT.Sqrt, bias=eps_col[:, EPS1:EPS1 + 1])\
                            .then_inc(std, 1)

                    def norm(s):
                        take(act, affine)
                        norm_rows(act, outr, y, rr, bb, s).then_inc(out_ok, 1)

                    def both(i, o, s, nxt, more):
                        relus(hs, hs_ok, b_hs, hs_relu)
                        if not is_first(i, o):
                            root(1 - s)
                        relus(hd, hd_ok, b_hd, hd_relu)
                        if not is_first(i, o):
                            norm(1 - s)
                        if nxt is not None:
                            front(i + o, nxt, more > 1)
                        act.wait_ge(h2l_st[s], 16 * i + 16)
                        take(act, y_ok)
                        nc.scalar.activation(h2l[s][:], tiles(b_os[:]), ACT.Copy).then_inc(os_copied, 1)

                    skewed(act, (0, 1), lambda s: front(0, s, True), both, peel=2, head=1)
                    root(1)
                    norm(1)

                @block.vector
                def _(dve):
                    ch = Chain(dve, dve_done)
                    V = nc.vector
                    ch.link(V.memset(sums[1][:], 0.0))
                    ch.close()
                    for s in range(2):
                        local_put(V, 1, aff, stage, 0, s, aff_ok, staged)

                    def front(b, s, more):
                        dve.wait_ge(d_in[s], 48 * b + 48)
                        take(dve, s_copied)
                        V.tensor_tensor(y[s][:], xs[s][:], b2_all[:].unsqueeze(1).to_broadcast([P, TG, D]),
                                        ALU.add)
                        if more:
                            local_put(V, 1, aff, stage, b + 1, s, aff_ok, staged)
                        summed = ch.mark(V.tensor_tensor_scan(sums[s][:], keep[s][:, 0, :], b_s[:],
                                                              sums[1 - s][:, GE - 1:GE], ALU.mult, ALU.add))
                        take(dve, x3_turned)
                        ch.until(summed)
                        ch.link(V.tensor_tensor(uT[s][:], sums[s][:], b_d[:], ALU.add))
                        V.tensor_tensor(uT[s][:], uT[s][:], dinv_b[s][:, 0, :], ALU.mult).then_inc(u_ok, 1)

                    def finish(b, s):
                        take(dve, std)
                        scale = ch.mark(V.reciprocal(rr[s][:], sd[s][:]))
                        if not isinstance(b, int) or b:
                            dve.wait_ge(sent[s], 64 * b)
                        V.tensor_copy(stage_out[s][:], i_srcout[:, bass.ds(b * (2 * TG) + s * TG, TG)])
                        ch.until(scale)
                        V.scalar_tensor_tensor(out=bb[s][:], in0=mv[s][:, :, 0], scalar=-1.0, in1=rr[s][:],
                                               op0=ALU.mult, op1=ALU.mult).then_inc(affine, 1)

                    def both(i, o, s, nxt, more):
                        ch.link(times_col_plus(V, tmp[s], x3r[s], c_root, i, s, lambda j: b2_all[:]))
                        if more:
                            V.nop().then_inc(d_free2, 1)
                        if not is_first(i, o):
                            finish(i + (o - 1), 1 - s)
                        if nxt is not None:
                            front(i + o, nxt, more > 1)
                        take(dve, os_ok)
                        ch.link(V.tensor_tensor(y[s][:], tiles(b_os[:]), y[s][:], ALU.add))
                        V.nop().then_inc(y_ok, 1)
                        for j in range(TG):
                            last = V.bn_stats(stt[s][:, j, :], y[s][:, j, :])
                        stats = ch.mark(last)
                        dve.wait_ge(h2s_st[s], 16 * i + 16)
                        take(dve, od_ok)
                        product = ch.mark(V.tensor_tensor(h2s[s][:], tiles(b_od[:]), cols(c_dinv, i, s), ALU.mult))
                        ch.until(stats)
                        for j in range(TG):
                            last = V.bn_aggr(mv[s][:, j, :], stt[s][:, j, :])
                        last.then_inc(var, 1)
                        ch.until(product)
                        V.nop().then_inc(h2s_ok, 1)
                        dve.wait_ge(z_st[s], 16 * i + 16)
                        times_col_plus(V, zr[s], h2s[s], c_dinv, i, s, lambda j: tmp[s][:, j, :]).then_inc(z_ok, 1)

                    skewed(dve, (0, 1), lambda s: front(0, s, True), both, ch, peel=2, head=2)
                    finish(BODIES - 1, 1)
                    ch.close()

                @block.tensor
                def _(pe):
                    def first(banks, t, ok):
                        for c in range(2):
                            nc.tensor.matmul(banks[c][:], w1s[:, c * D:(c + 1) * D], t[:], start=True, stop=True)\
                                .then_inc(ok, 1)

                    def second(bank, h):
                        for j in range(TG):
                            for c in range(2):
                                last = nc.tensor.matmul(bank[:, j * P:(j + 1) * P], h[c][:, j * P:(j + 1) * P],
                                                        w2s[:, c, :], start=(c == 0), stop=(c == 1))
                        return last

                    def rows_turned(b, s):
                        pe.wait_ge(d_in[s], 48 * b + 48)
                        turn(b_d, x3r[s]).then_inc(x3_turned, 1)
                        pe.wait_ge(picked[s], 64 * b + 64)
                        turn(b_s, xs[s]).then_inc(s_turned, 1)

                    def both(i, o, s, nxt, more):
                        take(pe, u_ok)
                        first(b_hs, xsT[s], hs_ok)
                        first(b_hd, uT[s], hd_ok)
                        if nxt is not None:
                            rows_turned(i + o, nxt)
                        take(pe, hs_relu, 2)
                        second(b_os, hs).then_inc(os_ok, 1)
                        take(pe, hd_relu, 2)
                        second(b_od, hd).then_inc(od_ok, 1)

                    skewed(pe, (0, 1), lambda s: rows_turned(0, s), both)

        with Phase(nc) as st:
            xs, zr, y, outr = [two(sb, st, n, [P, TG, D]) for n in ("f_xs", "f_zr", "f_y", "f_outr")]
            stage = two(sb, st, "f_stage", [P, TG], I32)
            stage_out = two(sb, st, "f_stage_out", [P, TG], I32)
            keep = two(sb, st, "f_keep", [P, 1, GE], BF16)
            sums = two(sb, st, "f_sums", [P, GE])
            stt = two(sb, st, "f_stt", [P, TG, 6])
            mv = two(sb, st, "f_mv", [P, TG, 2])
            sd, rr, bb = [two(sb, st, n, [P, TG]) for n in ("f_sd", "f_rr", "f_bb")]
            b_s, b_r = two(pb, st, "f_bs"), two(pb, st, "f_br")
            h2_in, d_in, picked, sent = [two(sem, st, f"f_{n}") for n in ("h2_in", "d_in", "picked", "sent")]
            (staged, xs_free, d_free2, turned, scanned, back, var, std, affine, out_ok) = [
                sem(st, f"f_{n}") for n in ("staged", "xs_free", "d_free", "turned", "scanned", "back", "var", "std",
                                            "affine", "out_ok")]
            with nc.Block() as block:
                @block.sync
                def _(sp):
                    def load_h2(b, s):
                        sp.dma_start(xs[s][:], rows_of(h2_src, b, s)).then_inc(h2_in[s], 16)

                    def load_rest(b, s):
                        sp.dma_start(zr[s][:], rows_of(z_rows, b, s)).then_inc(d_in[s], 16)
                        sp.dma_start(keep[s][:], seq_of(seq_rows, b, s, KEEP, KEEP + 1)).then_inc(d_in[s], 16)

                    for s in range(2):
                        load_h2(0, s)
                        load_rest(0, s)
                    def first(s):
                        take(sp, xs_free)
                        load_h2(1, s)

                    def both(i, o, s, nxt, more):
                        if more > 1:
                            take(sp, xs_free)
                            load_h2(i + (1 + o), nxt)
                        if more:
                            take(sp, d_free2)
                            load_rest(i + 1, s)

                    skewed(sp, (0, 1), first, both, peel=2)

                @block.gpsimd
                def _(gp):
                    bound = gp.to_reg(EP - 1)
                    bound_out = gp.to_reg(N - 1)

                    def pick(i, s):
                        gp.wait_ge(h2_in[s], 16 * i + 16)
                        take(gp, staged)
                        picks(gp, bound, h2s_rows, xs, stage, picked, s)

                    def first(s):
                        for b, n in ((0, 0), (0, 1), (1, s)):
                            pick(b, n)

                    def both(i, o, s, nxt, more):
                        if more > 1:
                            pick(i + (1 + o), nxt)
                        take(gp, out_ok)
                        for j in range(TG):
                            gp.indirect_dma_start(out, bass.IndirectOffsetOnAxis(ap=stage_out[s][:, j:j + 1], axis=0),
                                                  outr[s][:, j, :], None, bounds_check=bound_out, oob_is_err=False)\
                                .then_inc(sent[s], 16)

                    skewed(gp, (0, 1), first, both, peel=2)
                    for s in range(2):
                        gp.wait_ge(sent[s], 64 * BODIES)

                @block.scalar
                def _(act):
                    nc.scalar.preload_act_table(ACT.Sqrt)
                    with act.Fori(0, BODIES) as i:
                        for s in range(2):
                            take(act, var)
                            nc.scalar.activation(sd[s][:], mv[s][:, :, 1], ACT.Sqrt, bias=eps_col[:, EPS1:EPS1 + 1])\
                                .then_inc(std, 1)
                            take(act, affine)
                            norm_rows(act, outr, y, rr, bb, s).then_inc(out_ok, 1)

                @block.vector
                def _(dve):
                    ch = Chain(dve, dve_done)
                    V = nc.vector
                    ch.link(V.memset(sums[1][:], 0.0))
                    ch.close()
                    for s in range(2):
                        local_put(V, None, None, stage, 0, s, None, staged)

                    def front(b, s, more):
                        dve.wait_ge(d_in[s], 32 * b + 32)
                        take(dve, turned)
                        if more:
                            local_put(V, None, None, stage, b + 1, s, None, staged)
                            V.nop().then_inc(xs_free, 1)
                        summed = ch.mark(V.tensor_tensor_scan(sums[s][:], keep[s][:, 0, :], b_s[s][:],
                                                              sums[1 - s][:, GE - 1:GE], ALU.mult, ALU.add))
                        ch.until(summed)
                        V.nop().then_inc(scanned, 1)

                    def both(i, o, s, nxt, more):
                        take(dve, back)
                        added = ch.mark(times_col_plus(V, y[s], tiles(b_r[s][:]), c_dinv, i, s,
                                                       lambda j: zr[s][:, j, :]))
                        if nxt is not None:
                            front(i + o, nxt, more > 1)
                        ch.until(added)
                        if more:
                            V.nop().then_inc(d_free2, 1)
                        norm_stats(V, ch, y, stt, mv, s, var)
                        take(dve, std)
                        ch.link(V.reciprocal(rr[s][:], sd[s][:]))
                        if not isinstance(i, int) or i:
                            dve.wait_ge(sent[s], 64 * i)
                        V.tensor_copy(stage_out[s][:], i_out[:, bass.ds(i * (2 * TG) + s * TG, TG)])
                        V.scalar_tensor_tensor(out=bb[s][:], in0=mv[s][:, :, 0], scalar=-1.0, in1=rr[s][:],
                                               op0=ALU.mult, op1=ALU.mult).then_inc(affine, 1)

                    skewed(dve, (0, 1), lambda s: front(0, s, True), both, ch, peel=2, head=1)

                @block.tensor
                def _(pe):
                    def front(b, s):
                        pe.wait_ge(picked[s], 64 * b + 64)
                        turn(b_s[s], xs[s]).then_inc(turned, 1)

                    def both(i, o, s, nxt, more):
                        if nxt is not None:
                            front(i + o, nxt)
                        take(pe, scanned)
                        turn(b_r[s], tiles(sums[s][:])).then_inc(back, 1)

                    skewed(pe, (0, 1), lambda s: front(0, s), both)


_INS = ["x", "src", "dst", "edge_type_4", "edge_weight", "node_type_3", "L1_gnn_W_kqv", "L1_gnn_W_a",
        "L1_gnn_rel_pri", "L1_gnn_rel_att", "L3_gnn_W1", "L3_gnn_b1", "L3_gnn_W2", "L3_gnn_b2"]


def kernel(**inputs):
    import numpy as _np
    import concourse.bacc as _bacc
    from concourse.bass_utils import run_bass_kernel_spmd as _run

    nc = _bacc.Bacc("TRN2", target_bir_lowering=False, num_devices=1)
    arrays, args = {}, []
    for name in _INS:
        a = _np.ascontiguousarray(inputs[name])
        arrays[f"in_{name}"] = a
        args.append(nc.dram_tensor(f"in_{name}", a.shape, mybir.dt.from_np(a.dtype), kind="ExternalInput").ap())
    x = inputs["x"]
    args.append(nc.dram_tensor("out_0", x.shape, F32, kind="ExternalOutput").ap())
    gnn_kernel(nc, *args)
    r = _run(nc, [arrays], core_ids=[0])
    return r.results[0]["out_0"]
```
